# Optimizing a Trainium2 kernel written in Bass

```python
import numpy as np
import jax
import jax.numpy as jnp

def _softmax(x, axis=-1):
    return jax.nn.softmax(x, axis=axis)

def _gelu(x):
    return jax.nn.gelu(x, approximate=True)

def _silu(x):
    return jax.nn.silu(x)

def _sigmoid(x):
    return jax.nn.sigmoid(x)

def _layernorm(x, axis=-1, eps=1e-05):
    m = jnp.mean(x, axis=axis, keepdims=True)
    v = jnp.var(x, axis=axis, keepdims=True)
    return (x - m) / jnp.sqrt(v + eps)

def _scatter_add(tgt, idx, src, axis=0):
    return tgt.at[idx].add(src)

def _segment_sum(src, seg, n):
    return jax.ops.segment_sum(src, seg, n)
kernel_name = 'mk_gnn_preln_d2_gnn_r32_0f345f'

def setup_inputs(seed: int=0):
    np.random.seed(seed)
    _w = jnp.asarray

    def _rec_inputs():
        import jax
        import jax.numpy as jnp
        _gk = jax.random.key(seed)
        x = -0.0003713 + 1 * jax.random.normal(jax.random.fold_in(_gk, 1), (50000, 128), jnp.float32)
        src = jax.random.randint(jax.random.fold_in(_gk, 2), (50000,), 0, 50000, jnp.int32)
        dst = jnp.minimum((50000 * jax.random.uniform(jax.random.fold_in(_gk, 3), (50000,)) ** 2.0).astype(jnp.int32), 49999)
        _o = jnp.argsort(dst, stable=True)
        src = src[_o]
        dst = dst[_o]
        edge_attr_64 = 0.000189758 + 1.00013 * jax.random.normal(jax.random.fold_in(_gk, 12), (50000, 64), jnp.float32)
        return (x, src, dst, edge_attr_64)
    x, src, dst, edge_attr_64 = _rec_inputs()

    def _L0_gnn_setup():
        import jax, jax.numpy as jnp
        import numpy as np
        HIDDEN = 128
        N_PARENT = 3125
        N_CHILD = 6250
        N_EDGES = 18750
        LN_EPS = 1e-05
        key = jax.random.key(seed)
        ks = jax.random.split(key, 12)
        s = 0.02
        return {'x_parent': jax.random.normal(ks[0], (N_PARENT, HIDDEN), jnp.float32), 'x_child': jax.random.normal(ks[1], (N_CHILD, HIDDEN), jnp.float32), 'src': jax.random.randint(ks[2], (N_EDGES,), 0, N_PARENT, jnp.int32), 'dst': jax.random.randint(ks[3], (N_EDGES,), 0, N_CHILD, jnp.int32), 'W1': jax.random.normal(ks[4], (HIDDEN, HIDDEN), jnp.float32) * s, 'b1': jnp.zeros((HIDDEN,), jnp.float32), 'W2': jax.random.normal(ks[5], (HIDDEN, HIDDEN), jnp.float32) * s, 'b2': jnp.zeros((HIDDEN,), jnp.float32), 'Wu': jax.random.normal(ks[6], (HIDDEN, HIDDEN), jnp.float32) * s, 'bu': jnp.zeros((HIDDEN,), jnp.float32), 'gamma': jnp.ones((HIDDEN,), jnp.float32), 'beta': jnp.zeros((HIDDEN,), jnp.float32)}
    _L0_gnn_all = _L0_gnn_setup()
    _L0_gnn_in = {k: v for k, v in _L0_gnn_all.items() if k in ('x_child', 'W1', 'b1', 'W2', 'b2', 'Wu', 'bu', 'gamma', 'beta')}
    del _L0_gnn_all

    def _L1_gnn_setup():
        import jax, jax.numpy as jnp
        import numpy as np
        N_NODES = 3125
        N_EDGES = 25000
        IN_CH = 128
        EDGE_CH = 64
        OUT_CH = 128
        EPS = 1e-12

        def l2_normalize(v, axis=-1):
            norm = jnp.sqrt(jnp.sum(v * v, axis=axis, keepdims=True))
            return v / jnp.maximum(norm, EPS)
        key = jax.random.key(seed)
        k1, k2, k3, k4, k5 = jax.random.split(key, 5)
        x = jax.random.normal(k1, (N_NODES, IN_CH), dtype=jnp.float32)
        edge_index = jax.random.randint(k2, (2, N_EDGES), 0, N_NODES, dtype=jnp.int64)
        edge_attr = jax.random.normal(k3, (N_EDGES, EDGE_CH), dtype=jnp.float32)
        fan_in = IN_CH + EDGE_CH
        bound = 1.0 / np.sqrt(fan_in)
        W = jax.random.uniform(k4, (OUT_CH, fan_in), minval=-bound, maxval=bound, dtype=jnp.float32)
        b = jax.random.uniform(k5, (OUT_CH,), minval=-bound, maxval=bound, dtype=jnp.float32)
        return {'x': x, 'edge_index': edge_index, 'edge_attr': edge_attr, 'W': W, 'b': b}
    _L1_gnn_all = _L1_gnn_setup()
    _L1_gnn_in = {k: v for k, v in _L1_gnn_all.items() if k in ('W', 'b')}
    del _L1_gnn_all
    return {'x': x, 'src': src, 'dst': dst, 'edge_attr_64': edge_attr_64, 'L0_gnn_x_child': _L0_gnn_in['x_child'], 'L0_gnn_W1': _L0_gnn_in['W1'], 'L0_gnn_b1': _L0_gnn_in['b1'], 'L0_gnn_W2': _L0_gnn_in['W2'], 'L0_gnn_b2': _L0_gnn_in['b2'], 'L0_gnn_Wu': _L0_gnn_in['Wu'], 'L0_gnn_bu': _L0_gnn_in['bu'], 'L0_gnn_gamma': _L0_gnn_in['gamma'], 'L0_gnn_beta': _L0_gnn_in['beta'], 'L1_gnn_W': _L1_gnn_in['W'], 'L1_gnn_b': _L1_gnn_in['b']}

def reference(x, src, dst, edge_attr_64, L0_gnn_x_child, L0_gnn_W1, L0_gnn_b1, L0_gnn_W2, L0_gnn_b2, L0_gnn_Wu, L0_gnn_bu, L0_gnn_gamma, L0_gnn_beta, L1_gnn_W, L1_gnn_b):
    import jax
    import jax.numpy as jnp

    def _L0_gnn_ref(x_parent, x_child, src, dst, W1, b1, W2, b2, Wu, bu, gamma, beta):
        import jax, jax.numpy as jnp
        import numpy as np
        HIDDEN = 128
        N_PARENT = 3125
        N_CHILD = 6250
        N_EDGES = 18750
        LN_EPS = 1e-05
        n_parent = x_parent.shape[0]
        h = jax.nn.relu(x_parent[src] @ W1 + b1)
        pred = h @ W2 + b2
        res = x_child[dst] - pred
        ssum = jax.ops.segment_sum(res, src, num_segments=n_parent)
        cnt = jax.ops.segment_sum(jnp.ones_like(src, jnp.float32), src, num_segments=n_parent)
        agg = ssum / jnp.maximum(cnt, 1.0)[:, None]
        y = x_parent + (agg @ Wu + bu)
        mu = jnp.mean(y, axis=-1, keepdims=True)
        var = jnp.mean(jnp.square(y - mu), axis=-1, keepdims=True)
        out = (y - mu) * jax.lax.rsqrt(var + LN_EPS) * gamma + beta
        return out

    def _L1_gnn_ref(x, edge_index, edge_attr, W, b):
        import jax, jax.numpy as jnp
        import numpy as np
        N_NODES = 3125
        N_EDGES = 25000
        IN_CH = 128
        EDGE_CH = 64
        OUT_CH = 128
        EPS = 1e-12

        def l2_normalize(v, axis=-1):
            norm = jnp.sqrt(jnp.sum(v * v, axis=axis, keepdims=True))
            return v / jnp.maximum(norm, EPS)
        row, col = (edge_index[0], edge_index[1])
        n_nodes = x.shape[0]
        msg = jnp.concatenate([x[row], edge_attr], axis=1)
        msg = l2_normalize(msg, axis=1)
        sums = jax.ops.segment_sum(msg, col, num_segments=n_nodes)
        counts = jax.ops.segment_sum(jnp.ones((msg.shape[0],), dtype=msg.dtype), col, num_segments=n_nodes)
        agg = sums / jnp.maximum(counts, 1.0)[:, None]
        out = agg @ W.T + b
        return l2_normalize(out, axis=1)
    edge_index = jnp.stack([src, dst])
    h = jnp.maximum(_layernorm(x, axis=-1), 0.0)
    x = x + _L0_gnn_ref(h, L0_gnn_x_child, src, dst, L0_gnn_W1, L0_gnn_b1, L0_gnn_W2, L0_gnn_b2, L0_gnn_Wu, L0_gnn_bu, L0_gnn_gamma, L0_gnn_beta)
    h = jnp.maximum(_layernorm(x, axis=-1), 0.0)
    x = x + _L1_gnn_ref(h, edge_index, edge_attr_64, L1_gnn_W, L1_gnn_b)
    return x

_drawn_inputs = setup_inputs


def setup_inputs(seed=0):
    import zlib

    import numpy as np

    out = dict(_drawn_inputs(seed))
    spreads = {'L0_gnn_b1': (0.0, 0.8),
     'L0_gnn_b2': (0.0, 0.58),
     'L0_gnn_bu': (0.0, 0.1),
     'L0_gnn_gamma': (1.0, 0.2),
     'L0_gnn_beta': (0.0, 0.1)}
    factors = {'edge_attr_64': 3.755, 'L0_gnn_W1': 8.0, 'L0_gnn_W2': 8.0}
    for name, (base, spread) in spreads.items():
        noise = np.random.default_rng([zlib.crc32(name.encode()), seed]).standard_normal(out[name].shape)
        drawn = base * np.exp(spread * noise) if base else spread * noise
        out[name] = jnp.asarray(drawn.astype(out[name].dtype))
    for name, factor in factors.items():
        out[name] = (out[name] * factor).astype(out[name].dtype)
    return out
```

```python
from contextlib import ExitStack

import concourse.bass as bass
from concourse import mybir

P = 128
D = 128
N = 50000
E = 50000
NCHILD = 6250
EC = 64
LN_EPS = 1e-5
L2_EPS = 1e-12

PAIR = 2 * P
G = 4
PAIRS_A_STEP = 4
GROUPS_A_STEP = 2
STEP = PAIRS_A_STEP * PAIR
STEPS = -(-N // STEP)
NP = STEPS * STEP
TILES = NP // P
PAIRS = NP // PAIR
GROUPS = NP // (P * G)
ROWS = NP + PAIR
CT = -(-NCHILD // P)
CROWS = CT * P
CCHUNK = 7
assert CT % CCHUNK == 0 and STEPS % 2 == 1 and STEPS > 3 and NP > N
TW = D + 1
HTILES = STEP // P
OH = 4

ALU = mybir.AluOpType
ACT = mybir.ActivationFunctionType
F32 = mybir.dt.float32
F16 = mybir.dt.float16
I32 = mybir.dt.int32


def run_steps(eng, step):
    step(0, 0, 0, True, False)
    with eng.Fori(0, (STEPS - 3) // 2) as j:
        step(j * 2 + 1, 1, j, False, False)
        step(j * 2 + 2, 0, j + 1, False, False)
    step(STEPS - 2, 1, (STEPS - 3) // 2, False, False)
    step(STEPS - 1, 0, (STEPS - 1) // 2, False, True)


def build(nc, x, src_cols, dst_cols, src_rows, dst_rows, ea_t, child_t, w1, b1, w2_t, b2, wu, bu,
          gamma, beta, wn_t, we_t, b, out):
    with ExitStack() as ctx:
        def sb(name, shape, dt=F32):
            return ctx.enter_context(nc.sbuf_tensor(name, shape, dt))

        def bank(name):
            return ctx.enter_context(nc.psum_tensor(name, [P, 512], F32))

        def sem(name):
            return ctx.enter_context(nc.semaphore(name))

        def sems(name, n):
            return [sem(f"{name}{k}") for k in range(n)]

        def table(name, rows, width):
            return nc.dram_tensor(name, (rows, width), F32, kind="Internal").ap()

        child_proj = table("child_proj", CROWS, D)
        sum0 = table("sum0", ROWS, D)
        sum1 = table("sum1", ROWS, D)
        y_part = table("y_part", NP, D)
        x1 = table("x1", NP, D)
        node_msg = table("node_msg", NP, TW)

        def grouped(t):
            return t[0:NP, :].rearrange("(g p k) d -> g p (k d)", p=P, k=G)

        x_g, y_g, x1_g, out_g = grouped(x), grouped(y_part), grouped(x1), grouped(out)
        sum0_g, sum1_g, msg_g = grouped(sum0), grouped(sum1), grouped(node_msg)

        ident = sb("ident", [P, P])
        before = sb("before", [P, PAIR])
        iota_p = sb("iota_p", [P, P], F16)
        iota_t = sb("iota_t", [P, TILES], F16)
        spare_row = sb("spare_row", [P, 2])
        zeros = sb("zeros", [P, STEP * D * 7 // P])
        ones = sb("ones", [EC, 1])
        hzero = sb("hzero", [P, 512], F16)
        w1_s, wu_s, w2t_s, wc_s = (sb(n, [P, D]) for n in ("w1_s", "wu_s", "w2t_s", "wc_s"))
        wn_s, we_s = sb("wn_s", [P, D]), sb("we_s", [EC, D])
        b1_s, b2_s = sb("b1_s", [P, 1]), sb("b2_s", [P, 1])
        b2_cols = sb("b2_cols", [P, P])
        bu_g, b2u_g, gamma_g, beta_g, b_g = (sb(n, [P, G * D]) for n in
                                             ("bu_g", "b2u_g", "gamma_g", "beta_g", "b_g"))
        src_i, dst_i = sb("src_i", [P, TILES], I32), sb("dst_i", [P, TILES], I32)
        src_f, dst_f = sb("src_f", [P, TILES]), sb("dst_f", [P, TILES])
        to_spare = sb("to_spare", [P, TILES])
        key_i = sb("key_i", [P, 2, TILES], I32)
        key_p, key_t = sb("key_p", [P, TILES]), sb("key_t", [P, TILES])
        neg_has = sb("neg_has", [P, TILES])
        inv_cnt = sb("inv_cnt", [P, TILES])
        cnt = sb("cnt", [P, TILES])
        onehot_p = sb("onehot_p", [P, OH, P], F16)
        onehot_t = sb("onehot_t", [P, OH, TILES], F16)
        child_in = sb("child_in", [P, CCHUNK * P])
        child_out = sb("child_out", [P, CCHUNK, D])
        keys = sb("keys", [P, 4, PAIR], I32)
        take = sb("take", [P, 4, 2], I32)
        put = sb("put", [P, 4, 2], I32)
        taken = sb("taken", [P, 4, 2, TW])
        equal = sb("equal", [P, 4, 2, PAIR])
        junk = sb("junk", [P, 2, PAIR])
        repeat = sb("repeat", [P, 4, 2])
        combined = sb("combined", [P, 4, 2, D])
        ea_s = sb("ea_s", [EC, 4, PAIR])
        ea_sq = sb("ea_sq", [EC, 4, PAIR])
        norm2 = sb("norm2", [P, 4, 2])
        norm_s = sb("norm_s", [P, 4, 2])
        inv_norm = sb("inv_norm", [P, 4, 2])
        msg = sb("msg", [P, 4, 2, D])
        x_s = sb("x_s", [P, 4, G, D])
        y_s = sb("y_s", [P, 4, G, D])
        s_s = sb("s_s", [P, 4, G, D])
        x1_s = sb("x1_s", [P, 4, G, D])
        stats = sb("stats", [P, 2, G, 6])
        mean_var = sb("mean_var", [P, 2, G, 2])
        rstd, shift, root = (sb(n, [P, 2, G]) for n in ("rstd", "shift", "root"))
        eps_col = sb("eps_col", [P, 1])
        res_n2, res_inv = sb("res_n2", [P, 4, G]), sb("res_inv", [P, 4, G])
        stats2 = sb("stats2", [P, 2, G, 6])
        mean_var2 = sb("mean_var2", [P, 2, G, 2])
        rstd2, shift2, root2 = (sb(n, [P, 2, G]) for n in ("rstd2", "shift2", "root2"))
        h_s = sb("h_s", [P, 2, G, D])
        z_s = sb("z_s", [P, 2, G, D])
        ht_s = sb("ht_s", [P, 2, G * P])
        act_s = sb("act_s", [P, G * P])
        w_s = sb("w_s", [P, 2, G, D])
        msg_s = sb("msg_s", [P, 4, G, TW])
        sq_junk = sb("sq_junk", [P, 2, G, D])

        ps_sum = [bank("ps_sum0"), bank("ps_sum1")]
        ps_edge = [bank("ps_edge0"), bank("ps_edge1")]
        ps_a, ps_b, ps_c = bank("ps_a"), bank("ps_b"), bank("ps_c")
        ps_cnt = bank("ps_cnt")

        def ln_stats(dve, src, st, mv, u, r, bn_done, var_ready):
            for k in range(G):
                ins = nc.vector.bn_stats(st[:, u, k, :], src[:, k, :])
            ins.then_inc(bn_done, 1)
            dve.wait_ge(bn_done, r + 1)
            dve.nop(nofuse=True)
            for k in range(G):
                ins = nc.vector.bn_aggr(mv[:, u, k, :], st[:, u, k, :])
            ins.then_inc(var_ready, 1)

        def ln_root(act, mv, sd, u, r, var_ready, sd_ready):
            act.wait_ge(var_ready, r + 1)
            nc.scalar.activation(sd[:, u, :], mv[:, u, :, 1], ACT.Sqrt,
                                 bias=eps_col[:, 0:1]).then_inc(sd_ready, 1)

        def ln_terms(dve, mv, sd, rs, sh, u, r, sd_ready, rs_ready, terms_ready):
            dve.wait_ge(sd_ready, r + 1)
            nc.vector.reciprocal(rs[:, u, :], sd[:, u, :]).then_inc(rs_ready, 1)
            dve.wait_ge(rs_ready, r + 1)
            nc.vector.scalar_tensor_tensor(out=sh[:, u, :], in0=mv[:, u, :, 0], scalar=-1.0,
                                           in1=rs[:, u, :], op0=ALU.mult,
                                           op1=ALU.mult).then_inc(terms_ready, 1)

        def one_hots(dve, i, first, ready, used):
            for t in range(HTILES):
                if not (first and t < OH):
                    dve.wait_ge(used, i * HTILES + t - OH + 1)
                col = bass.ds(i * HTILES + t, 1)
                nc.vector.tensor_scalar(onehot_p[:, t % OH, :], iota_p[:, :], key_p[:, col], None,
                                        ALU.is_equal)
                nc.vector.tensor_scalar(onehot_t[:, t % OH, :], iota_t[:, :], key_t[:, col], None,
                                        ALU.is_equal).then_inc(ready, 1)

        def add_counts(pe, i, ready, used):
            for t in range(HTILES):
                pe.wait_ge(ready, i * HTILES + t + 1)
                nc.tensor.matmul(ps_cnt[:, 0:TILES], onehot_p[:, t % OH, :],
                                 onehot_t[:, t % OH, :], start=False, stop=False,
                                 skip_group_check=True).then_inc(used, 1)

        def split_keys(dve, ints, done, count):
            k0, k1 = key_i[:, 0, :], key_i[:, 1, :]
            nc.vector.tensor_scalar(k0, ints[:, :], 2, P - 1, ALU.logical_shift_right,
                                    ALU.bitwise_and).then_inc(done, 1)
            dve.wait_ge(done, count)
            nc.vector.tensor_copy(key_p[:, :], k0).then_inc(done, 1)
            dve.wait_ge(done, count + 1)
            nc.vector.tensor_scalar(k0, ints[:, :], 9, 2, ALU.logical_shift_right,
                                    ALU.logical_shift_left).then_inc(done, 1)
            nc.vector.tensor_scalar(k1, ints[:, :], G - 1, None, ALU.bitwise_and).then_inc(done, 1)
            dve.wait_ge(done, count + 3)
            nc.vector.tensor_tensor(key_t[:, :], k0, k1, ALU.add).then_inc(done, 1)

        with ExitStack() as phase:
            def psem(name):
                return sem("set_" + name)

            ld_w, ld_keys, ld_small, zero_set, sum_zeroed = (psem(n) for n in
                                                             ("ld_w", "ld_keys", "ld_small", "zero_set", "sum_zeroed"))
            pool_step, consts, dve_step, b2_ready, wc_ready, wc_copied = (psem(n) for n in (
                "pool_step", "consts", "dve_step", "b2_ready", "wc_ready", "wc_copied"))
            hot_ready, hot_used, cnt_open, cnt_closed, hzeroed = (psem(n) for n in (
                "hot_ready", "hot_used", "cnt_open", "cnt_closed", "hzeroed"))
            child_ld, child_ready, child_copied, child_st = (psem(n) for n in (
                "child_ld", "child_ready", "child_copied", "child_st"))
            zero_parts = STEPS // 7
            block = phase.enter_context(nc.Block())

            @block.sync
            def _(sp):
                for t, a in ((src_i, src_cols), (dst_i, dst_cols)):
                    sp.dma_start(t[:, :], a).then_inc(ld_keys, 16)
                for t, a in ((wu_s, wu), (w2t_s, w2_t), (w1_s, w1), (wn_s, wn_t), (we_s, we_t)):
                    sp.dma_start(t[:, :], a).then_inc(ld_w, 16)
                with nc.allow_non_contiguous_dma(reason="two columns of 128"):
                    for t, a in ((b1_s, b1), (b2_s, b2)):
                        sp.dma_start(t[:, :], a.rearrange("(p a) -> p a", a=1)).then_inc(ld_w, 16)
                for t, a in ((bu_g, bu), (gamma_g, gamma), (beta_g, beta), (b_g, b)):
                    for k in range(G):
                        sp.dma_start(t[:, k * D:(k + 1) * D],
                                     a.partition_broadcast(P)).then_inc(ld_small, 16)
                with sp.Fori(0, CT // CCHUNK) as c:
                    sp.wait_ge(child_ready, c)
                    sp.dma_start(child_in[:, :],
                                 child_t[:, bass.ds(c * (CCHUNK * P), CCHUNK * P)]).then_inc(child_ld, 16)
                    sp.wait_ge(child_copied, c + 1)
                    sp.dma_start(child_proj[:, :].rearrange("(c t p) d -> c p t d", p=P, t=CCHUNK)[
                        bass.ds(c, 1)].rearrange("c p t d -> (c p) t d"),
                        child_out[:, :, :]).then_inc(child_st, 16)
                sp.wait_ge(child_st, 16 * (CT // CCHUNK))
                sp.wait_ge(ld_small, 16 * 4 * G)

            @block.gpsimd
            def _(pool):
                nc.gpsimd.memset(ident[:, :], 0.0)
                nc.gpsimd.memset(before[:, :], 1.0)
                nc.gpsimd.memset(eps_col[:, :], LN_EPS)
                nc.gpsimd.memset(ones[:, :], 1.0).then_inc(pool_step, 1)
                pool.wait_ge(pool_step, 1)
                nc.gpsimd.affine_select(out=ident[:, :], in_=ident[:, :], compare_op=ALU.not_equal,
                                        fill=1.0, base=0, pattern=[[-1, P]], channel_multiplier=1)
                nc.gpsimd.affine_select(out=before[:, P:PAIR], in_=before[:, P:PAIR],
                                        compare_op=ALU.is_gt, fill=0.0, base=0,
                                        pattern=[[-1, P]], channel_multiplier=1)
                nc.gpsimd.iota(iota_p[:, :], [[1, P]], base=0, channel_multiplier=0,
                               allow_small_or_imprecise_dtypes=True)
                nc.gpsimd.iota(iota_t[:, :], [[1, TILES]], base=0, channel_multiplier=0,
                               allow_small_or_imprecise_dtypes=True)
                nc.gpsimd.iota(spare_row[:, :], [[1, 2]], base=NP, channel_multiplier=2,
                               allow_small_or_imprecise_dtypes=True).then_inc(consts, 1)

            @block.vector
            def _(dve):
                nc.vector.memset(hzero[:, :], 0.0).then_inc(hzeroed, 1)
                nc.vector.memset(zeros[:, :], 0.0).then_inc(zero_set, 1)
                dve.wait_ge(ld_keys, 32)
                split_keys(dve, src_i, dve_step, 1)
                nc.vector.tensor_copy(src_f[:, :], src_i[:, :])
                nc.vector.tensor_copy(dst_f[:, :], dst_i[:, :]).then_inc(dve_step, 1)
                dve.wait_ge(dve_step, 6)
                dve.wait_ge(consts, 1)
                for h in range(2):
                    nc.vector.tensor_scalar(to_spare[:, h::2], src_f[:, h::2], -1.0,
                                            spare_row[:, h:h + 1], ALU.mult, ALU.add)
                dve.wait_ge(ld_w, 16 * 7)
                dve.wait_ge(consts, 1)
                nc.vector.tensor_scalar(b2_cols[:, :], ident[:, :], 0.0, b2_s[:, 0:1], ALU.mult,
                                        ALU.add).then_inc(b2_ready, 1)
                dve.wait_ge(wc_ready, 1)
                nc.vector.tensor_copy(wc_s[:, :], ps_a[:, 0:D])
                nc.vector.tensor_copy(b2u_g[:, :], ps_b[:, :]).then_inc(wc_copied, 1)
                one_hots(dve, 0, True, hot_ready, hot_used)
                with dve.Fori(1, STEPS) as i:
                    one_hots(dve, i, False, hot_ready, hot_used)
                dve.wait_ge(cnt_closed, 1)
                nc.vector.tensor_scalar(neg_has[:, :], ps_cnt[:, 0:TILES], 1.0, -1.0, ALU.min,
                                        ALU.mult)
                nc.vector.tensor_scalar(cnt[:, :], ps_cnt[:, 0:TILES], 1.0, None,
                                        ALU.max).then_inc(dve_step, 1)
                dve.wait_ge(dve_step, 7)
                nc.vector.reciprocal(inv_cnt[:, :], cnt[:, :])

            @block.tensor
            def _(pe):
                pe.wait_ge(hzeroed, 1)
                nc.tensor.matmul(ps_cnt[:, :], hzero[:, 0:P], hzero[:, :], start=True, stop=False,
                                 skip_group_check=True)
                pe.wait_ge(ld_w, 16 * 7)
                nc.tensor.matmul(ps_a[:, 0:D], w2t_s[:, :], wu_s[:, :], start=True, stop=True)
                pe.wait_ge(b2_ready, 1)
                for k in range(G):
                    ins = nc.tensor.matmul(ps_b[:, k * D:(k + 1) * D], b2_cols[:, :], wu_s[:, :],
                                           start=True, stop=True)
                ins.then_inc(wc_ready, 1)
                with pe.Fori(0, STEPS) as i:
                    add_counts(pe, i, hot_ready, hot_used)
                nc.tensor.matmul(ps_cnt[:, :], hzero[:, 0:P], hzero[:, :], start=False, stop=True,
                                 skip_group_check=True).then_inc(cnt_closed, 1)
                with pe.Fori(0, CT // CCHUNK) as c:
                    pe.wait_ge(child_ld, c * 16 + 16)
                    pe.wait_ge(child_copied, c)
                    for t in range(CCHUNK):
                        ins = nc.tensor.matmul(ps_edge[t // G][:, (t % G) * D:(t % G + 1) * D],
                                               child_in[:, t * P:(t + 1) * P], wu_s[:, :],
                                               start=True, stop=True)
                    ins.then_inc(child_ready, 1)

            @block.scalar
            def _(act):
                act.wait_ge(zero_set, 1)
                for z in range(zero_parts):
                    act.dma_start(sum0[z * 7 * STEP:(z + 1) * 7 * STEP, :].rearrange(
                        "(p r) d -> p (r d)", p=P), zeros[:, :]).then_inc(sum_zeroed, 16)
                for s in (sum0, sum1):
                    act.dma_start(s[NP:ROWS, :].rearrange("(p r) d -> p (r d)", p=P),
                                  zeros[:, 0:2 * D]).then_inc(sum_zeroed, 16)
                with act.Fori(0, CT // CCHUNK) as c:
                    act.wait_ge(child_ready, c + 1)
                    act.wait_ge(child_st, c * 16)
                    nc.scalar.copy(child_out[:, 0:G, :].rearrange("p t d -> p (t d)"),
                                   ps_edge[0][:, :])
                    nc.scalar.copy(child_out[:, G:CCHUNK, :].rearrange("p t d -> p (t d)"),
                                   ps_edge[1][:, 0:(CCHUNK - G) * D]).then_inc(child_copied, 1)
                act.wait_ge(sum_zeroed, 16 * (zero_parts + 2))

        with ExitStack() as phase:
            keys_in, x_in, y_out = sems("l0_keys_in", 4), sems("l0_x_in", 4), sems("l0_y_out", 4)
            got, added = sems("l0_got", 4), sems("l0_added", 4)
            zero1 = sem("l0_zero1")
            take_ready, eq_ready, rep_ready, put_half, put_ready, sum_ready, comb_ready = (
                sem("l0_" + n) for n in ("take_ready", "eq_ready", "rep_ready", "put_half",
                                         "put_ready", "sum_ready", "comb_ready"))
            (bn_done, var_ready, sd_ready, rs_ready, terms_ready, h_ready, tr_ready, ht_ready, hid_ready,
             act_ready, proj_ready, proj_read, y_ready) = (
                sem("l0_" + n) for n in ("bn_done", "var_ready", "sd_ready", "rs_ready", "terms_ready", "h_ready", "tr_ready", "ht_ready", "hid_ready",
                                         "act_ready", "proj_ready", "proj_read", "y_ready"))
            block = phase.enter_context(nc.Block())

            @block.sync
            def _(sp):
                def load_keys(q, s, first):
                    if not first:
                        sp.wait_ge(eq_ready, q - 3)
                    sp.dma_start(keys[:, s, :], src_rows[bass.ds(q, 1), :].rearrange(
                        "a e -> (a e)").partition_broadcast(P)).then_inc(keys_in[s], 16)

                def load_x(r, xs, first):
                    if not first:
                        sp.wait_ge(h_ready, r - 3)
                    sp.dma_start(x_s[:, xs, :, :].rearrange("p k d -> p (k d)"), x_g[
                        bass.ds(r, 1)].rearrange("a p f -> (a p) f")).then_inc(x_in[xs], 16)

                def load(i, odd, first):
                    for u in range(GROUPS_A_STEP):
                        load_x(i * 2 + u, odd * 2 + u, first)
                    for s in range(PAIRS_A_STEP):
                        load_keys(i * 4 + s, s, first)

                def step(i, odd, n, first, last):
                    if first:
                        load(0, 0, True)
                        for u in range(GROUPS_A_STEP):
                            load_x(2 + u, 2 + u, True)
                        for s in range(PAIRS_A_STEP):
                            load_keys(4 + s, s, False)
                    elif not last:
                        load(i + 1, 1 - odd, False)
                    sp.dma_start(sum1[bass.ds(i * STEP, STEP), :].rearrange(
                        "(p r) d -> p (r d)", p=P), zeros[:, 0:STEP * D // P]).then_inc(zero1, 16)
                    for u in range(GROUPS_A_STEP):
                        xs = odd * 2 + u
                        sp.wait_ge(y_ready, i * 2 + u + 1)
                        sp.dma_start(y_g[bass.ds(i * 2 + u, 1)].rearrange("a p f -> (a p) f"),
                                     y_s[:, xs, :, :].rearrange("p k d -> p (k d)")).then_inc(y_out[xs], 16)

                run_steps(sp, step)
                sp.wait_ge(zero1, 16 * STEPS)
                for xs in range(4):
                    sp.wait_ge(y_out[xs], 16 * (STEPS // 2 + (xs < 2)))

            @block.gpsimd
            def _(pool):
                def gather(q, s, first):
                    if not first:
                        pool.wait_ge(sum_ready, q - 3)
                    pool.wait_ge(take_ready, q + 1)
                    pool.nop(nofuse=True)
                    for h in range(2):
                        nc.gpsimd.indirect_dma_start(
                            taken[:, s, h, 0:D], None, child_proj[:, :],
                            bass.IndirectOffsetOnAxis(ap=take[:, s, h:h + 1], axis=0)).then_inc(got[s], 16)

                def scatter(i, s, first):
                    q = i * 4 + s
                    if s:
                        pool.wait_ge(added[s - 1], i * 32 + 32)
                    elif not first:
                        pool.wait_ge(added[3], i * 32)
                    pool.wait_ge(put_ready, q + 1)
                    pool.wait_ge(comb_ready, q + 1)
                    pool.nop(nofuse=True)
                    for h in range(2):
                        nc.gpsimd.indirect_dma_start(
                            sum0[:, :], bass.IndirectOffsetOnAxis(ap=put[:, s, h:h + 1], axis=0),
                            combined[:, s, h, :], None, compute_op=ALU.add).then_inc(added[s], 16)

                def step(i, odd, n, first, last):
                    if first:
                        gather(0, 0, True)
                        gather(1, 1, True)
                    for s in range(4):
                        if not (last and s >= 2):
                            gather(i * 4 + s + 2, (s + 2) % 4, first and s < 2)
                        scatter(i, s, first)

                run_steps(pool, step)
                for s in range(4):
                    pool.wait_ge(added[s], 32 * STEPS)

            @block.vector
            def _(dve):
                def rows_to_take(i, s, before_first):
                    if not before_first:
                        dve.wait_ge(got[s], i * 32)
                    nc.vector.tensor_scalar(take[:, s, :], dst_i[:, bass.ds((i * 4 + s) * 2, 2)],
                                            NCHILD - 1, None, ALU.min).then_inc(take_ready, 1)

                def compare(i, s, first):
                    q = i * 4 + s
                    if not first:
                        dve.wait_ge(sum_ready, q - 3)
                        dve.wait_ge(added[s], i * 32)
                    dve.wait_ge(keys_in[s], i * 16 + 16)
                    for h in range(2):
                        ins = nc.vector.tensor_scalar(equal[:, s, h, :], keys[:, s, :],
                                                      src_f[:, bass.ds(q * 2 + h, 1)], None, ALU.is_equal)
                    ins.then_inc(eq_ready, 1)
                    dve.wait_ge(eq_ready, q + 1)
                    nc.vector.tensor_tensor_reduce(
                        out=junk[:, 0, 0:P], in0=equal[:, s, 0, 0:P], in1=before[:, P:PAIR],
                        scale=1.0, scalar=0.0, op0=ALU.mult, op1=ALU.add,
                        accum_out=repeat[:, s, 0:1])
                    nc.vector.tensor_tensor_reduce(
                        out=junk[:, 1, :], in0=equal[:, s, 1, :], in1=before[:, :],
                        scale=1.0, scalar=0.0, op0=ALU.mult, op1=ALU.add,
                        accum_out=repeat[:, s, 1:2]).then_inc(rep_ready, 1)
                    dve.wait_ge(rep_ready, q + 1)
                    nc.vector.tensor_scalar(repeat[:, s, :], repeat[:, s, :], 0.0, None,
                                            ALU.is_gt).then_inc(put_half, 1)
                    dve.wait_ge(put_half, q * 2 + 1)
                    nc.vector.tensor_tensor(repeat[:, s, :], repeat[:, s, :],
                                            to_spare[:, bass.ds(q * 2, 2)], ALU.mult).then_inc(put_half, 1)
                    dve.wait_ge(put_half, q * 2 + 2)
                    nc.vector.tensor_tensor(put[:, s, :], repeat[:, s, :],
                                            src_f[:, bass.ds(q * 2, 2)], ALU.add).then_inc(put_ready, 1)

                def norm_stats(i, u, odd, n):
                    dve.wait_ge(x_in[odd * 2 + u], n * 16 + 16)
                    ln_stats(dve, x_s[:, odd * 2 + u, :, :], stats, mean_var, u, i * 2 + u, bn_done,
                             var_ready)

                def norm_terms(i, u, first):
                    r = i * 2 + u
                    if not first:
                        dve.wait_ge(h_ready, r - 1)
                    ln_terms(dve, mean_var, root, rstd, shift, u, r, sd_ready, rs_ready, terms_ready)

                def finish(i, u, odd, n, first):
                    r, xs = i * 2 + u, odd * 2 + u
                    dve.wait_ge(y_out[xs], n * 16)
                    dve.wait_ge(proj_ready, r + 1)
                    nc.vector.tensor_tensor(w_s[:, u, :, :].rearrange("p k d -> p (k d)"), ps_c[:, :],
                                            b2u_g[:, :], ALU.add).then_inc(proj_read, 1)
                    nc.vector.tensor_tensor(y_s[:, xs, :, :].rearrange("p k d -> p (k d)"),
                                            h_s[:, u, :, :].rearrange("p k d -> p (k d)"),
                                            bu_g[:, :], ALU.add).then_inc(proj_read, 1)
                    dve.wait_ge(proj_read, r * 2 + 2)
                    for k in range(G):
                        ins = nc.vector.scalar_tensor_tensor(
                            out=y_s[:, xs, k, :], in0=w_s[:, u, k, :],
                            scalar=neg_has[:, bass.ds(r * G + k, 1)], in1=y_s[:, xs, k, :],
                            op0=ALU.mult, op1=ALU.add)
                    ins.then_inc(y_ready, 1)

                def step(i, odd, n, first, last):
                    if first:
                        rows_to_take(0, 0, True)
                        rows_to_take(0, 1, True)

                    def pair(s):
                        if s < 2:
                            rows_to_take(i, s + 2, first)
                        elif not last:
                            rows_to_take(i + 1, s - 2, False)
                        compare(i, s, first)

                    if first:
                        norm_stats(0, 0, 0, 0)
                        norm_terms(0, 0, True)
                    norm_stats(i, 1, odd, n)
                    pair(0)
                    norm_terms(i, 1, first)
                    pair(1)
                    finish(i, 0, odd, n, first)
                    if not last:
                        norm_stats(i + 1, 0, 1 - odd, n + 1 if odd else n)
                    pair(2)
                    if not last:
                        norm_terms(i + 1, 0, False)
                    pair(3)
                    finish(i, 1, odd, n, first)

                run_steps(dve, step)

            @block.tensor
            def _(pe):
                def pair_sums(i, s, first):
                    q = i * 4 + s
                    if not (first and s < 2):
                        pe.wait_ge(comb_ready, q - 1)
                    pe.wait_ge(eq_ready, q + 1)
                    pe.wait_ge(got[s], i * 32 + 32)
                    for to in range(2):
                        for h in range(2):
                            ins = nc.tensor.matmul(ps_sum[s % 2][:, to * D:(to + 1) * D],
                                                   equal[:, s, h, to * P:(to + 1) * P],
                                                   taken[:, s, h, 0:D], start=(h == 0), stop=(h == 1))
                    ins.then_inc(sum_ready, 1)

                def turn(r, u):
                    pe.wait_ge(h_ready, r + 1)
                    for k in range(G):
                        ins = nc.tensor.transpose(ps_a[:, k * P:(k + 1) * P], h_s[:, u, k, :],
                                                  ident[:, :])
                    ins.then_inc(tr_ready, 1)

                def hidden(r):
                    pe.wait_ge(ht_ready, r + 1)
                    nc.tensor.matmul(ps_b[:, :], w1_s[:, :], ht_s[:, 0, :], start=True,
                                     stop=True).then_inc(hid_ready, 1)

                def project(r):
                    pe.wait_ge(proj_read, r * 2)
                    pe.wait_ge(act_ready, r + 1)
                    for k in range(G):
                        ins = nc.tensor.matmul(ps_c[:, k * D:(k + 1) * D],
                                               act_s[:, k * P:(k + 1) * P], wc_s[:, :],
                                               start=True, stop=True)
                    ins.then_inc(proj_ready, 1)

                def step(i, odd, n, first, last):
                    for u in range(GROUPS_A_STEP):
                        r = i * 2 + u
                        turn(r, u)
                        pair_sums(i, 2 * u, first)
                        hidden(r)
                        pair_sums(i, 2 * u + 1, first)
                        project(r)

                run_steps(pe, step)

            @block.scalar
            def _(act):
                def copy_sums(i, s, first):
                    q = i * 4 + s
                    if not first:
                        act.wait_ge(added[s], i * 32)
                    act.wait_ge(sum_ready, q + 1)
                    nc.scalar.copy(combined[:, s, :, :].rearrange("p h d -> p (h d)"),
                                   ps_sum[s % 2][:, 0:2 * D]).then_inc(comb_ready, 1)

                def step(i, odd, n, first, last):
                    if first:
                        ln_root(act, mean_var, root, 0, 0, var_ready, sd_ready)
                    for u in range(GROUPS_A_STEP):
                        r, xs = i * 2 + u, odd * 2 + u
                        if not first:
                            act.wait_ge(y_ready, r - 1)
                        act.wait_ge(terms_ready, r + 1)
                        act.wait_ge(x_in[xs], n * 16 + 16)
                        for k in range(G):
                            ins = nc.scalar.activation(h_s[:, u, k, :], x_s[:, xs, k, :], ACT.Relu,
                                                       bias=shift[:, u, k:k + 1],
                                                       scale=rstd[:, u, k:k + 1])
                        ins.then_inc(h_ready, 1)
                        if not (last and u):
                            ln_root(act, mean_var, root, 1 - u, r + 1, var_ready, sd_ready)
                        copy_sums(i, 2 * u, first)
                        act.wait_ge(tr_ready, r + 1)
                        nc.scalar.copy(ht_s[:, 0, :], ps_a[:, :]).then_inc(ht_ready, 1)
                        copy_sums(i, 2 * u + 1, first)
                        act.wait_ge(proj_ready, r)
                        act.wait_ge(hid_ready, r + 1)
                        nc.scalar.activation(act_s[:, :], ps_b[:, :], ACT.Relu,
                                             bias=b1_s[:, 0:1]).then_inc(act_ready, 1)

                run_steps(act, step)

        with ExitStack() as phase:
            x_in, y_in, s_in, x1_out, m_out = (sems("up_" + n, 4) for n in
                                               ("x_in", "y_in", "s_in", "x1_out", "m_out"))
            y_step, z_ready, x1_half, x1_ready, h_ready, nh_ready = (
                sem("up_" + n) for n in ("y_step", "z_ready", "x1_half", "x1_ready", "h_ready",
                                         "nh_ready"))
            bn_done, var_ready, sd_ready, rs_ready, terms_ready = (
                sem("up_" + n) for n in ("bn_done", "var_ready", "sd_ready", "rs_ready", "terms_ready"))
            bn2_done, var2_ready, sd2_ready, rs2_ready, terms2_ready = (
                sem("up_" + n) for n in ("bn2_done", "var2_ready", "sd2_ready", "rs2_ready",
                                         "terms2_ready"))
            xb_ready, tr_ready, ht_ready, proj_ready, m_ready = (sem("up_" + n) for n in (
                "xb_ready", "tr_ready", "ht_ready", "proj_ready", "m_ready"))
            tr_bank, proj_bank = [ps_a, ps_b], [ps_c, ps_edge[0]]
            block = phase.enter_context(nc.Block())

            @block.sync
            def _(sp):
                def load(i, odd, first):
                    for u in range(GROUPS_A_STEP):
                        r, xs = i * 2 + u, odd * 2 + u
                        if not first:
                            sp.wait_ge(x1_ready, r - 3)
                        for t, a, s in ((x_s, x_g, x_in), (y_s, y_g, y_in), (s_s, sum0_g, s_in)):
                            sp.dma_start(t[:, xs, :, :].rearrange("p k d -> p (k d)"), a[
                                bass.ds(r, 1)].rearrange("a p f -> (a p) f")).then_inc(s[xs], 16)

                def step(i, odd, n, first, last):
                    if first:
                        load(0, 0, True)
                        load(1, 1, True)
                    elif not last:
                        load(i + 1, 1 - odd, False)
                    for u in range(GROUPS_A_STEP):
                        r, xs = i * 2 + u, odd * 2 + u
                        sp.wait_ge(x1_ready, r + 1)
                        sp.dma_start(x1_g[bass.ds(r, 1)].rearrange("a p f -> (a p) f"),
                                     x1_s[:, xs, :, :].rearrange("p k d -> p (k d)")).then_inc(x1_out[xs], 16)

                run_steps(sp, step)
                for xs in range(4):
                    sp.wait_ge(x1_out[xs], 16 * (STEPS // 2 + (xs < 2)))

            @block.gpsimd
            def _(pool):
                def step(i, odd, n, first, last):
                    for u in range(GROUPS_A_STEP):
                        xs = odd * 2 + u
                        pool.wait_ge(x_in[xs], n * 16 + 16)
                        nc.gpsimd.tensor_tensor(x_s[:, xs, :, :].rearrange("p k d -> p (k d)"),
                                                x_s[:, xs, :, :].rearrange("p k d -> p (k d)"),
                                                beta_g[:, :], ALU.add).then_inc(xb_ready, 1)

                run_steps(pool, step)

            @block.vector
            def _(dve):
                def y_terms(i, u, odd, n, first):
                    r, xs = i * 2 + u, odd * 2 + u
                    dve.wait_ge(y_in[xs], n * 16 + 16)
                    dve.wait_ge(s_in[xs], n * 16 + 16)
                    for k in range(G):
                        ins = nc.vector.scalar_tensor_tensor(
                            out=y_s[:, xs, k, :], in0=s_s[:, xs, k, :],
                            scalar=inv_cnt[:, bass.ds(r * G + k, 1)], in1=y_s[:, xs, k, :],
                            op0=ALU.mult, op1=ALU.add)
                    ins.then_inc(y_step, 1)
                    dve.wait_ge(y_step, r + 1)
                    ln_stats(dve, y_s[:, xs, :, :], stats, mean_var, u, r, bn_done, var_ready)

                def z_norm(i, u, first):
                    r = i * 2 + u
                    if not first:
                        dve.wait_ge(z_ready, r - 1)
                    ln_terms(dve, mean_var, root, rstd, shift, u, r, sd_ready, rs_ready, terms_ready)

                def x1_terms(i, u, odd, n, first):
                    r, xs = i * 2 + u, odd * 2 + u
                    dve.wait_ge(z_ready, r + 1)
                    z, xo = (t.rearrange("p k d -> p (k d)") for t in (z_s[:, u, :, :], x1_s[:, xs, :, :]))
                    nc.vector.tensor_tensor(z, z, gamma_g[:, :], ALU.mult).then_inc(x1_half, 1)
                    dve.wait_ge(x1_out[xs], n * 16)
                    dve.wait_ge(xb_ready, r + 1)
                    dve.wait_ge(x1_half, r + 1)
                    nc.vector.tensor_tensor(xo, z, x_s[:, xs, :, :].rearrange("p k d -> p (k d)"),
                                            ALU.add).then_inc(x1_ready, 1)
                    dve.wait_ge(x1_ready, r + 1)
                    ln_stats(dve, x1_s[:, xs, :, :], stats2, mean_var2, u, r, bn2_done, var2_ready)

                def h_norm(i, u, first):
                    r = i * 2 + u
                    if not first:
                        dve.wait_ge(h_ready, r - 1)
                    ln_terms(dve, mean_var2, root2, rstd2, shift2, u, r, sd2_ready, rs2_ready,
                             terms2_ready)

                def messages(i, u, odd, n, first):
                    r, xs = i * 2 + u, odd * 2 + u
                    dve.wait_ge(m_out[xs], n * 16)
                    dve.wait_ge(proj_ready, r + 1)
                    nc.vector.tensor_copy(msg_s[:, xs, :, 0:D], proj_bank[u][:, :].rearrange(
                        "p (k d) -> p k d", k=G)).then_inc(m_ready, 1)

                def step(i, odd, n, first, last):
                    if first:
                        y_terms(0, 0, 0, 0, True)
                        y_terms(0, 1, 0, 0, True)
                        z_norm(0, 0, True)
                    for u in range(GROUPS_A_STEP):
                        x1_terms(i, u, odd, n, first)
                        if not u:
                            z_norm(i, 1, first)
                        elif not last:
                            z_norm(i + 1, 0, False)
                        if not last:
                            y_terms(i + 1, u, 1 - odd, n + 1 if odd else n, False)
                        h_norm(i, u, first)
                        if u:
                            messages(i, 0, odd, n, first)
                    messages(i, 1, odd, n, first)

                run_steps(dve, step)

            @block.tensor
            def _(pe):
                def step(i, odd, n, first, last):
                    for u in range(GROUPS_A_STEP):
                        r = i * 2 + u
                        if not first:
                            pe.wait_ge(ht_ready, r - 1)
                        pe.wait_ge(h_ready, r + 1)
                        for k in range(G):
                            ins = nc.tensor.transpose(tr_bank[u][:, k * P:(k + 1) * P],
                                                      h_s[:, u, k, :], ident[:, :])
                        ins.then_inc(tr_ready, 1)
                        if not first:
                            pe.wait_ge(m_ready, r - 1)
                        pe.wait_ge(ht_ready, r + 1)
                        for k in range(G):
                            ins = nc.tensor.matmul(proj_bank[u][:, k * D:(k + 1) * D],
                                                   ht_s[:, u, k * P:(k + 1) * P], wn_s[:, :],
                                                   start=True, stop=True)
                        ins.then_inc(proj_ready, 1)

                run_steps(pe, step)

            @block.scalar
            def _(act):
                def z_terms(i, u, odd, n, first):
                    r, xs = i * 2 + u, odd * 2 + u
                    if not first:
                        act.wait_ge(x1_ready, r - 1)
                    act.wait_ge(terms_ready, r + 1)
                    for k in range(G):
                        ins = nc.scalar.activation(z_s[:, u, k, :], y_s[:, xs, k, :], ACT.Identity,
                                                   bias=shift[:, u, k:k + 1],
                                                   scale=rstd[:, u, k:k + 1])
                    ins.then_inc(z_ready, 1)

                def h_terms(i, u, odd, n, first):
                    r, xs = i * 2 + u, odd * 2 + u
                    if not first:
                        act.wait_ge(tr_ready, r - 1)
                    act.wait_ge(terms2_ready, r + 1)
                    for k in range(G):
                        ins = nc.scalar.activation(h_s[:, u, k, :], x1_s[:, xs, k, :], ACT.Relu,
                                                   bias=shift2[:, u, k:k + 1],
                                                   scale=rstd2[:, u, k:k + 1])
                    ins.then_inc(h_ready, 1)
                    act.wait_ge(m_out[xs], n * 16)
                    act.wait_ge(h_ready, r + 1)
                    for k in range(G):
                        ins = nc.scalar.activation(sq_junk[:, u, k, :], h_s[:, u, k, :], ACT.Square,
                                                   accum_out=msg_s[:, xs, k, D:TW])
                    ins.then_inc(nh_ready, 1)
                    if not first:
                        act.wait_ge(proj_ready, r - 1)
                    act.wait_ge(tr_ready, r + 1)
                    nc.scalar.copy(ht_s[:, u, :], tr_bank[u][:, :]).then_inc(ht_ready, 1)

                def store(i, u, odd):
                    r, xs = i * 2 + u, odd * 2 + u
                    act.wait_ge(m_ready, r + 1)
                    act.wait_ge(nh_ready, r + 1)
                    act.dma_start(msg_g[bass.ds(r, 1)].rearrange("a p f -> (a p) f"),
                                  msg_s[:, xs, :, :].rearrange("p k d -> p (k d)")).then_inc(m_out[xs], 16)

                def step(i, odd, n, first, last):
                    if first:
                        ln_root(act, mean_var, root, 0, 0, var_ready, sd_ready)
                        ln_root(act, mean_var, root, 1, 1, var_ready, sd_ready)
                        z_terms(0, 0, 0, 0, True)
                    for u in range(GROUPS_A_STEP):
                        ln_root(act, mean_var2, root2, u, i * 2 + u, var2_ready, sd2_ready)
                        if not u:
                            z_terms(i, 1, odd, n, first)
                        elif not last:
                            z_terms(i + 1, 0, 1 - odd, n, False)
                        if not last:
                            ln_root(act, mean_var, root, u, i * 2 + u + 2, var_ready, sd_ready)
                        h_terms(i, u, odd, n, first)
                        if u:
                            store(i, 0, odd)
                    store(i, 1, odd)

                run_steps(act, step)
                for xs in range(4):
                    act.wait_ge(m_out[xs], 16 * (STEPS // 2 + (xs < 2)))

        with ExitStack() as phase:
            keys_in, ea_in, got, added = (sems("l1_" + n, 4) for n in ("keys_in", "ea_in", "got", "added"))
            (take_ready, eq_ready, rep_ready, put_half, put_ready, sum_ready, comb_ready, sq_ready,
             edge_ready, n2_ready, n2_added, n2_root, m_ready, hot_ready, hot_used, key_step, cnt_open,
             cnt_closed, spare_ready) = (
                sem("l1_" + n) for n in (
                    "take_ready", "eq_ready", "rep_ready", "put_half", "put_ready", "sum_ready",
                    "comb_ready", "sq_ready", "edge_ready", "n2_ready", "n2_added", "n2_root", "m_ready",
                    "hot_ready", "hot_used", "key_step", "cnt_open", "cnt_closed", "spare_ready"))
            inv_ready = sem("l1_inv_ready")
            NRM = 2 * D
            block = phase.enter_context(nc.Block())

            @block.sync
            def _(sp):
                def load(i, first):
                    for s in range(PAIRS_A_STEP):
                        q = i * 4 + s
                        if not first:
                            sp.wait_ge(edge_ready, q - 3)
                        sp.dma_start(ea_s[:, s, :], ea_t[:, bass.ds(q * PAIR, PAIR)]).then_inc(ea_in[s], 16)
                        if not first:
                            sp.wait_ge(eq_ready, q - 3)
                        sp.dma_start(keys[:, s, :], dst_rows[bass.ds(q, 1), :].rearrange(
                            "a e -> (a e)").partition_broadcast(P)).then_inc(keys_in[s], 16)

                load(0, True)
                with sp.Fori(1, STEPS) as i:
                    load(i, False)

            @block.gpsimd
            def _(pool):
                def gather(q, s, first):
                    if not first:
                        pool.wait_ge(m_ready, q - 3)
                    pool.wait_ge(take_ready, q + 1)
                    pool.nop(nofuse=True)
                    for h in range(2):
                        nc.gpsimd.indirect_dma_start(
                            taken[:, s, h, :], None, node_msg[:, :],
                            bass.IndirectOffsetOnAxis(ap=take[:, s, h:h + 1], axis=0)).then_inc(got[s], 16)

                def scatter(i, s, first):
                    q = i * 4 + s
                    if s:
                        pool.wait_ge(added[s - 1], i * 32 + 32)
                    elif not first:
                        pool.wait_ge(added[3], i * 32)
                    pool.wait_ge(put_ready, q + 1)
                    pool.wait_ge(comb_ready, q + 1)
                    pool.nop(nofuse=True)
                    for h in range(2):
                        nc.gpsimd.indirect_dma_start(
                            sum1[:, :], bass.IndirectOffsetOnAxis(ap=put[:, s, h:h + 1], axis=0),
                            combined[:, s, h, :], None, compute_op=ALU.add).then_inc(added[s], 16)

                def step(i, odd, n, first, last):
                    if first:
                        gather(0, 0, True)
                        gather(1, 1, True)
                    for s in range(4):
                        if not (last and s >= 2):
                            gather(i * 4 + s + 2, (s + 2) % 4, first and s < 2)
                        scatter(i, s, first)

                run_steps(pool, step)
                for s in range(4):
                    pool.wait_ge(added[s], 32 * STEPS)

            @block.vector
            def _(dve):
                def rows_to_take(i, s, before_first):
                    if not before_first:
                        dve.wait_ge(got[s], i * 32)
                    nc.vector.tensor_scalar(take[:, s, :], src_i[:, bass.ds((i * 4 + s) * 2, 2)],
                                            0, None, ALU.max).then_inc(take_ready, 1)

                def messages(i, s, first):
                    q = i * 4 + s
                    if not first:
                        dve.wait_ge(sum_ready, q - 3)
                    dve.wait_ge(edge_ready, q + 1)
                    dve.wait_ge(got[s], i * 32 + 32)
                    nc.vector.tensor_tensor(norm2[:, s, :], ps_edge[s % 2][:, NRM:NRM + 2],
                                            taken[:, s, :, D], ALU.add).then_inc(n2_added, 1)
                    nc.vector.tensor_tensor(msg[:, s, :, :], ps_edge[s % 2][:, 0:NRM].rearrange(
                        "p (h d) -> p h d", h=2), taken[:, s, :, 0:D], ALU.add).then_inc(m_ready, 1)
                    dve.wait_ge(n2_added, q + 1)
                    nc.vector.tensor_scalar(norm2[:, s, :], norm2[:, s, :], L2_EPS * L2_EPS, None,
                                            ALU.max).then_inc(n2_ready, 1)

                def compare(i, s, first):
                    q = i * 4 + s
                    if not first:
                        dve.wait_ge(added[s], i * 32)
                    dve.wait_ge(keys_in[s], i * 16 + 16)
                    dve.wait_ge(n2_root, q + 1)
                    nc.vector.reciprocal(inv_norm[:, s, :], norm_s[:, s, :]).then_inc(inv_ready, 1)
                    dve.wait_ge(inv_ready, q + 1)
                    for h in range(2):
                        ins = nc.vector.tensor_scalar(equal[:, s, h, :], keys[:, s, :],
                                                      dst_f[:, bass.ds(q * 2 + h, 1)],
                                                      inv_norm[:, s, h:h + 1], ALU.is_equal, ALU.mult)
                    ins.then_inc(eq_ready, 1)
                    dve.wait_ge(eq_ready, q + 1)
                    nc.vector.tensor_tensor_reduce(
                        out=junk[:, 0, 0:P], in0=equal[:, s, 0, 0:P], in1=before[:, P:PAIR],
                        scale=1.0, scalar=0.0, op0=ALU.mult, op1=ALU.add,
                        accum_out=repeat[:, s, 0:1])
                    nc.vector.tensor_tensor_reduce(
                        out=junk[:, 1, :], in0=equal[:, s, 1, :], in1=before[:, :],
                        scale=1.0, scalar=0.0, op0=ALU.mult, op1=ALU.add,
                        accum_out=repeat[:, s, 1:2]).then_inc(rep_ready, 1)
                    dve.wait_ge(rep_ready, q + 1)
                    nc.vector.tensor_scalar(repeat[:, s, :], repeat[:, s, :], 0.0, None,
                                            ALU.is_gt).then_inc(put_half, 1)
                    dve.wait_ge(put_half, q * 2 + 1)
                    nc.vector.tensor_tensor(repeat[:, s, :], repeat[:, s, :],
                                            to_spare[:, bass.ds(q * 2, 2)], ALU.mult).then_inc(put_half, 1)
                    dve.wait_ge(put_half, q * 2 + 2)
                    nc.vector.tensor_tensor(put[:, s, :], repeat[:, s, :],
                                            dst_f[:, bass.ds(q * 2, 2)], ALU.add).then_inc(put_ready, 1)

                def step(i, odd, n, first, last):
                    if first:
                        rows_to_take(0, 0, True)
                        rows_to_take(0, 1, True)
                        messages(0, 0, True)
                        split_keys(dve, dst_i, key_step, 1)
                        for h in range(2):
                            ins = nc.vector.tensor_scalar(to_spare[:, h::2], dst_f[:, h::2], -1.0,
                                                          spare_row[:, h:h + 1], ALU.mult, ALU.add)
                        ins.then_inc(spare_ready, 1)
                        dve.wait_ge(spare_ready, 1)
                        dve.wait_ge(key_step, 5)
                    for s in range(4):
                        if s < 2:
                            rows_to_take(i, s + 2, first)
                        elif not last:
                            rows_to_take(i + 1, s - 2, False)
                        if s < 3:
                            messages(i, s + 1, first)
                        elif not last:
                            messages(i + 1, 0, False)
                        compare(i, s, first)
                    one_hots(dve, i, first, hot_ready, hot_used)

                run_steps(dve, step)
                dve.wait_ge(cnt_closed, 1)
                nc.vector.tensor_scalar(cnt[:, :], ps_cnt[:, 0:TILES], 1.0, None,
                                        ALU.max).then_inc(key_step, 1)
                dve.wait_ge(key_step, 6)
                nc.vector.reciprocal(inv_cnt[:, :], cnt[:, :])

            @block.tensor
            def _(pe):
                nc.tensor.matmul(ps_cnt[:, :], hzero[:, 0:P], hzero[:, :], start=True, stop=False,
                                 skip_group_check=True)

                def edge_parts(i, s, first):
                    q = i * 4 + s
                    if not first:
                        pe.wait_ge(m_ready, q - 1)
                        pe.wait_ge(n2_added, q - 1)
                    pe.wait_ge(ea_in[s], i * 16 + 16)
                    for h in range(2):
                        nc.tensor.matmul(ps_edge[s % 2][:, h * D:(h + 1) * D],
                                         ea_s[:, s, h * P:(h + 1) * P], we_s[:, :],
                                         start=True, stop=True)
                    pe.wait_ge(sq_ready, q + 1)
                    for h in range(2):
                        ins = nc.tensor.matmul(ps_edge[s % 2][:, NRM + h:NRM + h + 1],
                                               ea_sq[:, s, h * P:(h + 1) * P], ones[:, :],
                                               start=True, stop=True)
                    ins.then_inc(edge_ready, 1)

                def pair_sums(i, s, first):
                    q = i * 4 + s
                    if not (first and s < 2):
                        pe.wait_ge(comb_ready, q - 1)
                    pe.wait_ge(eq_ready, q + 1)
                    pe.wait_ge(m_ready, q + 1)
                    for to in range(2):
                        for h in range(2):
                            ins = nc.tensor.matmul(ps_sum[s % 2][:, to * D:(to + 1) * D],
                                                   equal[:, s, h, to * P:(to + 1) * P],
                                                   msg[:, s, h, :], start=(h == 0), stop=(h == 1))
                    ins.then_inc(sum_ready, 1)

                def step(i, odd, n, first, last):
                    if first:
                        edge_parts(0, 0, True)
                    for s in range(4):
                        if s < 3:
                            edge_parts(i, s + 1, first and s < 1)
                        elif not last:
                            edge_parts(i + 1, 0, False)
                        pair_sums(i, s, first)
                    add_counts(pe, i, hot_ready, hot_used)

                run_steps(pe, step)
                nc.tensor.matmul(ps_cnt[:, :], hzero[:, 0:P], hzero[:, :], start=False, stop=True,
                                 skip_group_check=True).then_inc(cnt_closed, 1)

            @block.scalar
            def _(act):
                def squares(i, s, first):
                    q = i * 4 + s
                    if not first:
                        act.wait_ge(edge_ready, q - 3)
                    act.wait_ge(ea_in[s], i * 16 + 16)
                    nc.scalar.activation(ea_sq[:, s, :], ea_s[:, s, :],
                                         ACT.Square).then_inc(sq_ready, 1)

                def roots(i, s):
                    act.wait_ge(n2_ready, i * 4 + s + 1)
                    nc.scalar.activation(norm_s[:, s, :], norm2[:, s, :],
                                         ACT.Sqrt).then_inc(n2_root, 1)

                def copy_sums(i, s, first):
                    q = i * 4 + s
                    if not first:
                        act.wait_ge(added[s], i * 32)
                    act.wait_ge(sum_ready, q + 1)
                    nc.scalar.copy(combined[:, s, :, :].rearrange("p h d -> p (h d)"),
                                   ps_sum[s % 2][:, 0:2 * D]).then_inc(comb_ready, 1)

                def step(i, odd, n, first, last):
                    if first:
                        squares(0, 0, True)
                        squares(0, 1, True)
                        roots(0, 0)
                    for s in range(4):
                        if s < 2:
                            squares(i, s + 2, first)
                        elif not last:
                            squares(i + 1, s - 2, False)
                        if s < 3:
                            roots(i, s + 1)
                        elif not last:
                            roots(i + 1, 0)
                        copy_sums(i, s, first)

                run_steps(act, step)

        with ExitStack() as phase:
            x1_in, s_in, res_out = (sems("out_" + n, 4) for n in ("x1_in", "s_in", "res_out"))
            o_ready, n_ready, max_ready, rn_ready, root_ready, res_ready = (
                sem("out_" + n) for n in ("o_ready", "n_ready", "max_ready", "rn_ready", "root_ready",
                                          "res_ready"))
            block = phase.enter_context(nc.Block())

            @block.sync
            def _(sp):
                def load(i, odd, first):
                    for u in range(GROUPS_A_STEP):
                        r, xs = i * 2 + u, odd * 2 + u
                        if not first:
                            sp.wait_ge(res_ready, r - 3)
                        for t, a, s in ((x_s, x1_g, x1_in), (s_s, sum1_g, s_in)):
                            sp.dma_start(t[:, xs, :, :].rearrange("p k d -> p (k d)"), a[
                                bass.ds(r, 1)].rearrange("a p f -> (a p) f")).then_inc(s[xs], 16)

                def step(i, odd, n, first, last):
                    if first:
                        load(0, 0, True)
                        load(1, 1, True)
                    elif not last:
                        load(i + 1, 1 - odd, False)
                    for u in range(GROUPS_A_STEP):
                        r, xs = i * 2 + u, odd * 2 + u
                        sp.wait_ge(res_ready, r + 1)
                        sp.dma_start(out_g[bass.ds(r, 1)].rearrange("a p f -> (a p) f"),
                                     y_s[:, xs, :, :].rearrange("p k d -> p (k d)")).then_inc(res_out[xs], 16)

                run_steps(sp, step)
                for xs in range(4):
                    sp.wait_ge(res_out[xs], 16 * (STEPS // 2 + (xs < 2)))

            @block.vector
            def _(dve):
                def rows(i, u, odd, n):
                    r, xs = i * 2 + u, odd * 2 + u
                    dve.wait_ge(s_in[xs], n * 16 + 16)
                    for k in range(G):
                        ins = nc.vector.scalar_tensor_tensor(
                            out=s_s[:, xs, k, :], in0=s_s[:, xs, k, :],
                            scalar=inv_cnt[:, bass.ds(r * G + k, 1)], in1=b_g[:, k * D:(k + 1) * D],
                            op0=ALU.mult, op1=ALU.add)
                    ins.then_inc(o_ready, 1)

                def inverse(i, u, odd):
                    r, xs = i * 2 + u, odd * 2 + u
                    dve.wait_ge(n_ready, r + 1)
                    nc.vector.tensor_scalar(res_n2[:, xs, :], res_n2[:, xs, :], L2_EPS * L2_EPS,
                                            None, ALU.max).then_inc(max_ready, 1)
                    dve.wait_ge(max_ready, r + 1)
                    nc.vector.reciprocal(res_n2[:, xs, :], res_n2[:, xs, :]).then_inc(rn_ready, 1)

                def result(i, u, odd, n):
                    r, xs = i * 2 + u, odd * 2 + u
                    dve.wait_ge(x1_in[xs], n * 16 + 16)
                    dve.wait_ge(res_out[xs], n * 16)
                    dve.wait_ge(root_ready, r + 1)
                    for k in range(G):
                        ins = nc.vector.scalar_tensor_tensor(
                            out=y_s[:, xs, k, :], in0=s_s[:, xs, k, :], scalar=res_inv[:, xs, k:k + 1],
                            in1=x_s[:, xs, k, :], op0=ALU.mult, op1=ALU.add)
                    ins.then_inc(res_ready, 1)

                def step(i, odd, n, first, last):
                    if first:
                        rows(0, 0, 0, 0)
                        rows(0, 1, 0, 0)
                        inverse(0, 0, 0)
                    for u in range(GROUPS_A_STEP):
                        if not last:
                            rows(i + 1, u, 1 - odd, n + 1 if odd else n)
                        if not u:
                            inverse(i, 1, odd)
                        elif not last:
                            inverse(i + 1, 0, 1 - odd)
                        result(i, u, odd, n)

                run_steps(dve, step)

            @block.scalar
            def _(act):
                def squares(i, u, odd, first):
                    r, xs = i * 2 + u, odd * 2 + u
                    if not first:
                        act.wait_ge(n_ready, r - 1)
                    act.wait_ge(o_ready, r + 1)
                    for k in range(G):
                        ins = nc.scalar.activation(sq_junk[:, u, k, :], s_s[:, xs, k, :], ACT.Square,
                                                   accum_out=res_n2[:, xs, k:k + 1])
                    ins.then_inc(n_ready, 1)

                def roots(i, u, odd, first):
                    r, xs = i * 2 + u, odd * 2 + u
                    if not first:
                        act.wait_ge(res_ready, r - 3)
                    act.wait_ge(rn_ready, r + 1)
                    nc.scalar.activation(res_inv[:, xs, :], res_n2[:, xs, :],
                                         ACT.Sqrt).then_inc(root_ready, 1)

                def step(i, odd, n, first, last):
                    if first:
                        squares(0, 0, 0, True)
                        squares(0, 1, 0, True)
                        roots(0, 0, 0, True)
                    for u in range(GROUPS_A_STEP):
                        if not last:
                            squares(i + 1, u, 1 - odd, False)
                        if not u:
                            roots(i, 1, odd, first)
                        elif not last:
                            roots(i + 1, 0, 1 - odd, first)

                run_steps(act, step)


def kernel(x, src, dst, edge_attr_64, L0_gnn_x_child, L0_gnn_W1, L0_gnn_b1, L0_gnn_W2, L0_gnn_b2,
           L0_gnn_Wu, L0_gnn_bu, L0_gnn_gamma, L0_gnn_beta, L1_gnn_W, L1_gnn_b):
    import numpy as np
    import concourse.bacc as bacc
    from concourse.bass_utils import run_bass_kernel_spmd

    def pad(a, rows, fill=0):
        a = np.asarray(a)
        return np.concatenate([a, np.full((rows - a.shape[0],) + a.shape[1:], fill, a.dtype)])

    src_p, dst_p = pad(src, NP, N), pad(dst, NP, N)
    w_t = np.ascontiguousarray(np.asarray(L1_gnn_W).T)
    arrays = {
        "x": pad(x, NP),
        "src_cols": np.ascontiguousarray(src_p.reshape(TILES, P).T),
        "dst_cols": np.ascontiguousarray(dst_p.reshape(TILES, P).T),
        "src_rows": src_p.reshape(PAIRS, PAIR),
        "dst_rows": dst_p.reshape(PAIRS, PAIR),
        "ea_t": np.ascontiguousarray(pad(edge_attr_64, NP).T),
        "child_t": np.ascontiguousarray(pad(L0_gnn_x_child, CROWS).T),
        "w1": np.asarray(L0_gnn_W1), "b1": np.asarray(L0_gnn_b1),
        "w2_t": np.ascontiguousarray(np.asarray(L0_gnn_W2).T), "b2": np.asarray(L0_gnn_b2),
        "wu": np.asarray(L0_gnn_Wu), "bu": np.asarray(L0_gnn_bu),
        "gamma": np.asarray(L0_gnn_gamma), "beta": np.asarray(L0_gnn_beta),
        "wn_t": np.ascontiguousarray(w_t[:D]), "we_t": np.ascontiguousarray(w_t[D:]),
        "b": np.asarray(L1_gnn_b),
    }
    nc = bacc.Bacc("TRN2", target_bir_lowering=False, num_devices=1)
    args = [nc.dram_tensor(f"in_{name}", a.shape, mybir.dt.from_np(a.dtype), kind="ExternalInput").ap()
            for name, a in arrays.items()]
    args.append(nc.dram_tensor("out", (NP, D), F32, kind="ExternalOutput").ap())
    build(nc, *args)
    r = run_bass_kernel_spmd(nc, [{f"in_{name}": a for name, a in arrays.items()}], core_ids=[0])
    return r.results[0]["out"][:N]
```

```python
from contextlib import ExitStack

import concourse.bass as bass
from concourse import mybir

P = 128
D = 128
N = 50000
E = 50000
NCHILD = 6250
EC = 64
LN_EPS = 1e-5
L2_EPS = 1e-12

G = 4
UNIT = G * P
UNROLL = 4
UNITS = -(-max(N, E) // (2 * UNIT)) * 2
NP = UNITS * UNIT
TILES = NP // P
ROWS = NP + UNIT
CT = -(-NCHILD // P)
CROWS = CT * P
CCHUNK = 7
TAIL = 6
PARTS = 3
TW = D + 1
RES = 2
RES_SLOTS = -(-UNITS // UNROLL) * RES
HT = 8
SQ = [b * (b + 1) // 2 * P for b in range(G + 1)]
assert CT % CCHUNK == 0 and TILES % HT == 0 and NP > N and NP > E

ALU = mybir.AluOpType
ACT = mybir.ActivationFunctionType
F32 = mybir.dt.float32
F16 = mybir.dt.float16
BF16 = mybir.dt.bfloat16
I32 = mybir.dt.int32


class Unit:

    def __init__(self, r, c, n):
        self.r, self.c, self.n = r, c, n
        self.c2 = c % 2
        self.stays = c < RES
        self.place = n * RES + c
        self.d = c - RES

    def ahead(self, d):
        if isinstance(self.r, int) and not 0 <= self.r + d < UNITS:
            return None
        return Unit(self.r + d, (self.c + d) % UNROLL, self.n + (self.c + d) // UNROLL)


def due(count):
    return not isinstance(count, int) or count > 0


def run_units(eng, step, lead):
    for r in range(-lead, UNROLL):
        step(Unit(r, r % UNROLL, r // UNROLL))
    turns = (UNITS - TAIL) // UNROLL
    with eng.Fori(1, turns) as n:
        for c in range(UNROLL):
            step(Unit(n * UNROLL + c, c, n))
    for r in range(turns * UNROLL, UNITS):
        step(Unit(r, r % UNROLL, r // UNROLL))


def uses(slot, slots):
    return (UNITS - slot + slots - 1) // slots


def flat(ap):
    return ap.rearrange("p k d -> p (k d)")


def build(nc, x, src_cols, dst_cols, src_rows, dst_rows, ea_t, child_t, w1, b1, w2_t, b2, wu, bu,
          gamma, beta, wn_t, we_t, b, out):
    with ExitStack() as ctx:
        def sb(name, shape, dt=F32, scope=ctx):
            return scope.enter_context(nc.sbuf_tensor(name, shape, dt))

        def bank(name):
            return ctx.enter_context(nc.psum_tensor(name, [P, 512], F32))

        def sem(name):
            return ctx.enter_context(nc.semaphore(name))

        def sems(name, n):
            return [sem(f"{name}{k}") for k in range(n)]

        def table(name, rows, width, dt=F32):
            return nc.dram_tensor(name, (rows, width), dt, kind="Internal").ap()

        child_proj = table("child_proj", CROWS, PARTS * D, BF16)
        sum0, sum1 = table("sum0", ROWS, D), table("sum1", ROWS, D)
        y_part, x1 = table("y_part", NP, D), table("x1", NP, D)
        node_msg = table("node_msg", NP, TW)

        def group(t, r):
            return t[0:NP, :].rearrange("(g p k) d -> g p (k d)", p=P, k=G)[
                bass.ds(r, 1)].rearrange("a p f -> (a p) f")

        ident = sb("ident", [P, P])
        before = sb("before", [P, SQ[G]], BF16)
        iota_p = sb("iota_p", [P, P], F16)
        iota_t = sb("iota_t", [P, TILES], F16)
        spare_row = sb("spare_row", [P, G])
        eps_col = sb("eps_col", [P, 1])
        zeros = sb("zeros", [P, UNIT * D // P])
        ones = sb("ones", [EC, 1])
        hzero = sb("hzero", [P, 512], F16)
        w1_s, wc_s, wn_s, we_s = sb("w1_s", [P, D]), sb("wc_s", [P, D]), sb("wn_s", [P, D]), sb("we_s", [EC, D])
        b1_s = sb("b1_s", [P, 1])
        bu_g, b2u_g, gamma_g, beta_g, b_s = (sb(n, [P, w * D]) for n, w in (
            ("bu_g", G), ("b2u_g", G), ("gamma_g", G), ("beta_g", G), ("b_s", 1)))
        src_i, dst_i = sb("src_i", [P, TILES], I32), sb("dst_i", [P, TILES], I32)
        src_f, dst_f = sb("src_f", [P, TILES]), sb("dst_f", [P, TILES])
        to_spare = sb("to_spare", [P, TILES])
        key_p, key_t = sb("key_p", [P, TILES]), sb("key_t", [P, TILES])
        neg_has = sb("neg_has", [P, TILES])
        inv_cnt = sb("inv_cnt", [P, TILES])
        cnt = sb("cnt", [P, TILES])
        onehot_p = sb("onehot_p", [P, HT, P], F16)
        onehot_t = sb("onehot_t", [P, HT, TILES], F16)
        kept = sb("kept", [P, RES_SLOTS, G * D])

        ps_sum = [bank("ps_sum0"), bank("ps_sum1")]
        ps_e = [bank("ps_e0"), bank("ps_e1")]
        ps_a, ps_b, ps_c, ps_cnt = bank("ps_a"), bank("ps_b"), bank("ps_c"), bank("ps_cnt")

        def one_hots(dve, t0, n, first, ready, used):
            for t in range(n):
                if not first:
                    dve.wait_ge(used, t0 + t - HT + 1)
                col = bass.ds(t0 + t, 1)
                slot = t
                nc.vector.tensor_scalar(onehot_p[:, slot, :], iota_p[:, :], key_p[:, col], None,
                                        ALU.is_equal)
                nc.vector.tensor_scalar(onehot_t[:, slot, :], iota_t[:, :], key_t[:, col], None,
                                        ALU.is_equal).then_inc(ready, 1)

        def split_keys(dve, ints, halves, done):
            k0, k1 = halves[:, 0, :], halves[:, 1, :]
            nc.vector.tensor_scalar(k0, ints[:, :], 2, P - 1, ALU.logical_shift_right,
                                    ALU.bitwise_and).then_inc(done, 1)
            dve.wait_ge(done, 1)
            nc.vector.tensor_copy(key_p[:, :], k0).then_inc(done, 1)
            dve.wait_ge(done, 2)
            nc.vector.tensor_scalar(k0, ints[:, :], 9, 2, ALU.logical_shift_right,
                                    ALU.logical_shift_left).then_inc(done, 1)
            nc.vector.tensor_scalar(k1, ints[:, :], G - 1, None, ALU.bitwise_and).then_inc(done, 1)
            dve.wait_ge(done, 4)
            nc.vector.tensor_tensor(key_t[:, :], k0, k1, ALU.add).then_inc(done, 1)
            dve.wait_ge(done, 5)

        def spare_distance(dve, keys_f, done):
            for k in range(G):
                ins = nc.vector.tensor_scalar(to_spare[:, k::G], keys_f[:, k::G], -1.0,
                                              spare_row[:, k:k + 1], ALU.mult, ALU.add)
            ins.then_inc(done, 1)

        def open_counts():
            nc.tensor.matmul(ps_cnt[:, :], hzero[:, 0:P], hzero[:, :], start=True, stop=False,
                             skip_group_check=True)

        def close_counts(closed):
            nc.tensor.matmul(ps_cnt[:, :], hzero[:, 0:P], hzero[:, :], start=False, stop=True,
                             skip_group_check=True).then_inc(closed, 1)

        def add_counts(pe, t0, n, ready, used):
            for t in range(n):
                pe.wait_ge(ready, t0 + t + 1)
                nc.tensor.matmul(ps_cnt[:, 0:TILES], onehot_p[:, t, :], onehot_t[:, t, :],
                                 start=False, stop=False, skip_group_check=True).then_inc(used, 1)

        def norm_stats(dve, src, st, mv, u, bn_done, var_ready):
            dve.nop(nofuse=True)
            for k in range(G):
                ins = nc.vector.bn_stats(st[:, u.c, k, :], src[:, k * D:(k + 1) * D])
            ins.then_inc(bn_done, 1)
            dve.wait_ge(bn_done, u.r + 1)
            dve.nop(nofuse=True)
            for k in range(G):
                ins = nc.vector.bn_aggr(mv[:, u.c, k, :], st[:, u.c, k, :])
            ins.then_inc(var_ready, 1)

        def norm_root(act, mv, sd, u, var_ready, sd_ready):
            act.wait_ge(var_ready, u.r + 1)
            nc.scalar.activation(sd[:, u.c, :], mv[:, u.c, :, 1], ACT.Sqrt,
                                 bias=eps_col[:, 0:1]).then_inc(sd_ready, 1)

        def mark_repeats(dve, u, marks, junk, repeat, put, keys_f, rep_ready, put_half, put_ready):
            for k in range(G):
                ins = nc.vector.tensor_tensor_reduce(
                    out=junk[:, SQ[k]:SQ[k + 1]], in0=marks[:, u.c2, SQ[k]:SQ[k + 1]],
                    in1=before[:, SQ[k]:SQ[k + 1]], scale=1.0, scalar=0.0, op0=ALU.mult,
                    op1=ALU.add, accum_out=repeat[:, u.c, k:k + 1])
            ins.then_inc(rep_ready, 1)
            dve.wait_ge(rep_ready, u.r + 1)
            cols = bass.ds(u.r * G, G)
            nc.vector.scalar_tensor_tensor(out=repeat[:, u.c, :], in0=repeat[:, u.c, :], scalar=0.0,
                                           in1=to_spare[:, cols], op0=ALU.is_gt,
                                           op1=ALU.mult).then_inc(put_half, 1)
            dve.wait_ge(put_half, u.r + 1)
            nc.vector.tensor_tensor(put[:, u.c, :], repeat[:, u.c, :], keys_f[:, cols],
                                    ALU.add).then_inc(put_ready, 1)

        def sum_quad(pe, u, marks, rows, parts, sum_ready):
            for to in range(G):
                for b in range(to, G):
                    for part in range(parts):
                        ins = nc.tensor.matmul(
                            ps_sum[u.c2][:, to * D:(to + 1) * D],
                            marks[:, u.c2, SQ[b] + to * P:SQ[b] + (to + 1) * P],
                            rows[:, u.c, b, part * D:(part + 1) * D],
                            start=(b == to and part == 0), stop=(b == G - 1 and part == parts - 1))
            ins.then_inc(sum_ready, 1)

        def copy_sums(act, u, combined, added, sum_ready, comb_ready):
            if due(u.r - 1):
                act.wait_ge(added, (u.r - 1) * 16 * G)
            act.wait_ge(sum_ready, u.r + 1)
            nc.scalar.copy(combined[:, u.c2, :], ps_sum[u.c2][:, :]).then_inc(comb_ready, 1)

        def gather_quad(pool, u, rows, source, take, take_ready, rows_used, got):
            if due(u.r - 3):
                pool.wait_ge(rows_used, u.r - 3)
            pool.wait_ge(take_ready, u.r + 1)
            pool.nop(nofuse=True)
            for k in range(G):
                nc.gpsimd.indirect_dma_start(
                    rows[:, u.c, k, :], None, source[:, :],
                    bass.IndirectOffsetOnAxis(ap=take[:, u.c, k:k + 1], axis=0)).then_inc(got[u.c], 16)

        def scatter_quad(pool, u, combined, target, put, put_ready, comb_ready, added):
            if due(u.r):
                pool.wait_ge(added, u.r * 16 * G)
            pool.wait_ge(put_ready, u.r + 1)
            pool.wait_ge(comb_ready, u.r + 1)
            pool.nop(nofuse=True)
            for k in range(G):
                nc.gpsimd.indirect_dma_start(
                    target[:, :], bass.IndirectOffsetOnAxis(ap=put[:, u.c, k:k + 1], axis=0),
                    combined[:, u.c2, k * D:(k + 1) * D], None, compute_op=ALU.add).then_inc(added, 16)

        def load_keys(sp, u, keys, rows, eq_ready, keys_in):
            if due(u.r - 3):
                sp.wait_ge(eq_ready, u.r - 3)
            sp.dma_start(keys[:, u.c, :], rows[bass.ds(u.r, 1), :].rearrange(
                "a e -> (a e)").partition_broadcast(P)).then_inc(keys_in[u.c], 16)

        with ExitStack() as phase:
            ZR = 7
            zeros_big = sb("zeros_big", [P, ZR * UNIT * D // P], scope=phase)
            wu_s, w2t_s = sb("wu_s", [P, D], scope=phase), sb("w2t_s", [P, D], scope=phase)
            b2_s, b2_cols = sb("b2_s", [P, 1], scope=phase), sb("b2_cols", [P, P], scope=phase)
            halves = sb("halves", [P, 2, TILES], I32, scope=phase)
            child_in = sb("child_in", [P, CCHUNK * P], scope=phase)
            child_full = sb("child_full", [P, CCHUNK, D], scope=phase)
            child_rest = sb("child_rest", [P, CCHUNK, D], scope=phase)
            child_out = sb("child_out", [P, CCHUNK, PARTS, D], BF16, scope=phase)
            ld_w, ld_keys, ld_small, zero_set, sum_zeroed, pool_step, consts = (sem("set_" + n) for n in (
                "ld_w", "ld_keys", "ld_small", "zero_set", "sum_zeroed", "pool_step", "consts"))
            split_step, as_float, spare_done, b2_ready, wc_ready, wc_copied, max_done = (sem("set_" + n) for n in (
                "split_step", "as_float", "spare_done", "b2_ready", "wc_ready", "wc_copied", "max_done"))
            hot_ready, hot_used, cnt_closed, hzeroed = (sem("set_" + n) for n in (
                "hot_ready", "hot_used", "cnt_closed", "hzeroed"))
            child_ld, child_ready, child_copied, child_half, child_split, child_st = (sem("set_" + n) for n in (
                "child_ld", "child_ready", "child_copied", "child_half", "child_split", "child_st"))
            CHUNKS = CT // CCHUNK
            assert UNITS % ZR == 0
            block = phase.enter_context(nc.Block())

            def chunks(eng, chunk):
                chunk(0)
                with eng.Fori(1, CHUNKS) as c:
                    chunk(c)

            @block.sync
            def _(sp):
                for t, a in ((src_i, src_cols), (dst_i, dst_cols)):
                    sp.dma_start(t[:, :], a).then_inc(ld_keys, 16)
                for t, a in ((wu_s, wu), (w2t_s, w2_t), (w1_s, w1), (wn_s, wn_t), (we_s, we_t)):
                    sp.dma_start(t[:, :], a).then_inc(ld_w, 16)
                with nc.allow_non_contiguous_dma(reason="two columns of 128"):
                    for t, a in ((b1_s, b1), (b2_s, b2)):
                        sp.dma_start(t[:, :], a.rearrange("(p a) -> p a", a=1)).then_inc(ld_w, 16)
                for t, a in ((bu_g, bu), (gamma_g, gamma), (beta_g, beta)):
                    for k in range(G):
                        sp.dma_start(t[:, k * D:(k + 1) * D],
                                     a.partition_broadcast(P)).then_inc(ld_small, 16)
                sp.dma_start(b_s[:, :], b.partition_broadcast(P)).then_inc(ld_small, 16)

                def chunk(c):
                    if due(c):
                        sp.wait_ge(child_ready, c)
                    sp.dma_start(child_in[:, :], child_t[:, bass.ds(c * (CCHUNK * P), CCHUNK * P)]
                                 ).then_inc(child_ld, 16)
                    sp.wait_ge(child_split, c + 1)
                    sp.dma_start(child_proj[:, :].rearrange("(c t p) d -> c p t d", p=P, t=CCHUNK)[
                        bass.ds(c, 1)].rearrange("c p t d -> (c p) t d"),
                        child_out[:, :, :, :].rearrange("p t a d -> p t (a d)")).then_inc(child_st, 16)

                chunks(sp, chunk)
                sp.wait_ge(child_st, 16 * CHUNKS)
                sp.wait_ge(ld_small, 16 * (3 * G + 1))

            @block.gpsimd
            def _(pool):
                nc.gpsimd.memset(ident[:, :], 0.0)
                nc.gpsimd.memset(before[:, :], 1.0)
                nc.gpsimd.memset(eps_col[:, :], LN_EPS)
                nc.gpsimd.memset(zeros[:, :], 0.0)
                nc.gpsimd.memset(ones[:, :], 1.0).then_inc(pool_step, 1)
                pool.wait_ge(pool_step, 1)
                nc.gpsimd.affine_select(out=ident[:, :], in_=ident[:, :], compare_op=ALU.not_equal,
                                        fill=1.0, base=0, pattern=[[-1, P]], channel_multiplier=1)
                for k in range(G):
                    own = before[:, SQ[k + 1] - P:SQ[k + 1]]
                    nc.gpsimd.affine_select(out=own, in_=own, compare_op=ALU.is_gt, fill=0.0, base=0,
                                            pattern=[[-1, P]], channel_multiplier=1)
                nc.gpsimd.iota(iota_p[:, :], [[1, P]], base=0, channel_multiplier=0,
                               allow_small_or_imprecise_dtypes=True)
                nc.gpsimd.iota(iota_t[:, :], [[1, TILES]], base=0, channel_multiplier=0,
                               allow_small_or_imprecise_dtypes=True)
                nc.gpsimd.iota(spare_row[:, :], [[1, G]], base=NP, channel_multiplier=G,
                               allow_small_or_imprecise_dtypes=True).then_inc(consts, 1)

                def chunk(c):
                    pool.wait_ge(child_copied, c + 1)
                    if due(c):
                        pool.wait_ge(child_st, c * 16)
                    pool.nop(nofuse=True)
                    nc.gpsimd.tensor_copy(child_out[:, :, 0, :], child_full[:, :, :]).then_inc(child_half, 1)
                    for part in range(1, PARTS):
                        pool.wait_ge(child_half, c * 4 + part * 2 - 1)
                        rest = child_full if part == 1 else child_rest
                        nc.gpsimd.tensor_tensor(child_rest[:, :, :], rest[:, :, :],
                                                child_out[:, :, part - 1, :],
                                                ALU.subtract).then_inc(child_half, 1)
                        pool.wait_ge(child_half, c * 4 + part * 2)
                        pool.nop(nofuse=True)
                        ins = nc.gpsimd.tensor_copy(child_out[:, :, part, :], child_rest[:, :, :])
                        ins.then_inc(child_half if part < PARTS - 1 else child_split, 1)

                chunks(pool, chunk)

            @block.vector
            def _(dve):
                nc.vector.memset(hzero[:, :], 0.0).then_inc(hzeroed, 1)
                nc.vector.memset(zeros_big[:, :], 0.0).then_inc(zero_set, 1)
                dve.wait_ge(ld_keys, 32)
                split_keys(dve, src_i, halves, split_step)
                nc.vector.tensor_copy(src_f[:, :], src_i[:, :])
                nc.vector.tensor_copy(dst_f[:, :], dst_i[:, :]).then_inc(as_float, 1)
                dve.wait_ge(as_float, 1)
                dve.wait_ge(consts, 1)
                spare_distance(dve, src_f, spare_done)
                dve.wait_ge(ld_w, 16 * 7)
                nc.vector.tensor_scalar(b2_cols[:, :], ident[:, :], 0.0, b2_s[:, 0:1], ALU.mult,
                                        ALU.add).then_inc(b2_ready, 1)
                dve.wait_ge(wc_ready, 1)
                nc.vector.tensor_copy(wc_s[:, :], ps_a[:, 0:D])
                nc.vector.tensor_copy(b2u_g[:, :], ps_b[:, :]).then_inc(wc_copied, 1)
                one_hots(dve, 0, HT, True, hot_ready, hot_used)
                with dve.Fori(1, TILES // HT) as i:
                    one_hots(dve, i * HT, HT, False, hot_ready, hot_used)
                dve.wait_ge(cnt_closed, 1)
                nc.vector.tensor_scalar(neg_has[:, :], ps_cnt[:, 0:TILES], 1.0, -1.0, ALU.min,
                                        ALU.mult)
                nc.vector.tensor_scalar(cnt[:, :], ps_cnt[:, 0:TILES], 1.0, None,
                                        ALU.max).then_inc(max_done, 1)
                dve.wait_ge(max_done, 1)
                nc.vector.reciprocal(inv_cnt[:, :], cnt[:, :])

            @block.tensor
            def _(pe):
                pe.wait_ge(hzeroed, 1)
                open_counts()
                pe.wait_ge(ld_w, 16 * 7)
                nc.tensor.matmul(ps_a[:, 0:D], w2t_s[:, :], wu_s[:, :], start=True, stop=True)
                pe.wait_ge(b2_ready, 1)
                for k in range(G):
                    ins = nc.tensor.matmul(ps_b[:, k * D:(k + 1) * D], b2_cols[:, :], wu_s[:, :],
                                           start=True, stop=True)
                ins.then_inc(wc_ready, 1)

                def chunk(c):
                    if due(c):
                        pe.wait_ge(child_copied, c)
                    pe.wait_ge(child_ld, c * 16 + 16)
                    for t in range(CCHUNK):
                        ins = nc.tensor.matmul(ps_e[t // G][:, (t % G) * D:(t % G + 1) * D],
                                               child_in[:, t * P:(t + 1) * P], wu_s[:, :],
                                               start=True, stop=True)
                    ins.then_inc(child_ready, 1)
                    for s in range(TILES // HT // CHUNKS):
                        add_counts(pe, (c * (TILES // HT // CHUNKS) + s) * HT, HT, hot_ready, hot_used)

                assert TILES // HT % CHUNKS == 0
                chunks(pe, chunk)
                close_counts(cnt_closed)

            @block.scalar
            def _(act):
                act.wait_ge(zero_set, 1)
                for z in range(UNITS // ZR):
                    act.dma_start(sum0[z * ZR * UNIT:(z + 1) * ZR * UNIT, :].rearrange(
                        "(p r) d -> p (r d)", p=P), zeros_big[:, :]).then_inc(sum_zeroed, 16)
                for s in (sum0, sum1):
                    act.dma_start(s[NP:ROWS, :].rearrange("(p r) d -> p (r d)", p=P),
                                  zeros_big[:, 0:G * D]).then_inc(sum_zeroed, 16)

                def chunk(c):
                    act.wait_ge(child_ready, c + 1)
                    if due(c):
                        act.wait_ge(child_split, c)
                    nc.scalar.copy(flat(child_full[:, 0:G, :]), ps_e[0][:, :])
                    nc.scalar.copy(flat(child_full[:, G:CCHUNK, :]),
                                   ps_e[1][:, 0:(CCHUNK - G) * D]).then_inc(child_copied, 1)

                chunks(act, chunk)
                act.wait_ge(sum_zeroed, 16 * (UNITS // ZR + 2))

        with ExitStack() as phase:
            def pb(name, shape, dt=F32):
                return sb("l0_" + name, shape, dt, phase)

            keys = pb("keys", [P, 4, UNIT], I32)
            take, put = pb("take", [P, 4, G], I32), pb("put", [P, 4, G], I32)
            taken = pb("taken", [P, 4, G, PARTS * D], BF16)
            marks, junk = pb("marks", [P, 2, SQ[G]], BF16), pb("junk", [P, SQ[G]], BF16)
            repeat = pb("repeat", [P, 4, G])
            combined = pb("combined", [P, 2, UNIT])
            x_s = pb("x_s", [P, 4, G * D])
            stats, mean_var = pb("stats", [P, 4, G, 6]), pb("mean_var", [P, 4, G, 2])
            root, rstd, shift = pb("root", [P, 4, G]), pb("rstd", [P, 4, G]), pb("shift", [P, 4, G])
            h_s = pb("h_s", [P, 4, G * D])
            ht_s, act_s = pb("ht_s", [P, UNIT]), pb("act_s", [P, UNIT])
            w_s = pb("w_s", [P, 2, G * D])
            y_s = pb("y_s", [P, UNROLL - RES, G * D])

            keys_in, x_in, y_out = sems("l0_keys_in", 4), sems("l0_x_in", 4), sems("l0_y_out", UNROLL - RES)
            got, added, zeroed = sems("l0_got", 4), sem("l0_added"), sem("l0_zeroed")
            take_ready, eq_ready, rep_ready, put_half, put_ready, sum_ready, comb_ready = (
                sem("l0_" + n) for n in ("take_ready", "eq_ready", "rep_ready", "put_half",
                                         "put_ready", "sum_ready", "comb_ready"))
            (bn_done, var_ready, sd_ready, rs_ready, terms_ready, h_ready, tr_ready, ht_ready,
             hid_ready, act_ready, proj_ready, proj_read, y_ready) = (
                sem("l0_" + n) for n in ("bn_done", "var_ready", "sd_ready", "rs_ready", "terms_ready",
                                         "h_ready", "tr_ready", "ht_ready", "hid_ready", "act_ready",
                                         "proj_ready", "proj_read", "y_ready"))
            proj_bank = [ps_c, ps_e[0]]
            block = phase.enter_context(nc.Block())

            @block.sync
            def _(sp):
                def step(at):
                    if u := at.ahead(4):
                        if due(u.r - 3):
                            sp.wait_ge(h_ready, u.r - 3)
                        sp.dma_start(x_s[:, u.c, :], group(x, u.r)).then_inc(x_in[u.c], 16)
                    if u := at.ahead(4):
                        load_keys(sp, u, keys, src_rows, eq_ready, keys_in)
                    if u := at.ahead(0):
                        sp.dma_start(sum1[bass.ds(u.r * UNIT, UNIT), :].rearrange(
                            "(p r) d -> p (r d)", p=P), zeros[:, :]).then_inc(zeroed, 16)
                        if not u.stays:
                            sp.wait_ge(y_ready, u.r + 1)
                            sp.dma_start(group(y_part, u.r), y_s[:, u.d, :]).then_inc(y_out[u.d], 16)

                run_units(sp, step, 4)
                sp.wait_ge(zeroed, 16 * UNITS)
                for d in range(UNROLL - RES):
                    sp.wait_ge(y_out[d], 16 * uses(RES + d, UNROLL))

            @block.gpsimd
            def _(pool):
                def step(at):
                    if u := at.ahead(1):
                        gather_quad(pool, u, taken, child_proj, take, take_ready, sum_ready, got)
                    if u := at.ahead(0):
                        scatter_quad(pool, u, combined, sum0, put, put_ready, comb_ready, added)

                run_units(pool, step, 1)
                pool.wait_ge(added, 16 * G * UNITS)

            @block.vector
            def _(dve):
                def rows_to_take(u):
                    if due(u.n):
                        dve.wait_ge(got[u.c], u.n * 16 * G)
                    nc.vector.tensor_scalar(take[:, u.c, :], dst_i[:, bass.ds(u.r * G, G)],
                                            NCHILD - 1, None, ALU.min).then_inc(take_ready, 1)

                def compare(u):
                    if due(u.r - 1):
                        dve.wait_ge(sum_ready, u.r - 1)
                    if due(u.r - 3):
                        dve.wait_ge(added, (u.r - 3) * 16 * G)
                    dve.wait_ge(keys_in[u.c], u.n * 16 + 16)
                    for k in range(G):
                        ins = nc.vector.tensor_scalar(marks[:, u.c2, SQ[k]:SQ[k + 1]],
                                                      keys[:, u.c, 0:(k + 1) * P],
                                                      src_f[:, bass.ds(u.r * G + k, 1)], None,
                                                      ALU.is_equal)
                    ins.then_inc(eq_ready, 1)
                    dve.wait_ge(eq_ready, u.r + 1)
                    mark_repeats(dve, u, marks, junk, repeat, put, src_f, rep_ready, put_half, put_ready)

                def norm_terms(u):
                    if due(u.r - 3):
                        dve.wait_ge(h_ready, u.r - 3)
                    dve.wait_ge(sd_ready, u.r + 1)
                    nc.vector.reciprocal(rstd[:, u.c, :], root[:, u.c, :]).then_inc(rs_ready, 1)
                    dve.wait_ge(rs_ready, u.r + 1)
                    nc.vector.scalar_tensor_tensor(
                        out=shift[:, u.c, :], in0=mean_var[:, u.c, :, 0], scalar=-1.0,
                        in1=rstd[:, u.c, :], op0=ALU.mult, op1=ALU.mult).then_inc(terms_ready, 1)

                def finish(u):
                    y = kept[:, bass.ds(u.place, 1), :].rearrange("p a f -> p (a f)") if u.stays else y_s[:, u.d, :]
                    if not u.stays and due(u.n):
                        dve.wait_ge(y_out[u.d], u.n * 16)
                    dve.wait_ge(proj_ready, u.r + 1)
                    nc.vector.tensor_tensor(w_s[:, u.c2, :], proj_bank[u.c2][:, :], b2u_g[:, :],
                                            ALU.add).then_inc(proj_read, 1)
                    nc.vector.tensor_tensor(y, h_s[:, u.c, :], bu_g[:, :], ALU.add).then_inc(proj_read, 1)
                    dve.wait_ge(proj_read, u.r * 2 + 2)
                    for k in range(G):
                        cols = slice(k * D, (k + 1) * D)
                        ins = nc.vector.scalar_tensor_tensor(
                            out=y[:, cols], in0=w_s[:, u.c2, cols],
                            scalar=neg_has[:, bass.ds(u.r * G + k, 1)], in1=y[:, cols],
                            op0=ALU.mult, op1=ALU.add)
                    ins.then_inc(y_ready, 1)

                def step(at):
                    if u := at.ahead(3):
                        rows_to_take(u)
                    if u := at.ahead(1):
                        compare(u)
                    if u := at.ahead(2):
                        norm_terms(u)
                    if u := at.ahead(3):
                        dve.wait_ge(x_in[u.c], u.n * 16 + 16)
                        norm_stats(dve, x_s[:, u.c, :], stats, mean_var, u, bn_done, var_ready)
                    if u := at.ahead(0):
                        finish(u)

                run_units(dve, step, 3)

            @block.tensor
            def _(pe):
                def step(at):
                    if u := at.ahead(1):
                        pe.wait_ge(h_ready, u.r + 1)
                        for k in range(G):
                            ins = nc.tensor.transpose(ps_a[:, k * P:(k + 1) * P],
                                                      h_s[:, u.c, k * D:(k + 1) * D], ident[:, :])
                        ins.then_inc(tr_ready, 1)
                    if u := at.ahead(0):
                        if due(u.r - 1):
                            pe.wait_ge(comb_ready, u.r - 1)
                        pe.wait_ge(eq_ready, u.r + 1)
                        pe.wait_ge(got[u.c], (u.n + 1) * 16 * G)
                        sum_quad(pe, u, marks, taken, PARTS, sum_ready)
                    if u := at.ahead(1):
                        pe.wait_ge(ht_ready, u.r + 1)
                        nc.tensor.matmul(ps_b[:, :], w1_s[:, :], ht_s[:, :], start=True,
                                         stop=True).then_inc(hid_ready, 1)
                        if due(u.r - 1):
                            pe.wait_ge(proj_read, (u.r - 1) * 2)
                        pe.wait_ge(act_ready, u.r + 1)
                        for k in range(G):
                            ins = nc.tensor.matmul(proj_bank[u.c2][:, k * D:(k + 1) * D],
                                                   act_s[:, k * P:(k + 1) * P], wc_s[:, :],
                                                   start=True, stop=True)
                        ins.then_inc(proj_ready, 1)

                run_units(pe, step, 1)

            @block.scalar
            def _(act):
                def step(at):
                    if u := at.ahead(2):
                        if due(u.r - 3):
                            act.wait_ge(y_ready, u.r - 3)
                        act.wait_ge(terms_ready, u.r + 1)
                        act.wait_ge(x_in[u.c], u.n * 16 + 16)
                        for k in range(G):
                            cols = slice(k * D, (k + 1) * D)
                            ins = nc.scalar.activation(h_s[:, u.c, cols], x_s[:, u.c, cols], ACT.Relu,
                                                       bias=shift[:, u.c, k:k + 1],
                                                       scale=rstd[:, u.c, k:k + 1])
                        ins.then_inc(h_ready, 1)
                    if u := at.ahead(3):
                        norm_root(act, mean_var, root, u, var_ready, sd_ready)
                    if u := at.ahead(1):
                        act.wait_ge(tr_ready, u.r + 1)
                        nc.scalar.copy(ht_s[:, :], ps_a[:, :]).then_inc(ht_ready, 1)
                    if u := at.ahead(0):
                        copy_sums(act, u, combined, added, sum_ready, comb_ready)
                    if u := at.ahead(1):
                        if due(u.r):
                            act.wait_ge(proj_ready, u.r)
                        act.wait_ge(hid_ready, u.r + 1)
                        nc.scalar.activation(act_s[:, :], ps_b[:, :], ACT.Relu,
                                             bias=b1_s[:, 0:1]).then_inc(act_ready, 1)

                run_units(act, step, 3)

        with ExitStack() as phase:
            def pb(name, shape, dt=F32):
                return sb("up_" + name, shape, dt, phase)

            x_s, s_s = pb("x_s", [P, 4, G * D]), pb("s_s", [P, 4, G * D])
            y_s, x1_s = pb("y_s", [P, UNROLL - RES, G * D]), pb("x1_s", [P, UNROLL - RES, G * D])
            z_s = pb("z_s", [P, 2, G * D])
            stats, mean_var = pb("stats", [P, 4, G, 6]), pb("mean_var", [P, 4, G, 2])
            root, rstd = pb("root", [P, 4, G]), pb("rstd", [P, 4, G])
            stats2, mean_var2 = pb("stats2", [P, 4, G, 6]), pb("mean_var2", [P, 4, G, 2])
            root2, rstd2 = pb("root2", [P, 4, G]), pb("rstd2", [P, 4, G])
            h_s, ht_s = pb("h_s", [P, 2, G * D]), pb("ht_s", [P, 2, UNIT])
            msg_s = pb("msg_s", [P, 4, G, TW])
            sq_junk = pb("sq_junk", [P, 2, G * D])

            x_in, y_in, s_in, x1_out, m_out = (sems("up_" + n, 4) for n in
                                               ("x_in", "y_in", "s_in", "x1_out", "m_out"))
            (y_step, z_ready, xb_ready, zg_ready, x1_ready, h_ready, nh_ready, tr_ready, ht_ready,
             proj_ready, m_ready) = (
                sem("up_" + n) for n in ("y_step", "z_ready", "xb_ready", "zg_ready", "x1_ready",
                                         "h_ready", "nh_ready", "tr_ready", "ht_ready", "proj_ready",
                                         "m_ready"))
            bn_done, var_ready, sd_ready, rs_ready = (sem("up_" + n) for n in (
                "bn_done", "var_ready", "sd_ready", "rs_ready"))
            bn2_done, var2_ready, sd2_ready, rs2_ready = (sem("up_" + n) for n in (
                "bn2_done", "var2_ready", "sd2_ready", "rs2_ready"))
            tr_bank, proj_bank = [ps_a, ps_b], [ps_c, ps_e[0]]

            def y_of(u):
                return kept[:, bass.ds(u.place, 1), :].rearrange("p a f -> p (a f)") if u.stays else y_s[:, u.d, :]

            def x1_of(u):
                return kept[:, bass.ds(u.place, 1), :].rearrange("p a f -> p (a f)") if u.stays else x1_s[:, u.d, :]

            block = phase.enter_context(nc.Block())

            @block.sync
            def _(sp):
                def step(at):
                    if u := at.ahead(3):
                        if due(u.r - 3):
                            sp.wait_ge(x1_ready, u.r - 3)
                        sp.dma_start(s_s[:, u.c, :], group(sum0, u.r)).then_inc(s_in[u.c], 16)
                        if not u.stays:
                            sp.dma_start(y_s[:, u.d, :], group(y_part, u.r)).then_inc(y_in[u.d], 16)
                        sp.dma_start(x_s[:, u.c, :], group(x, u.r)).then_inc(x_in[u.c], 16)
                    if u := at.ahead(0):
                        if not u.stays:
                            sp.wait_ge(x1_ready, u.r + 1)
                            sp.dma_start(group(x1, u.r), x1_s[:, u.d, :]).then_inc(x1_out[u.d], 16)

                run_units(sp, step, 3)
                for d in range(UNROLL - RES):
                    sp.wait_ge(x1_out[d], 16 * uses(RES + d, UNROLL))

            @block.gpsimd
            def _(pool):
                def step(at):
                    if u := at.ahead(1):
                        pool.wait_ge(x_in[u.c], u.n * 16 + 16)
                        nc.gpsimd.tensor_tensor(x_s[:, u.c, :], x_s[:, u.c, :], beta_g[:, :],
                                                ALU.add).then_inc(xb_ready, 1)
                    if u := at.ahead(0):
                        pool.wait_ge(z_ready, u.r + 1)
                        nc.gpsimd.tensor_tensor(z_s[:, u.c2, :], z_s[:, u.c2, :], gamma_g[:, :],
                                                ALU.mult).then_inc(zg_ready, 1)
                        if not u.stays and due(u.n):
                            pool.wait_ge(x1_out[u.d], u.n * 16)
                            pool.wait_ge(h_ready, u.r - 3)
                        pool.wait_ge(xb_ready, u.r + 1)
                        pool.wait_ge(zg_ready, u.r + 1)
                        pool.nop(nofuse=True)
                        nc.gpsimd.tensor_tensor(x1_of(u), z_s[:, u.c2, :], x_s[:, u.c, :],
                                                ALU.add).then_inc(x1_ready, 1)

                run_units(pool, step, 1)

            @block.vector
            def _(dve):
                def y_terms(u):
                    y = y_of(u)
                    if not u.stays:
                        dve.wait_ge(y_in[u.d], u.n * 16 + 16)
                    dve.wait_ge(s_in[u.c], u.n * 16 + 16)
                    for k in range(G):
                        cols = slice(k * D, (k + 1) * D)
                        ins = nc.vector.scalar_tensor_tensor(
                            out=y[:, cols], in0=s_s[:, u.c, cols],
                            scalar=inv_cnt[:, bass.ds(u.r * G + k, 1)], in1=y[:, cols],
                            op0=ALU.mult, op1=ALU.add)
                    ins.then_inc(y_step, 1)
                    dve.wait_ge(y_step, u.r + 1)
                    norm_stats(dve, y, stats, mean_var, u, bn_done, var_ready)

                def z_terms(u):
                    y = y_of(u)
                    dve.wait_ge(sd_ready, u.r + 1)
                    nc.vector.reciprocal(rstd[:, u.c, :], root[:, u.c, :]).then_inc(rs_ready, 1)
                    if due(u.r - 1):
                        dve.wait_ge(x1_ready, u.r - 1)
                    dve.wait_ge(rs_ready, u.r + 1)
                    for k in range(G):
                        cols = slice(k * D, (k + 1) * D)
                        ins = nc.vector.tensor_scalar(z_s[:, u.c2, cols], y[:, cols],
                                                      mean_var[:, u.c, k, 0:1], rstd[:, u.c, k:k + 1],
                                                      ALU.subtract, ALU.mult)
                    ins.then_inc(z_ready, 1)

                def h_terms(u):
                    xo = x1_of(u)
                    if due(u.r - 1):
                        dve.wait_ge(tr_ready, u.r - 1)
                        dve.wait_ge(nh_ready, u.r - 1)
                    dve.wait_ge(sd2_ready, u.r + 1)
                    if due(u.r - 3):
                        dve.wait_ge(m_ready, u.r - 3)
                    nc.vector.reciprocal(rstd2[:, u.c, :], root2[:, u.c, :]).then_inc(rs2_ready, 1)
                    for k in range(G):
                        cols = slice(k * D, (k + 1) * D)
                        ins = nc.vector.tensor_scalar(h_s[:, u.c2, cols], xo[:, cols],
                                                      mean_var2[:, u.c, k, 0:1], 0.0,
                                                      ALU.subtract, ALU.max)
                    ins.then_inc(h_ready, 1)

                def step(at):
                    if u := at.ahead(2):
                        z_terms(u)
                    if u := at.ahead(3):
                        y_terms(u)
                    if u := at.ahead(0):
                        h_terms(u)
                    if u := at.ahead(1):
                        dve.wait_ge(x1_ready, u.r + 1)
                        norm_stats(dve, x1_of(u), stats2, mean_var2, u, bn2_done, var2_ready)

                run_units(dve, step, 3)

            @block.tensor
            def _(pe):
                def step(at):
                    if u := at.ahead(1):
                        if due(u.r - 1):
                            pe.wait_ge(ht_ready, u.r - 1)
                        pe.wait_ge(h_ready, u.r + 1)
                        for k in range(G):
                            ins = nc.tensor.transpose(tr_bank[u.c2][:, k * P:(k + 1) * P],
                                                      h_s[:, u.c2, k * D:(k + 1) * D], ident[:, :])
                        ins.then_inc(tr_ready, 1)
                    if u := at.ahead(0):
                        if due(u.r - 1):
                            pe.wait_ge(m_ready, u.r - 1)
                        pe.wait_ge(ht_ready, u.r + 1)
                        for k in range(G):
                            ins = nc.tensor.matmul(proj_bank[u.c2][:, k * D:(k + 1) * D],
                                                   ht_s[:, u.c2, k * P:(k + 1) * P], wn_s[:, :],
                                                   start=True, stop=True)
                        ins.then_inc(proj_ready, 1)

                run_units(pe, step, 1)

            @block.scalar
            def _(act):
                def square_norms(u):
                    if due(u.n):
                        act.wait_ge(m_out[u.c], u.n * 16)
                    if due(u.r - 1):
                        act.wait_ge(nh_ready, u.r - 1)
                    act.wait_ge(rs2_ready, u.r + 1)
                    act.wait_ge(h_ready, u.r + 1)
                    for k in range(G):
                        cols = slice(k * D, (k + 1) * D)
                        ins = nc.scalar.activation(sq_junk[:, u.c2, cols], h_s[:, u.c2, cols],
                                                   ACT.Square, scale=rstd2[:, u.c, k:k + 1],
                                                   accum_out=msg_s[:, u.c, k, D:TW])
                    ins.then_inc(nh_ready, 1)

                def messages(u):
                    act.wait_ge(proj_ready, u.r + 1)
                    for k in range(G):
                        ins = nc.scalar.activation(msg_s[:, u.c, k, 0:D],
                                                   proj_bank[u.c2][:, k * D:(k + 1) * D],
                                                   ACT.Copy, scale=rstd2[:, u.c, k:k + 1])
                    ins.then_inc(m_ready, 1)
                    act.wait_ge(m_ready, u.r + 1)
                    act.wait_ge(nh_ready, u.r + 1)
                    act.dma_start(group(node_msg, u.r), flat(msg_s[:, u.c, :, :])).then_inc(m_out[u.c], 16)

                def step(at):
                    if u := at.ahead(4):
                        norm_root(act, mean_var, root, u, var_ready, sd_ready)
                    if u := at.ahead(2):
                        norm_root(act, mean_var2, root2, u, var2_ready, sd2_ready)
                    if u := at.ahead(1):
                        if due(u.r - 1):
                            act.wait_ge(proj_ready, u.r - 1)
                        act.wait_ge(tr_ready, u.r + 1)
                        nc.scalar.copy(ht_s[:, u.c2, :], tr_bank[u.c2][:, :]).then_inc(ht_ready, 1)
                    if u := at.ahead(1):
                        square_norms(u)
                    if u := at.ahead(0):
                        messages(u)

                run_units(act, step, 4)
                for c in range(4):
                    act.wait_ge(m_out[c], 16 * uses(c, 4))

        with ExitStack() as phase:
            def pb(name, shape, dt=F32):
                return sb("l1_" + name, shape, dt, phase)

            keys = pb("keys", [P, 4, UNIT], I32)
            halves = pb("halves", [P, 2, TILES], I32)
            take, put = pb("take", [P, 4, G], I32), pb("put", [P, 4, G], I32)
            taken = pb("taken", [P, 4, G, TW])
            marks, junk = pb("marks", [P, 2, SQ[G]]), pb("junk", [P, SQ[G]], BF16)
            repeat = pb("repeat", [P, 4, G])
            combined = pb("combined", [P, 2, UNIT])
            ea_s, ea_sq = pb("ea_s", [EC, 4, UNIT]), pb("ea_sq", [EC, 2, UNIT])
            norm2, norm, inv_norm = pb("norm2", [P, 4, G]), pb("norm", [P, 4, G]), pb("inv_norm", [P, 4, G])
            msg = pb("msg", [P, 4, G, D])

            keys_in, ea_in, got, added = sems("l1_keys_in", 4), sems("l1_ea_in", 4), sems("l1_got", 4), sem("l1_added")
            (take_ready, eq_ready, rep_ready, put_half, put_ready, sum_ready, comb_ready, sq_ready,
             edge_ready, n2_added, n2_ready, n2_root, inv_ready, m_ready, hot_ready, hot_used,
             split_step, spare_done, max_done, cnt_closed) = (
                sem("l1_" + n) for n in (
                    "take_ready", "eq_ready", "rep_ready", "put_half", "put_ready", "sum_ready",
                    "comb_ready", "sq_ready", "edge_ready", "n2_added", "n2_ready", "n2_root",
                    "inv_ready", "m_ready", "hot_ready", "hot_used", "split_step", "spare_done",
                    "max_done", "cnt_closed"))
            ps_n = [ps_a, ps_b]
            block = phase.enter_context(nc.Block())

            @block.sync
            def _(sp):
                def step(at):
                    if u := at.ahead(0):
                        if due(u.r - 3):
                            sp.wait_ge(edge_ready, u.r - 3)
                        sp.dma_start(ea_s[:, u.c, :], ea_t[:, bass.ds(u.r * UNIT, UNIT)]).then_inc(ea_in[u.c], 16)
                        load_keys(sp, u, keys, dst_rows, eq_ready, keys_in)

                run_units(sp, step, 0)

            @block.gpsimd
            def _(pool):
                def step(at):
                    if u := at.ahead(3):
                        gather_quad(pool, u, taken, node_msg, take, take_ready, m_ready, got)
                    if u := at.ahead(0):
                        scatter_quad(pool, u, combined, sum1, put, put_ready, comb_ready, added)

                run_units(pool, step, 3)
                pool.wait_ge(added, 16 * G * UNITS)

            @block.vector
            def _(dve):
                def rows_to_take(u):
                    if due(u.n):
                        dve.wait_ge(got[u.c], u.n * 16 * G)
                    nc.vector.tensor_scalar(take[:, u.c, :], src_i[:, bass.ds(u.r * G, G)],
                                            0, None, ALU.max).then_inc(take_ready, 1)

                def messages(u):
                    if due(u.r - 3):
                        dve.wait_ge(sum_ready, u.r - 3)
                    dve.wait_ge(edge_ready, u.r + 1)
                    dve.wait_ge(got[u.c], (u.n + 1) * 16 * G)
                    nc.vector.tensor_tensor(norm2[:, u.c, :], ps_n[u.c2][:, 0:G],
                                            taken[:, u.c, :, D], ALU.add).then_inc(n2_added, 1)
                    nc.vector.tensor_tensor(msg[:, u.c, :, :], ps_e[u.c2][:, :].rearrange(
                        "p (k d) -> p k d", k=G), taken[:, u.c, :, 0:D], ALU.add).then_inc(m_ready, 1)
                    dve.wait_ge(n2_added, u.r + 1)
                    nc.vector.tensor_scalar(norm2[:, u.c, :], norm2[:, u.c, :], L2_EPS * L2_EPS, None,
                                            ALU.max).then_inc(n2_ready, 1)

                def compare(u):
                    dve.wait_ge(n2_root, u.r + 1)
                    nc.vector.reciprocal(inv_norm[:, u.c, :], norm[:, u.c, :]).then_inc(inv_ready, 1)
                    if due(u.r - 1):
                        dve.wait_ge(sum_ready, u.r - 1)
                    if due(u.r - 3):
                        dve.wait_ge(added, (u.r - 3) * 16 * G)
                    dve.wait_ge(keys_in[u.c], u.n * 16 + 16)
                    dve.wait_ge(inv_ready, u.r + 1)
                    for k in range(G):
                        ins = nc.vector.tensor_scalar(marks[:, u.c2, SQ[k]:SQ[k + 1]],
                                                      keys[:, u.c, 0:(k + 1) * P],
                                                      dst_f[:, bass.ds(u.r * G + k, 1)],
                                                      inv_norm[:, u.c, k:k + 1],
                                                      ALU.is_equal, ALU.mult)
                    ins.then_inc(eq_ready, 1)
                    dve.wait_ge(eq_ready, u.r + 1)
                    mark_repeats(dve, u, marks, junk, repeat, put, dst_f, rep_ready, put_half, put_ready)

                def counts(u):
                    for t in range(G):
                        if due(u.r - 1):
                            dve.wait_ge(hot_used, (u.r - 2) * G + t + 1)
                        col = bass.ds(u.r * G + t, 1)
                        nc.vector.tensor_scalar(onehot_p[:, u.c2 * G + t, :], iota_p[:, :],
                                                key_p[:, col], None, ALU.is_equal)
                        nc.vector.tensor_scalar(onehot_t[:, u.c2 * G + t, :], iota_t[:, :],
                                                key_t[:, col], None, ALU.is_equal).then_inc(hot_ready, 1)

                def step(at):
                    if u := at.ahead(4):
                        rows_to_take(u)
                    if u := at.ahead(1):
                        compare(u)
                    if u := at.ahead(2):
                        messages(u)
                    if u := at.ahead(0):
                        counts(u)

                split_keys(dve, dst_i, halves, split_step)
                spare_distance(dve, dst_f, spare_done)
                dve.wait_ge(spare_done, 1)
                run_units(dve, step, 4)
                dve.wait_ge(cnt_closed, 1)
                nc.vector.tensor_scalar(cnt[:, :], ps_cnt[:, 0:TILES], 1.0, None,
                                        ALU.max).then_inc(max_done, 1)
                dve.wait_ge(max_done, 1)
                nc.vector.reciprocal(inv_cnt[:, :], cnt[:, :])

            @block.tensor
            def _(pe):
                def edge_parts(u):
                    if due(u.r - 1):
                        pe.wait_ge(m_ready, u.r - 1)
                        pe.wait_ge(n2_added, u.r - 1)
                    pe.wait_ge(ea_in[u.c], u.n * 16 + 16)
                    for k in range(G):
                        nc.tensor.matmul(ps_e[u.c2][:, k * D:(k + 1) * D],
                                         ea_s[:, u.c, k * P:(k + 1) * P], we_s[:, :],
                                         start=True, stop=True)
                    pe.wait_ge(sq_ready, u.r + 1)
                    for k in range(G):
                        ins = nc.tensor.matmul(ps_n[u.c2][:, k:k + 1], ea_sq[:, u.c2, k * P:(k + 1) * P],
                                               ones[:, :], start=True, stop=True)
                    ins.then_inc(edge_ready, 1)

                def step(at):
                    if u := at.ahead(0):
                        if due(u.r - 1):
                            pe.wait_ge(comb_ready, u.r - 1)
                        pe.wait_ge(eq_ready, u.r + 1)
                        pe.wait_ge(m_ready, u.r + 1)
                        sum_quad(pe, u, marks, msg, 1, sum_ready)
                    if u := at.ahead(2):
                        edge_parts(u)
                    if u := at.ahead(0):
                        for t in range(G):
                            pe.wait_ge(hot_ready, u.r * G + t + 1)
                            nc.tensor.matmul(ps_cnt[:, 0:TILES], onehot_p[:, u.c2 * G + t, :],
                                             onehot_t[:, u.c2 * G + t, :], start=False, stop=False,
                                             skip_group_check=True).then_inc(hot_used, 1)

                open_counts()
                run_units(pe, step, 2)
                close_counts(cnt_closed)

            @block.scalar
            def _(act):
                def step(at):
                    if u := at.ahead(3):
                        if due(u.r - 1):
                            act.wait_ge(edge_ready, u.r - 1)
                        act.wait_ge(ea_in[u.c], u.n * 16 + 16)
                        nc.scalar.activation(ea_sq[:, u.c2, :], ea_s[:, u.c, :],
                                             ACT.Square).then_inc(sq_ready, 1)
                    if u := at.ahead(0):
                        copy_sums(act, u, combined, added, sum_ready, comb_ready)
                    if u := at.ahead(2):
                        act.wait_ge(n2_ready, u.r + 1)
                        nc.scalar.activation(norm[:, u.c, :], norm2[:, u.c, :],
                                             ACT.Sqrt).then_inc(n2_root, 1)

                run_units(act, step, 3)

        with ExitStack() as phase:
            def pb(name, shape, dt=F32):
                return sb("out_" + name, shape, dt, phase)

            s_s, o_s = pb("s_s", [P, 4, G * D]), pb("o_s", [P, 4, G * D])
            x1_s = pb("x1_s", [P, UNROLL - RES, G * D])
            res_s = pb("res_s", [P, 4, G * D])
            sq_junk = pb("sq_junk", [P, 2, G * D])
            norm2, inv_norm = pb("norm2", [P, 4, G]), pb("inv_norm", [P, 4, G])
            x1_in, s_in, res_out = (sems("out_" + n, 4) for n in ("x1_in", "s_in", "res_out"))
            o_ready, n_ready, max_ready, rn_ready, root_ready, res_ready = (
                sem("out_" + n) for n in ("o_ready", "n_ready", "max_ready", "rn_ready", "root_ready",
                                          "res_ready"))
            block = phase.enter_context(nc.Block())

            @block.sync
            def _(sp):
                def step(at):
                    if u := at.ahead(4):
                        if due(u.r - 3):
                            sp.wait_ge(o_ready, u.r - 3)
                        sp.dma_start(s_s[:, u.c, :], group(sum1, u.r)).then_inc(s_in[u.c], 16)
                    if u := at.ahead(3):
                        if not u.stays:
                            if due(u.r - 3):
                                sp.wait_ge(res_ready, u.r - 3)
                            sp.dma_start(x1_s[:, u.d, :], group(x1, u.r)).then_inc(x1_in[u.d], 16)
                    if u := at.ahead(0):
                        sp.wait_ge(res_ready, u.r + 1)
                        sp.dma_start(group(out, u.r), res_s[:, u.c, :]).then_inc(res_out[u.c], 16)

                run_units(sp, step, 4)
                for c in range(4):
                    sp.wait_ge(res_out[c], 16 * uses(c, 4))

            @block.vector
            def _(dve):
                def rows(u):
                    if due(u.r - 3):
                        dve.wait_ge(n_ready, u.r - 3)
                    dve.wait_ge(s_in[u.c], u.n * 16 + 16)
                    for k in range(G):
                        cols = slice(k * D, (k + 1) * D)
                        ins = nc.vector.scalar_tensor_tensor(
                            out=o_s[:, u.c, cols], in0=s_s[:, u.c, cols],
                            scalar=inv_cnt[:, bass.ds(u.r * G + k, 1)], in1=b_s[:, :],
                            op0=ALU.mult, op1=ALU.add)
                    ins.then_inc(o_ready, 1)

                def inverse(u):
                    dve.wait_ge(n_ready, u.r + 1)
                    nc.vector.tensor_scalar(norm2[:, u.c, :], norm2[:, u.c, :], L2_EPS * L2_EPS,
                                            None, ALU.max).then_inc(max_ready, 1)
                    dve.wait_ge(max_ready, u.r + 1)
                    nc.vector.reciprocal(norm2[:, u.c, :], norm2[:, u.c, :]).then_inc(rn_ready, 1)

                def result(u):
                    x1_u = kept[:, bass.ds(u.place, 1), :].rearrange("p a f -> p (a f)") if u.stays else x1_s[:, u.d, :]
                    if not u.stays:
                        dve.wait_ge(x1_in[u.d], u.n * 16 + 16)
                    if due(u.n):
                        dve.wait_ge(res_out[u.c], u.n * 16)
                    dve.wait_ge(root_ready, u.r + 1)
                    for k in range(G):
                        cols = slice(k * D, (k + 1) * D)
                        ins = nc.vector.scalar_tensor_tensor(
                            out=res_s[:, u.c, cols], in0=o_s[:, u.c, cols],
                            scalar=inv_norm[:, u.c, k:k + 1], in1=x1_u[:, cols],
                            op0=ALU.mult, op1=ALU.add)
                    ins.then_inc(res_ready, 1)

                def step(at):
                    if u := at.ahead(2):
                        rows(u)
                    if u := at.ahead(1):
                        inverse(u)
                    if u := at.ahead(0):
                        result(u)

                run_units(dve, step, 2)

            @block.scalar
            def _(act):
                def step(at):
                    if u := at.ahead(2):
                        if due(u.r - 1):
                            act.wait_ge(n_ready, u.r - 1)
                        if due(u.r - 3):
                            act.wait_ge(root_ready, u.r - 3)
                        act.wait_ge(o_ready, u.r + 1)
                        for k in range(G):
                            cols = slice(k * D, (k + 1) * D)
                            ins = nc.scalar.activation(sq_junk[:, u.c2, cols], o_s[:, u.c, cols],
                                                       ACT.Square, accum_out=norm2[:, u.c, k:k + 1])
                        ins.then_inc(n_ready, 1)
                    if u := at.ahead(1):
                        if due(u.r - 3):
                            act.wait_ge(res_ready, u.r - 3)
                        act.wait_ge(rn_ready, u.r + 1)
                        nc.scalar.activation(inv_norm[:, u.c, :], norm2[:, u.c, :],
                                             ACT.Sqrt).then_inc(root_ready, 1)

                run_units(act, step, 2)


def kernel(x, src, dst, edge_attr_64, L0_gnn_x_child, L0_gnn_W1, L0_gnn_b1, L0_gnn_W2, L0_gnn_b2,
           L0_gnn_Wu, L0_gnn_bu, L0_gnn_gamma, L0_gnn_beta, L1_gnn_W, L1_gnn_b):
    import numpy as np
    import concourse.bacc as bacc
    from concourse.bass_utils import run_bass_kernel_spmd

    def pad(a, rows, fill=0):
        a = np.asarray(a)
        return np.concatenate([a, np.full((rows - a.shape[0],) + a.shape[1:], fill, a.dtype)])

    src_p, dst_p = pad(src, NP, N), pad(dst, NP, N)
    w_t = np.ascontiguousarray(np.asarray(L1_gnn_W).T)
    arrays = {
        "x": pad(x, NP),
        "src_cols": np.ascontiguousarray(src_p.reshape(TILES, P).T),
        "dst_cols": np.ascontiguousarray(dst_p.reshape(TILES, P).T),
        "src_rows": src_p.reshape(UNITS, UNIT),
        "dst_rows": dst_p.reshape(UNITS, UNIT),
        "ea_t": np.ascontiguousarray(pad(edge_attr_64, NP).T),
        "child_t": np.ascontiguousarray(pad(L0_gnn_x_child, CROWS).T),
        "w1": np.asarray(L0_gnn_W1), "b1": np.asarray(L0_gnn_b1),
        "w2_t": np.ascontiguousarray(np.asarray(L0_gnn_W2).T), "b2": np.asarray(L0_gnn_b2),
        "wu": np.asarray(L0_gnn_Wu), "bu": np.asarray(L0_gnn_bu),
        "gamma": np.asarray(L0_gnn_gamma), "beta": np.asarray(L0_gnn_beta),
        "wn_t": np.ascontiguousarray(w_t[:D]), "we_t": np.ascontiguousarray(w_t[D:]),
        "b": np.asarray(L1_gnn_b),
    }
    nc = bacc.Bacc("TRN2", target_bir_lowering=False, num_devices=1)
    args = [nc.dram_tensor(f"in_{name}", a.shape, mybir.dt.from_np(a.dtype), kind="ExternalInput").ap()
            for name, a in arrays.items()]
    args.append(nc.dram_tensor("out", (NP, D), F32, kind="ExternalOutput").ap())
    build(nc, *args)
    r = run_bass_kernel_spmd(nc, [{f"in_{name}": a for name, a in arrays.items()}], core_ids=[0])
    return r.results[0]["out"][:N]
```

```python
from contextlib import ExitStack

import concourse.bass as bass
from concourse import mybir

P = 128
D = 128
N = 50000
E = 50000
NCHILD = 6250
EC = 64
LN_EPS = 1e-5
L2_EPS = 1e-12

G = 4
UNIT = G * P
UNROLL = 4
UNITS = -(-max(N, E) // (2 * UNIT)) * 2
NP = UNITS * UNIT
TILES = NP // P
CT = -(-NCHILD // P)
CROWS = CT * P
CCHUNK = 7
MORE = 128
SPARE = MORE * UNIT
ROWS = SPARE + UNIT
PARTS = 3
TW = D + 1
WIDE = 8
RES = 4
RES_SLOTS = UNITS // WIDE * RES + min(UNITS % WIDE, RES)
HT = 8
TURNS = -(-UNITS // UNROLL)
FIRST_TURNS = 2
TERMS = 2 * G + 1
FAR = 2.0 ** 100
CHUNKS = CT // CCHUNK
assert (TURNS + CHUNKS) * UNROLL <= MORE
SQ = [b * (b + 1) // 2 * P for b in range(G + 1)]
assert CT % CCHUNK == 0 and NP > N and NP > E

ALU = mybir.AluOpType
ACT = mybir.ActivationFunctionType
F32 = mybir.dt.float32
F16 = mybir.dt.float16
BF16 = mybir.dt.bfloat16
I32 = mybir.dt.int32


class Unit:

    def __init__(self, r, c, n, wide=UNROLL, end=UNITS):
        self.r, self.c, self.n, self.wide, self.end = r, c, n, wide, end
        self.c2, self.c4 = c % 2, c % 4
        self.n4 = n * (wide // 4) + c // 4
        self.stays = c < RES
        self.place = n * RES + c
        self.d = c - RES

    def ahead(self, d):
        if isinstance(self.r, int) and not 0 <= self.r + d < self.end:
            return None
        return Unit(self.r + d, (self.c + d) % self.wide, self.n + (self.c + d) // self.wide,
                    self.wide, self.end)


def due(count):
    return not isinstance(count, int) or count > 0


def run_units(eng, step, lead, most=6, wide=UNROLL):
    for r in range(-lead, wide):
        step(Unit(r, r % wide, r // wide, wide))
    turns = (UNITS - most) // wide
    with eng.Fori(1, turns) as n:
        for c in range(wide):
            step(Unit(n * wide + c, c, n, wide))
    for r in range(turns * wide, UNITS):
        step(Unit(r, r % wide, r // wide, wide))


def run_edge_turns(eng, step, lead, edge_turns):
    for r in range(-lead, UNROLL):
        step(Unit(r, r % UNROLL, r // UNROLL, UNROLL, MORE))
    with eng.Fori(1, edge_turns) as n:
        for c in range(UNROLL):
            step(Unit(n * UNROLL + c, c, n, UNROLL, MORE))


def run_both_turns(eng, step, rest_turn, lead, edge_turns, both, rest_turns):
    for r in range(-lead, UNROLL):
        step(Unit(r, r % UNROLL, r // UNROLL, UNROLL, MORE))
    with eng.If(both > 0):
        with eng.Fori(1, both + 1) as n:
            for c in range(UNROLL):
                step(Unit(n * UNROLL + c, c, n, UNROLL, MORE))
            rest_turn(n - 1)
    with eng.If(both + 1 < edge_turns):
        with eng.Fori(both + 1, edge_turns) as n:
            for c in range(UNROLL):
                step(Unit(n * UNROLL + c, c, n, UNROLL, MORE))
    with eng.If(both < rest_turns):
        with eng.Fori(both, rest_turns) as m:
            rest_turn(m)


def uses(slot, slots):
    return (UNITS - slot + slots - 1) // slots


def flat(ap):
    return ap.rearrange("p k d -> p (k d)")


def build(nc, x, src_cols, dst_cols, src_rows, dst_rows, ea_t, child_t, w1, b1, w2_t, b2, wu, bu,
          gamma, beta, wn_t, we_t, b, out):
    with ExitStack() as ctx:
        def sb(name, shape, dt=F32, scope=ctx):
            return scope.enter_context(nc.sbuf_tensor(name, shape, dt))

        def bank(name):
            return ctx.enter_context(nc.psum_tensor(name, [P, 512], F32))

        def sem(name):
            return ctx.enter_context(nc.semaphore(name))

        def sems(name, n):
            return [sem(f"{name}{k}") for k in range(n)]

        def table(name, rows, width, dt=F32):
            return nc.dram_tensor(name, (rows, width), dt, kind="Internal").ap()

        child_proj = table("child_proj", CROWS, PARTS * D, BF16)
        sum0, sum1, x1 = table("sum0", ROWS, D), table("sum1", ROWS, D), table("x1", NP, D)
        last_weights, has_rows = table("last_weights", TILES, P), table("has_rows", TILES, P)
        far_rows = table("far_rows", UNITS, UNIT, BF16)
        node_msg = table("node_msg", NP, TW)

        def group(t, r):
            return t[0:NP, :].rearrange("(g p k) d -> g p (k d)", p=P, k=G)[
                bass.ds(r, 1)].rearrange("a p f -> (a p) f")

        ident = sb("ident", [P, P])
        before = sb("before", [P, SQ[G]], BF16)
        iota_p = sb("iota_p", [P, P], F16)
        iota_t = sb("iota_t", [P, TILES], F16)
        spare_row = sb("spare_row", [P, G])
        eps_col = sb("eps_col", [P, 1])
        zeros = sb("zeros", [P, UNIT * D // P])
        ones = sb("ones", [P, 1])
        hzero = sb("hzero", [P, 512], F16)
        w1_s, neg_wc_s, wn_s, we_s = sb("w1_s", [P, D]), sb("neg_wc_s", [P, D]), sb("wn_s", [P, D]), sb("we_s", [EC, D])
        b1_s = sb("b1_s", [P, 1])
        beta_g, gamma_g, b_s = sb("beta_g", [P, G * D]), sb("gamma_g", [P, G * D]), sb("b_s", [P, D])
        row_terms = sb("row_terms", [TERMS, UNIT])
        one_row = sb("one_row", [1, P], BF16)
        src_i, dst_i = sb("src_i", [P, MORE * G], I32), sb("dst_i", [P, MORE * G], I32)
        dst_f = sb("dst_f", [P, MORE * G])
        turns_i = sb("turns_i", [1, 3], I32)
        inv_cnt = sb("inv_cnt", [P, TILES])
        kept = sb("kept", [P, RES_SLOTS, G * D])

        layer_0 = ctx.enter_context(ExitStack())
        src_f = sb("src_f", [P, MORE * G], scope=layer_0)
        key_p, key_t, to_spare = (sb("l0_" + n, [P, MORE * G], scope=layer_0) for n in (
            "key_p", "key_t", "to_spare"))

        ps_sum = [bank("ps_sum0"), bank("ps_sum1")]
        ps_e = [bank("ps_e0"), bank("ps_e1")]
        ps_a, ps_b, ps_c, ps_cnt = bank("ps_a"), bank("ps_b"), bank("ps_c"), bank("ps_cnt")

        rest_hot_ready, rest_hot_used = sem("rest_hot_ready"), sem("rest_hot_used")
        count_a, count_b = ps_a, ps_cnt

        def edge_turns(eng):
            return eng.value_load(turns_i[0:1, 0:1], min_val=0,
                                  max_val=TURNS - FIRST_TURNS) + FIRST_TURNS

        def rest_turns(eng):
            return eng.value_load(turns_i[0:1, 1:2], min_val=0, max_val=TURNS - CHUNKS)

        def both_turns(eng):
            return eng.value_load(turns_i[0:1, 2:3], min_val=0, max_val=TURNS - CHUNKS)

        def last_turn(turn):
            return nc.s_assert_within(turn, 0, TURNS - 1, skip_runtime_bounds_check_because=(
                "rest_turns ends where the turns do"))

        def one_hots(dve, u, q, onehot_p, onehot_t, ready, used):
            for t in range(G):
                if due(q - 1):
                    dve.wait_ge(used, (q - 2) * G + t + 1)
                col = bass.ds(u.r * G + t, 1)
                nc.vector.tensor_scalar(onehot_p[:, u.c2 * G + t, :], iota_p[:, :],
                                        key_p[:, col], None, ALU.is_equal)
                nc.vector.tensor_scalar(onehot_t[:, u.c2 * G + t, :], iota_t[:, :],
                                        key_t[:, col], None, ALU.is_equal).then_inc(ready, 1)

        def split_keys(dve, ints, halves, done):
            k0, k1 = halves[:, 0, :], halves[:, 1, :]
            nc.vector.tensor_scalar(k0, ints[:, :], 2, P - 1, ALU.logical_shift_right,
                                    ALU.bitwise_and).then_inc(done, 1)
            dve.wait_ge(done, 1)
            nc.vector.tensor_copy(key_p[:, :], k0).then_inc(done, 1)
            dve.wait_ge(done, 2)
            nc.vector.tensor_scalar(k0, ints[:, :], 9, 2, ALU.logical_shift_right,
                                    ALU.logical_shift_left).then_inc(done, 1)
            nc.vector.tensor_scalar(k1, ints[:, :], G - 1, None, ALU.bitwise_and).then_inc(done, 1)
            dve.wait_ge(done, 4)
            nc.vector.tensor_tensor(key_t[:, :], k0, k1, ALU.add).then_inc(done, 1)
            dve.wait_ge(done, 5)

        def spare_distance(dve, keys_f, done):
            for k in range(G):
                ins = nc.vector.tensor_scalar(to_spare[:, k::G], keys_f[:, k::G], -1.0,
                                              spare_row[:, k:k + 1], ALU.mult, ALU.add)
            ins.then_inc(done, 1)

        def rest_hots(dve, n, c, k, onehot_p, onehot_t):
            one_hots(dve, Unit(n * UNROLL + k, k, n, UNROLL, MORE), c * UNROLL + k, onehot_p,
                     onehot_t, rest_hot_ready, rest_hot_used)

        def rest_counts(pe, n, c, k, onehot_p, onehot_t):
            add_counts(pe, Unit(n * UNROLL + k, k, n, UNROLL, MORE), c * UNROLL + k, count_b,
                       onehot_p, onehot_t, rest_hot_ready, rest_hot_used)

        def open_counts(cnt_bank):
            nc.tensor.matmul(cnt_bank[:, :], hzero[:, 0:P], hzero[:, :], start=True, stop=False,
                             skip_group_check=True)

        def close_counts(cnt_bank):
            return nc.tensor.matmul(cnt_bank[:, :], hzero[:, 0:P], hzero[:, :], start=False,
                                    stop=True, skip_group_check=True)

        def add_counts(pe, u, q, cnt_bank, onehot_p, onehot_t, ready, used):
            for t in range(G):
                pe.wait_ge(ready, q * G + t + 1)
                nc.tensor.matmul(cnt_bank[:, 0:TILES], onehot_p[:, u.c2 * G + t, :],
                                 onehot_t[:, u.c2 * G + t, :], start=False, stop=False,
                                 skip_group_check=True).then_inc(used, 1)

        def norm_stats(src, st, u, bn_done, dve):
            dve.nop(nofuse=True)
            for k in range(G):
                ins = nc.vector.bn_stats(st[:, u.c, k, :], src[:, k * D:(k + 1) * D])
            ins.then_inc(bn_done, 1)

        def norm_sums(dve, st, mv, u, bn_done, var_ready):
            dve.wait_ge(bn_done, u.r + 1)
            dve.nop(nofuse=True)
            for k in range(G):
                ins = nc.vector.bn_aggr(mv[:, u.c, k, :], st[:, u.c, k, :])
            ins.then_inc(var_ready, 1)

        def mark_repeats(dve, u, marks, junk, repeat, put, keys_f, put_step, put_ready):
            for k in range(G):
                ins = nc.vector.tensor_tensor_reduce(
                    out=junk[:, SQ[k]:SQ[k + 1]], in0=marks[:, u.c2, SQ[k]:SQ[k + 1]],
                    in1=before[:, SQ[k]:SQ[k + 1]], scale=1.0, scalar=0.0, op0=ALU.mult,
                    op1=ALU.add, accum_out=repeat[:, u.c, k:k + 1])
            ins.then_inc(put_step, 1)
            dve.wait_ge(put_step, u.r * 2 + 1)
            cols = bass.ds(u.r * G, G)
            nc.vector.scalar_tensor_tensor(out=repeat[:, u.c, :], in0=repeat[:, u.c, :], scalar=0.0,
                                           in1=to_spare[:, cols], op0=ALU.is_gt,
                                           op1=ALU.mult).then_inc(put_step, 1)
            dve.wait_ge(put_step, u.r * 2 + 2)
            nc.vector.tensor_tensor(put[:, u.c, :], repeat[:, u.c, :], keys_f[:, cols],
                                    ALU.add).then_inc(put_ready, 1)

        def sum_quad(pe, u, marks, rows, parts, sum_ready):
            for to in range(G):
                for b in range(to, G):
                    for part in range(parts):
                        ins = nc.tensor.matmul(
                            ps_sum[u.c2][:, to * D:(to + 1) * D],
                            marks[:, u.c2, SQ[b] + to * P:SQ[b] + (to + 1) * P],
                            rows[:, u.c, b, part * D:(part + 1) * D],
                            start=(b == to and part == 0), stop=(b == G - 1 and part == parts - 1))
            ins.then_inc(sum_ready, 1)

        def copy_sums(act, u, combined, added, sum_ready, comb_ready):
            if due(u.r - 1):
                act.wait_ge(added, (u.r - 1) * 16 * G)
            act.wait_ge(sum_ready, u.r + 1)
            nc.scalar.copy(combined[:, u.c2, :], ps_sum[u.c2][:, :]).then_inc(comb_ready, 1)

        def gather_quad(pool, u, rows, source, take, take_ready, rows_used, got):
            if due(u.r - 3):
                pool.wait_ge(rows_used, u.r - 3)
            pool.wait_ge(take_ready, u.r + 1)
            pool.nop(nofuse=True)
            for k in range(G):
                nc.gpsimd.indirect_dma_start(
                    rows[:, u.c, k, :], None, source[:, :],
                    bass.IndirectOffsetOnAxis(ap=take[:, u.c, k:k + 1], axis=0)).then_inc(got[u.c], 16)

        def scatter_quad(pool, u, combined, target, put, put_ready, comb_ready, added):
            if due(u.r):
                pool.wait_ge(added, u.r * 16 * G)
            pool.wait_ge(put_ready, u.r + 1)
            pool.wait_ge(comb_ready, u.r + 1)
            pool.nop(nofuse=True)
            for k in range(G):
                nc.gpsimd.indirect_dma_start(
                    target[:, :], bass.IndirectOffsetOnAxis(ap=put[:, u.c, k:k + 1], axis=0),
                    combined[:, u.c2, k * D:(k + 1) * D], None, compute_op=ALU.add).then_inc(added, 16)

        def load_keys(sp, u, keys, rows, eq_ready, keys_in):
            if due(u.r - 3):
                sp.wait_ge(eq_ready, u.r - 3)
            sp.dma_start(keys[:, u.c, :], rows[bass.ds(u.r, 1), :].rearrange(
                "a e -> (a e)").partition_broadcast(P)).then_inc(keys_in[u.c], 16)

        with ExitStack() as phase:
            ZR = 7
            zeros_big = sb("zeros_big", [P, ZR * UNIT * D // P], scope=phase)
            wu_s, w2t_s = sb("wu_s", [P, D], scope=phase), sb("w2t_s", [P, D], scope=phase)
            b2_s, last_s = sb("b2_s", [P, 1], scope=phase), sb("last_s", [P, 1], scope=phase)
            row_s = sb("row_s", [1, 2 * D], scope=phase)
            halves = sb("halves", [P, 2, MORE * G], I32, scope=phase)
            turn_of = sb("turn_of", [P, MORE // UNROLL, UNROLL * G], scope=phase)
            turn_if = sb("turn_if", [P, MORE * G], scope=phase)
            onehot_p = sb("set_onehot_p", [P, HT, P], F16, phase)
            onehot_t = sb("set_onehot_t", [P, HT, TILES], F16, phase)
            most_p = sb("most_p", [P, 1], scope=phase)
            most_1, rest_1 = sb("most_1", [1, 1], scope=phase), sb("rest_1", [1, 1], scope=phase)
            child_in = sb("child_in", [P, 2, CCHUNK * P], scope=phase)
            child_rest = sb("child_rest", [P, 2, CCHUNK, D], scope=phase)
            child_out = sb("child_out", [P, 2, CCHUNK, PARTS, D], BF16, scope=phase)
            ld_w, ld_keys, ld_small, zero_set, sum_zeroed, consts = (sem("set_" + n) for n in (
                "ld_w", "ld_keys", "ld_small", "zero_set", "sum_zeroed", "consts"))
            key_step, row_ready, row_copied, row_put = (sem("set_" + n) for n in (
                "key_step", "row_ready", "row_copied", "row_put"))
            if_step, most_ready, most_turned = (sem("set_" + n) for n in (
                "if_step", "most_ready", "most_turned"))
            child_ld, child_st = sems("set_child_ld", 2), sems("set_child_st", 2)
            child_ready, part_0, rest_0, part_1, child_split = (sem("set_" + n) for n in (
                "child_ready", "part_0", "rest_0", "part_1", "child_split"))
            LONE = 3
            ZEROINGS = UNITS // ZR // CHUNKS
            assert UNITS % (ZR * CHUNKS) == 0 and (CHUNKS - LONE) % 2 == 0
            child_banks = [(ps_e[0], ps_e[1]), (ps_sum[0], ps_sum[1])]
            block = phase.enter_context(nc.Block())

            def chunks(eng, chunk):
                for c in range(LONE):
                    chunk(c, c % 2, c // 2)
                with eng.Fori(LONE // 2, CHUNKS // 2) as n:
                    chunk(n * 2 + 1, 1, n)
                    chunk(n * 2 + 2, 0, n + 1)

            @block.sync
            def _(sp):
                for t, a in ((src_i, src_cols), (dst_i, dst_cols)):
                    sp.dma_start(t[:, :], a).then_inc(ld_keys, 16)
                for t, a in ((wu_s, wu), (w2t_s, w2_t), (w1_s, w1), (wn_s, wn_t), (we_s, we_t)):
                    sp.dma_start(t[:, :], a).then_inc(ld_w, 16)
                with nc.allow_non_contiguous_dma(reason="two columns of 128"):
                    for t, a in ((b1_s, b1), (b2_s, b2)):
                        sp.dma_start(t[:, :], a.rearrange("(p a) -> p a", a=1)).then_inc(ld_w, 16)
                    sp.dma_start(last_s[:, :], child_t[:, NCHILD - 1:NCHILD]).then_inc(ld_w, 16)
                for t, a in ((gamma_g, gamma), (beta_g, beta)):
                    for k in range(G):
                        sp.dma_start(t[:, k * D:(k + 1) * D],
                                     a.partition_broadcast(P)).then_inc(ld_small, 16)
                sp.dma_start(b_s[:, :], b.partition_broadcast(P)).then_inc(ld_small, 16)

                def load(c, slot):
                    if due(c - 1):
                        sp.wait_ge(child_ready, c - 1)
                    sp.dma_start(child_in[:, slot, :], child_t[:, bass.ds(c * (CCHUNK * P), CCHUNK * P)]
                                 ).then_inc(child_ld[slot], 16)

                def store(c, slot):
                    sp.wait_ge(child_split, c + 1)
                    sp.dma_start(child_proj[:, :].rearrange("(c t p) d -> c p t d", p=P, t=CCHUNK)[
                        bass.ds(c, 1)].rearrange("c p t d -> (c p) t d"),
                        child_out[:, slot, :, :, :].rearrange("p t a d -> p t (a d)")
                    ).then_inc(child_st[slot], 16)

                def chunk(c, slot, n):
                    load(c, slot)
                    if due(c):
                        store(c - 1, 1 - slot)

                chunks(sp, chunk)
                store(CHUNKS - 1, (CHUNKS - 1) % 2)
                sp.wait_ge(row_copied, 1)
                sp.wait_ge(zero_set, 1)
                for k in range(G):
                    block_k = slice(k * D, (k + 1) * D)
                    sp.dma_start(row_terms[k:k + 1, block_k], row_s[:, 0:D]).then_inc(row_put, 16)
                    sp.dma_start(row_terms[G + k:G + k + 1, block_k],
                                 row_s[:, D:2 * D]).then_inc(row_put, 16)
                    sp.dma_start(row_terms[2 * G:TERMS, block_k],
                                 bu.partition_broadcast(1)).then_inc(row_put, 16)
                sp.wait_ge(row_put, 16 * 3 * G)
                for slot in range(2):
                    sp.wait_ge(child_st[slot], 16 * ((CHUNKS + 1 - slot) // 2))
                sp.wait_ge(ld_small, 16 * (2 * G + 1))

            @block.gpsimd
            def _(pool):
                nc.gpsimd.memset(ident[:, :], 0.0)
                nc.gpsimd.memset(before[:, :], 1.0)
                nc.gpsimd.memset(eps_col[:, :], LN_EPS)
                nc.gpsimd.memset(zeros[:, :], 0.0)
                nc.gpsimd.memset(ones[:, :], 1.0).then_inc(consts, 1)
                pool.wait_ge(consts, 1)
                nc.gpsimd.affine_select(out=ident[:, :], in_=ident[:, :], compare_op=ALU.not_equal,
                                        fill=1.0, base=0, pattern=[[-1, P]], channel_multiplier=1)
                for k in range(G):
                    own = before[:, SQ[k + 1] - P:SQ[k + 1]]
                    nc.gpsimd.affine_select(out=own, in_=own, compare_op=ALU.is_gt, fill=0.0, base=0,
                                            pattern=[[-1, P]], channel_multiplier=1)
                nc.gpsimd.iota(iota_p[:, :], [[1, P]], base=0, channel_multiplier=0,
                               allow_small_or_imprecise_dtypes=True)
                nc.gpsimd.iota(iota_t[:, :], [[1, TILES]], base=0, channel_multiplier=0,
                               allow_small_or_imprecise_dtypes=True)
                nc.gpsimd.iota(turn_of[:, :, :], [[1, MORE // UNROLL], [0, UNROLL * G]], base=1,
                               channel_multiplier=0, allow_small_or_imprecise_dtypes=True)
                nc.gpsimd.iota(spare_row[:, :], [[1, G]], base=SPARE, channel_multiplier=G,
                               allow_small_or_imprecise_dtypes=True).then_inc(consts, 1)

            @block.vector
            def _(dve):
                nc.vector.memset(hzero[:, :], 0.0)
                nc.vector.memset(one_row[:, :], 1.0)
                nc.vector.memset(row_terms[:, :], 0.0)
                nc.vector.memset(zeros_big[:, :], 0.0).then_inc(zero_set, 1)
                dve.wait_ge(ld_keys, 32)
                split_keys(dve, src_i, halves, key_step)
                nc.vector.tensor_copy(src_f[:, :], src_i[:, :])
                nc.vector.tensor_copy(dst_f[:, :], dst_i[:, :]).then_inc(key_step, 1)
                dve.wait_ge(key_step, 6)
                dve.wait_ge(consts, 2)
                spare_distance(dve, src_f, key_step)
                nc.vector.scalar_tensor_tensor(
                    out=turn_if[:, 0:TILES], in0=dst_f[:, 0:TILES], scalar=float(NCHILD - 1),
                    in1=turn_of[:, :, :].rearrange("p a b -> p (a b)")[:, 0:TILES],
                    op0=ALU.is_lt, op1=ALU.mult).then_inc(if_step, 1)
                dve.wait_ge(if_step, 1)
                nc.vector.reduce_max(most_p[:, :], turn_if[:, 0:TILES],
                                     mybir.AxisListType.X).then_inc(most_ready, 1)
                dve.wait_ge(most_turned, 1)
                nc.vector.reduce_max(most_1[:, :], ps_c[0:1, 0:P], mybir.AxisListType.X).then_inc(if_step, 1)
                dve.wait_ge(if_step, 2)
                nc.vector.tensor_scalar(most_1[:, :], most_1[:, :], float(FIRST_TURNS), None,
                                        ALU.max).then_inc(if_step, 1)
                dve.wait_ge(if_step, 3)
                nc.vector.tensor_scalar(turns_i[:, 0:1], most_1[:, :], -float(FIRST_TURNS), None, ALU.add)
                nc.vector.tensor_scalar(rest_1[:, :], most_1[:, :], -1.0, float(TURNS - CHUNKS),
                                        ALU.mult, ALU.add).then_inc(if_step, 1)
                dve.wait_ge(if_step, 4)
                nc.vector.tensor_scalar(rest_1[:, :], rest_1[:, :], 0.0, None,
                                        ALU.max).then_inc(if_step, 1)
                dve.wait_ge(if_step, 5)
                nc.vector.tensor_copy(turns_i[:, 1:2], rest_1[:, :])
                nc.vector.scalar_tensor_tensor(out=turns_i[:, 2:3], in0=most_1[:, :], scalar=-1.0,
                                               in1=rest_1[:, :], op0=ALU.add,
                                               op1=ALU.min).then_inc(if_step, 1)
                dve.wait_ge(if_step, 6)
                turns = edge_turns(dve)
                dve.wait_ge(row_ready, 1)
                nc.vector.tensor_scalar(neg_wc_s[:, :], ps_a[:, 0:D], -1.0, None, ALU.mult)
                nc.vector.tensor_copy(row_s[:, 0:D], ps_b[0:1, 0:D])
                nc.vector.tensor_scalar(row_s[:, D:2 * D], ps_b[0:1, D:2 * D], -1.0, None,
                                        ALU.mult).then_inc(row_copied, 1)

                def chunk(c, slot, n):
                    dve.wait_ge(part_0, c + 1)
                    dve.nop(nofuse=True)
                    for half, (t0, t1) in enumerate(((0, G), (G, CCHUNK))):
                        ins = nc.vector.tensor_tensor(
                            child_rest[:, slot, t0:t1, :],
                            child_banks[slot][half][:, 0:(t1 - t0) * D].rearrange("p (t d) -> p t d", d=D),
                            child_out[:, slot, t0:t1, 0, :], ALU.subtract)
                    ins.then_inc(rest_0, 1)
                    rest_hots(dve, turns + c, c, 0, onehot_p, onehot_t)
                    rest_hots(dve, turns + c, c, 1, onehot_p, onehot_t)
                    dve.wait_ge(part_1, c + 1)
                    dve.nop(nofuse=True)
                    nc.vector.tensor_tensor(child_out[:, slot, :, 2, :], child_rest[:, slot, :, :],
                                            child_out[:, slot, :, 1, :],
                                            ALU.subtract).then_inc(child_split, 1)
                    rest_hots(dve, turns + c, c, 2, onehot_p, onehot_t)
                    rest_hots(dve, turns + c, c, 3, onehot_p, onehot_t)

                chunks(dve, chunk)

            @block.tensor
            def _(pe):
                pe.wait_ge(consts, 2)
                pe.wait_ge(most_ready, 1)
                nc.tensor.transpose(ps_c[0:1, 0:P], most_p[:, :], ident[:, :]).then_inc(most_turned, 1)
                pe.wait_ge(ld_w, 16 * 8)
                nc.tensor.matmul(ps_a[:, 0:D], w2t_s[:, :], wu_s[:, :], start=True, stop=True)
                nc.tensor.matmul(ps_b[0:1, 0:D], last_s[:, :], wu_s[:, :], start=True, stop=True)
                nc.tensor.matmul(ps_b[0:1, D:2 * D], b2_s[:, :], wu_s[:, :], start=True,
                                 stop=True).then_inc(row_ready, 1)

                open_counts(count_b)
                pe.wait_ge(if_step, 6)
                turns = edge_turns(pe)

                def chunk(c, slot, n):
                    if due(c - 1):
                        pe.wait_ge(rest_0, c - 1)
                    pe.wait_ge(child_ld[slot], n * 16 + 16)
                    for t in range(CCHUNK):
                        ins = nc.tensor.matmul(child_banks[slot][t // G][:, (t % G) * D:(t % G + 1) * D],
                                               child_in[:, slot, t * P:(t + 1) * P], wu_s[:, :],
                                               start=True, stop=True)
                    ins.then_inc(child_ready, 1)
                    for k in range(UNROLL):
                        rest_counts(pe, turns + c, c, k, onehot_p, onehot_t)

                chunks(pe, chunk)

            @block.scalar
            def _(act):
                act.wait_ge(zero_set, 1)
                act.wait_ge(ld_w, 16 * 8)
                act.wait_ge(ld_keys, 32)
                for s in (sum0, sum1):
                    act.dma_start(s[SPARE:ROWS, :].rearrange("(p r) d -> p (r d)", p=P),
                                  zeros_big[:, 0:G * D]).then_inc(sum_zeroed, 16)

                def chunk(c, slot, n):
                    act.wait_ge(child_ready, c + 1)
                    if due(n):
                        act.wait_ge(child_st[slot], n * 16)
                    act.nop(nofuse=True)
                    for half, (t0, t1) in enumerate(((0, G), (G, CCHUNK))):
                        ins = nc.scalar.copy(child_out[:, slot, t0:t1, 0, :],
                                             child_banks[slot][half][:, 0:(t1 - t0) * D].rearrange(
                                                 "p (t d) -> p t d", d=D))
                    ins.then_inc(part_0, 1)
                    act.wait_ge(rest_0, c + 1)
                    act.nop(nofuse=True)
                    nc.scalar.copy(child_out[:, slot, :, 1, :], child_rest[:, slot, :, :]
                                   ).then_inc(part_1, 1)
                    for z in range(ZEROINGS):
                        act.dma_start(sum0[bass.ds((c * ZEROINGS + z) * (ZR * UNIT), ZR * UNIT), :].rearrange(
                            "(p r) d -> p (r d)", p=P), zeros_big[:, :]).then_inc(sum_zeroed, 16)

                chunks(act, chunk)
                act.wait_ge(sum_zeroed, 16 * (UNITS // ZR + 2))

        with ExitStack() as phase:
            def pb(name, shape, dt=F32):
                return sb("l0_" + name, shape, dt, phase)

            keys = pb("keys", [P, 4, UNIT], I32)
            take, put = pb("take", [P, 4, G], I32), pb("put", [P, 4, G], I32)
            taken = pb("taken", [P, 4, G, PARTS * D], BF16)
            marks, junk = pb("marks", [P, 2, SQ[G]], BF16), pb("junk", [P, SQ[G]], BF16)
            repeat = pb("repeat", [P, 4, G])
            combined = pb("combined", [P, 2, UNIT])
            onehot_p, onehot_t = pb("onehot_p", [P, HT, P], F16), pb("onehot_t", [P, HT, TILES], F16)
            rest_hot_p, rest_hot_t = pb("rest_hot_p", [P, HT, P], F16), pb("rest_hot_t", [P, HT, TILES], F16)
            cnt, weight, has, far = (pb(n, [P, TILES]) for n in ("cnt", "weight", "has", "far"))
            weight_out_s, has_out_s = pb("weight_out_s", [P, G, P]), pb("has_out_s", [P, G, P])
            far_out_s = pb("far_out_s", [P, G, P], BF16)

            keys_in, got = sems("l0_keys_in", 4), sems("l0_got", 4)
            (take_ready, eq_ready, put_step, put_ready, sum_ready, comb_ready, added,
             hot_ready, hot_used, cnt_closed, cnt_step, weight_ready, weight_turned, weight_copied,
             weight_out) = (
                sem("l0_" + n) for n in (
                    "take_ready", "eq_ready", "put_step", "put_ready", "sum_ready",
                    "comb_ready", "added", "hot_ready", "hot_used", "cnt_closed",
                    "cnt_step", "weight_ready", "weight_turned", "weight_copied", "weight_out"))
            WT = TILES // G

            block = phase.enter_context(nc.Block())

            @block.sync
            def _(sp):
                turns = edge_turns(sp)

                def step(at):
                    if u := at.ahead(4):
                        load_keys(sp, u, keys, src_rows, eq_ready, keys_in)

                run_edge_turns(sp, step, 4, turns)
                for c in range(4):
                    sp.wait_ge(keys_in[c], turns * 16 + 16)
                far_tiles = far_rows[:, :].rearrange("g (k p) -> (g k) p", p=P)
                for n, (t, rows) in enumerate(((last_weights[:, :], weight_out_s),
                                               (has_rows[:, :], has_out_s), (far_tiles, far_out_s))):
                    sp.wait_ge(weight_copied, n + 1)
                    for k in range(G):
                        sp.dma_start(t[k * WT:(k + 1) * WT, :], rows[0:WT, k, :]).then_inc(weight_out, 16)
                sp.wait_ge(weight_out, 16 * 3 * G)

            @block.gpsimd
            def _(pool):
                turns = edge_turns(pool)

                def step(at):
                    if u := at.ahead(1):
                        gather_quad(pool, u, taken, child_proj, take, take_ready, sum_ready, got)
                    if u := at.ahead(0):
                        scatter_quad(pool, u, combined, sum0, put, put_ready, comb_ready, added)

                run_edge_turns(pool, step, 1, turns)
                pool.wait_ge(added, turns * (16 * G * UNROLL))
                for c in range(4):
                    pool.wait_ge(got[c], (turns + (c < 1)) * (16 * G))

            @block.vector
            def _(dve):
                turns = edge_turns(dve)

                def rows_to_take(u):
                    if due(u.n):
                        dve.wait_ge(got[u.c], u.n * 16 * G)
                    nc.vector.tensor_scalar(take[:, u.c, :], dst_i[:, bass.ds(u.r * G, G)],
                                            NCHILD - 1, None, ALU.min).then_inc(take_ready, 1)

                def compare(u):
                    if due(u.r - 1):
                        dve.wait_ge(sum_ready, u.r - 1)
                    if due(u.r - 3):
                        dve.wait_ge(added, (u.r - 3) * 16 * G)
                    dve.wait_ge(keys_in[u.c], u.n * 16 + 16)
                    for k in range(G):
                        ins = nc.vector.tensor_scalar(marks[:, u.c2, SQ[k]:SQ[k + 1]],
                                                      keys[:, u.c, 0:(k + 1) * P],
                                                      src_f[:, bass.ds(u.r * G + k, 1)], None,
                                                      ALU.is_equal)
                    ins.then_inc(eq_ready, 1)
                    dve.wait_ge(eq_ready, u.r + 1)
                    mark_repeats(dve, u, marks, junk, repeat, put, src_f, put_step, put_ready)

                def step(at):
                    if u := at.ahead(3):
                        rows_to_take(u)
                    if u := at.ahead(1):
                        compare(u)
                    if u := at.ahead(0):
                        one_hots(dve, u, u.r, onehot_p, onehot_t, hot_ready, hot_used)

                def rest_turn(m):
                    for k in range(UNROLL):
                        rest_hots(dve, last_turn(turns + CHUNKS + m), CHUNKS + m, k, rest_hot_p, rest_hot_t)

                run_both_turns(dve, step, rest_turn, 3, turns, both_turns(dve), rest_turns(dve))
                dve.wait_ge(cnt_closed, 1)
                nc.vector.tensor_copy(weight[:, :], count_b[:, 0:TILES]).then_inc(cnt_step, 1)
                dve.wait_ge(cnt_step, 1)
                nc.vector.tensor_tensor(cnt[:, :], count_a[:, 0:TILES], weight[:, :],
                                        ALU.add).then_inc(cnt_step, 1)
                dve.wait_ge(cnt_step, 2)
                nc.vector.tensor_scalar(has[:, :], cnt[:, :], 1.0, None, ALU.min)
                nc.vector.tensor_scalar(inv_cnt[:, :], cnt[:, :], 1.0, None,
                                        ALU.max).then_inc(cnt_step, 1)
                dve.wait_ge(cnt_step, 3)
                nc.vector.reciprocal(inv_cnt[:, :], inv_cnt[:, :]).then_inc(cnt_step, 1)
                dve.wait_ge(cnt_step, 4)
                nc.vector.tensor_scalar(far[:, :], has[:, :], FAR, FAR, ALU.mult, ALU.subtract)
                nc.vector.tensor_tensor(weight[:, :], weight[:, :], inv_cnt[:, :],
                                        ALU.mult).then_inc(weight_ready, 1)

            @block.tensor
            def _(pe):
                turns = edge_turns(pe)

                def step(at):
                    if u := at.ahead(0):
                        if due(u.r - 1):
                            pe.wait_ge(comb_ready, u.r - 1)
                        pe.wait_ge(eq_ready, u.r + 1)
                        pe.wait_ge(got[u.c], (u.n + 1) * 16 * G)
                        sum_quad(pe, u, marks, taken, PARTS, sum_ready)
                        add_counts(pe, u, u.r, count_a, onehot_p, onehot_t, hot_ready, hot_used)

                open_counts(count_a)
                def rest_turn(m):
                    for k in range(UNROLL):
                        rest_counts(pe, last_turn(turns + CHUNKS + m), CHUNKS + m, k, rest_hot_p, rest_hot_t)

                run_both_turns(pe, step, rest_turn, 0, turns, both_turns(pe), rest_turns(pe))
                close_counts(count_a)
                close_counts(count_b).then_inc(cnt_closed, 1)
                pe.wait_ge(weight_ready, 1)
                for t, turned in ((weight, ps_c), (has, ps_e[0]), (far, ps_e[1])):
                    for k in range(G):
                        ins = nc.tensor.transpose(turned[0:WT, k * P:(k + 1) * P],
                                                  t[:, k * WT:(k + 1) * WT], ident[:, :])
                    ins.then_inc(weight_turned, 1)

            @block.scalar
            def _(act):
                turns = edge_turns(act)

                def step(at):
                    if u := at.ahead(0):
                        copy_sums(act, u, combined, added, sum_ready, comb_ready)

                run_edge_turns(act, step, 0, turns)
                for n, (rows, turned) in enumerate(((weight_out_s, ps_c), (has_out_s, ps_e[0]),
                                                    (far_out_s, ps_e[1]))):
                    act.wait_ge(weight_turned, n + 1)
                    nc.scalar.copy(flat(rows[0:WT, :, :]), turned[0:WT, :]).then_inc(weight_copied, 1)

        layer_0.close()

        with ExitStack() as phase:
            def pb(name, shape, dt=F32):
                return sb("up_" + name, shape, dt, phase)

            x_s = pb("x_s", [P, WIDE, G * D])
            y_s = pb("y_s", [P, WIDE, G * D])
            s_s = pb("s_s", [P, 4, G * D])
            x1_s = pb("x1_s", [P, WIDE - RES, G * D])
            weight_s, far_s = pb("weight_s", [TERMS, 4, P]), pb("far_s", [1, 4, UNIT], BF16)
            st_x, st_y, st_1 = (pb(n, [P, WIDE, G, 6]) for n in ("st_x", "st_y", "st_1"))
            mv_x, mv_y, mv_1 = (pb(n, [P, WIDE, G, 2]) for n in ("mv_x", "mv_y", "mv_1"))
            sd_x, sd_y, sd_1, rs_x, rs_y, rs_1, shift_x, neg_1, rs2_1 = (pb(n, [P, WIDE, G]) for n in (
                "sd_x", "sd_y", "sd_1", "rs_x", "rs_y", "rs_1", "shift_x", "neg_1", "rs2_1"))
            ht_s, act_s = pb("ht_s", [P, UNIT]), pb("act_s", [P, UNIT])
            h1_s, h1t_s = pb("h1_s", [P, 2, G * D]), pb("h1t_s", [P, 2, UNIT])
            msg_s = pb("msg_s", [P, 4, G, TW])
            sq_s = pb("sq_s", [P, 2, UNIT])

            x_in, x1_out = sems("up_x_in", WIDE), sems("up_x1_out", WIDE - RES)
            s_in, w_in, m_out = (sems("up_" + n, 4) for n in ("s_in", "w_in", "m_out"))
            names = ("ones_set", "bn_x", "var_x", "root_x", "inv_x", "terms_x", "h_ready", "tr_ready",
                     "ht_ready", "hid_ready", "act_ready", "proj_ready", "y_ready", "bn_y",
                     "var_y", "root_y", "inv_y", "z_ready", "zg_ready", "xb_ready", "x1_ready", "bn_1", "var_1",
                     "root_1", "terms_1", "h1_ready", "tr1_ready", "h1t_ready", "m_proj", "m_ready",
                     "sq_ready", "n2_ready", "norm_ready", "zeroed")
            (ones_set, bn_x, var_x, root_x, inv_x, terms_x, h_ready, tr_ready,
             ht_ready, hid_ready, act_ready, proj_ready, y_ready, bn_y,
             var_y, root_y, inv_y, z_ready, zg_ready, xb_ready, x1_ready, bn_1, var_1,
             root_1, terms_1, h1_ready, tr1_ready, h1t_ready, m_proj, m_ready,
             sq_ready, n2_ready, norm_ready, zeroed) = (sem("up_" + n) for n in names)
            proj_bank, tr1_bank, msg_bank, n2_bank = [ps_c, ps_e[0]], ps_e[1], ps_sum, ps_cnt

            (LOAD_X, STATS_X, ROOT_X, H0, LOAD_W, MLP, LOAD_S, Y, Z, X1, STATS_1, ROOT_1, H1, MSG,
             SCALE) = (13, 12, 11, 10, 10, 9, 9, 8, 7, 6, 5, 4, 3, 2, 1)

            def x1_of(u):
                return kept[:, bass.ds(u.place, 1), :].rearrange("p a f -> p (a f)") if u.stays else x1_s[:, u.d, :]

            def run(eng, step, lead):
                run_units(eng, step, lead, LOAD_X, WIDE)

            block = phase.enter_context(nc.Block())

            @block.sync
            def _(sp):
                def step(at):
                    if u := at.ahead(LOAD_S):
                        if due(u.r - 3):
                            sp.wait_ge(y_ready, u.r - 3)
                        sp.dma_start(s_s[:, u.c4, :], group(sum0, u.r)).then_inc(s_in[u.c4], 16)
                    if u := at.ahead(LOAD_W):
                        if due(u.r - 3):
                            sp.wait_ge(proj_ready, u.r - 3)
                        else:
                            sp.wait_ge(ones_set, 1)
                        for n, t in enumerate((last_weights, has_rows)):
                            sp.dma_start(weight_s[n * G:(n + 1) * G, u.c4, :],
                                         t[bass.ds(u.r * G, G), :]).then_inc(w_in[u.c4], 16)
                        sp.dma_start(far_s[:, u.c4, :],
                                     far_rows[bass.ds(u.r, 1), :]).then_inc(w_in[u.c4], 16)
                    if u := at.ahead(LOAD_X):
                        if due(u.r - 7):
                            sp.wait_ge(x1_ready, u.r - 7)
                        sp.dma_start(x_s[:, u.c, :], group(x, u.r)).then_inc(x_in[u.c], 16)
                    if u := at.ahead(STATS_1):
                        if not u.stays:
                            sp.wait_ge(x1_ready, u.r + 1)
                            sp.dma_start(group(x1, u.r), x1_s[:, u.d, :]).then_inc(x1_out[u.d], 16)
                    if u := at.ahead(0):
                        sp.dma_start(sum1[bass.ds(u.r * UNIT, UNIT), :].rearrange(
                            "(p r) d -> p (r d)", p=P), zeros[:, :]).then_inc(zeroed, 16)
                        sp.wait_ge(m_ready, u.r + 1)
                        sp.wait_ge(norm_ready, u.r + 1)
                        sp.dma_start(group(node_msg, u.r),
                                     flat(msg_s[:, u.c4, :, :])).then_inc(m_out[u.c4], 16)

                run(sp, step, LOAD_X)
                for d in range(WIDE - RES):
                    sp.wait_ge(x1_out[d], 16 * uses(RES + d, WIDE))
                for c in range(4):
                    sp.wait_ge(m_out[c], 16 * uses(c, 4))
                sp.wait_ge(zeroed, 16 * UNITS)

            @block.gpsimd
            def _(pool):
                def step(at):
                    if u := at.ahead(SCALE):
                        if due(u.r - 1):
                            pool.wait_ge(n2_ready, u.r - 1)
                        pool.wait_ge(h1t_ready, u.r + 1)
                        nc.gpsimd.tensor_tensor(sq_s[:, u.c2, :], h1t_s[:, u.c2, :],
                                                h1t_s[:, u.c2, :], ALU.mult).then_inc(sq_ready, 1)
                    if u := at.ahead(X1):
                        pool.wait_ge(z_ready, u.r + 1)
                        nc.gpsimd.tensor_tensor(y_s[:, u.c, :], y_s[:, u.c, :], gamma_g[:, :],
                                                ALU.mult).then_inc(zg_ready, 1)
                    if u := at.ahead(MLP):
                        pool.wait_ge(h_ready, u.r + 1)
                        pool.wait_ge(var_x, u.r + 1)
                        nc.gpsimd.tensor_tensor(x_s[:, u.c, :], x_s[:, u.c, :], beta_g[:, :],
                                                ALU.add).then_inc(xb_ready, 1)
                    if u := at.ahead(X1):
                        if not u.stays and due(u.n):
                            pool.wait_ge(x1_out[u.d], u.n * 16)
                            pool.wait_ge(h1_ready, u.r - 7)
                        pool.wait_ge(xb_ready, u.r + 1)
                        pool.wait_ge(zg_ready, u.r + 1)
                        pool.nop(nofuse=True)
                        nc.gpsimd.tensor_tensor(x1_of(u), y_s[:, u.c, :], x_s[:, u.c, :],
                                                ALU.add).then_inc(x1_ready, 1)

                run(pool, step, MLP)

            @block.vector
            def _(dve):
                def inverse(root, inv, u, root_ready, inv_ready):
                    dve.wait_ge(root_ready, u.r + 1)
                    nc.vector.reciprocal(inv[:, u.c, :], root[:, u.c, :]).then_inc(inv_ready, 1)

                def step(at):
                    if u := at.ahead(Y):
                        dve.wait_ge(s_in[u.c4], u.n4 * 16 + 16)
                        dve.wait_ge(proj_ready, u.r + 1)
                        for k in range(G):
                            cols = slice(k * D, (k + 1) * D)
                            ins = nc.vector.scalar_tensor_tensor(
                                out=y_s[:, u.c, cols], in0=s_s[:, u.c4, cols],
                                scalar=inv_cnt[:, bass.ds(u.r * G + k, 1)],
                                in1=proj_bank[u.c2][:, cols],
                                op0=ALU.mult, op1=ALU.add)
                        ins.then_inc(y_ready, 1)
                    if u := at.ahead(Z):
                        inverse(sd_y, rs_y, u, root_y, inv_y)
                    if u := at.ahead(ROOT_1):
                        dve.wait_ge(root_1, u.r + 1)
                        nc.vector.tensor_scalar(neg_1[:, u.c, :], mv_1[:, u.c, :, 0], -1.0, None,
                                                ALU.mult)
                        nc.vector.reciprocal(rs_1[:, u.c, :], sd_1[:, u.c, :]).then_inc(terms_1, 1)
                    if u := at.ahead(ROOT_X):
                        inverse(sd_x, rs_x, u, root_x, inv_x)
                    if u := at.ahead(Y):
                        dve.wait_ge(y_ready, u.r + 1)
                        norm_stats(y_s[:, u.c, :], st_y, u, bn_y, dve)
                    if u := at.ahead(Z):
                        dve.wait_ge(inv_y, u.r + 1)
                        for k in range(G):
                            cols = slice(k * D, (k + 1) * D)
                            ins = nc.vector.tensor_scalar(y_s[:, u.c, cols], y_s[:, u.c, cols],
                                                          mv_y[:, u.c, k, 0:1], rs_y[:, u.c, k:k + 1],
                                                          ALU.subtract, ALU.mult)
                        ins.then_inc(z_ready, 1)
                    if u := at.ahead(ROOT_X):
                        dve.wait_ge(inv_x, u.r + 1)
                        nc.vector.scalar_tensor_tensor(
                            out=shift_x[:, u.c, :], in0=mv_x[:, u.c, :, 0], scalar=-1.0,
                            in1=rs_x[:, u.c, :], op0=ALU.mult, op1=ALU.mult).then_inc(terms_x, 1)
                    if u := at.ahead(STATS_1):
                        dve.wait_ge(x1_ready, u.r + 1)
                        norm_stats(x1_of(u), st_1, u, bn_1, dve)
                    if u := at.ahead(Y):
                        norm_sums(dve, st_y, mv_y, u, bn_y, var_y)
                    if u := at.ahead(STATS_X):
                        dve.wait_ge(x_in[u.c], u.n * 16 + 16)
                        norm_stats(x_s[:, u.c, :], st_x, u, bn_x, dve)
                    if u := at.ahead(STATS_1):
                        norm_sums(dve, st_1, mv_1, u, bn_1, var_1)
                    if u := at.ahead(H1):
                        dve.wait_ge(terms_1, u.r + 1)
                        nc.vector.tensor_tensor(rs2_1[:, u.c, :], rs_1[:, u.c, :], rs_1[:, u.c, :],
                                                ALU.mult)
                    if u := at.ahead(STATS_X):
                        norm_sums(dve, st_x, mv_x, u, bn_x, var_x)
                    if u := at.ahead(0):
                        if due(u.n4):
                            dve.wait_ge(m_out[u.c4], u.n4 * 16)
                        dve.wait_ge(n2_ready, u.r + 1)
                        nc.vector.tensor_tensor(msg_s[:, u.c4, :, D], n2_bank[:, u.c2 * G:(u.c2 + 1) * G],
                                                rs2_1[:, u.c, :], ALU.mult).then_inc(norm_ready, 1)

                nc.vector.memset(weight_s[:, :, :], 1.0).then_inc(ones_set, 1)
                run(dve, step, STATS_X)

            @block.tensor
            def _(pe):
                def step(at):
                    if u := at.ahead(MLP):
                        pe.wait_ge(h_ready, u.r + 1)
                        for k in range(G):
                            ins = nc.tensor.transpose(ps_a[:, k * P:(k + 1) * P],
                                                      y_s[:, u.c, k * D:(k + 1) * D], ident[:, :])
                        ins.then_inc(tr_ready, 1)
                    if u := at.ahead(MSG):
                        pe.wait_ge(h1_ready, u.r + 1)
                        if due(u.r):
                            pe.wait_ge(h1t_ready, u.r)
                        for k in range(G):
                            ins = nc.tensor.transpose(tr1_bank[:, k * P:(k + 1) * P],
                                                      h1_s[:, u.c2, k * D:(k + 1) * D], ident[:, :])
                        ins.then_inc(tr1_ready, 1)
                    if u := at.ahead(0):
                        pe.wait_ge(sq_ready, u.r + 1)
                        if due(u.r):
                            pe.wait_ge(norm_ready, u.r)
                        for k in range(G):
                            ins = nc.tensor.matmul(n2_bank[:, u.c2 * G + k:u.c2 * G + k + 1],
                                                   sq_s[:, u.c2, k * P:(k + 1) * P], ones[:, :],
                                                   start=True, stop=True)
                        ins.then_inc(n2_ready, 1)
                    if u := at.ahead(MLP):
                        pe.wait_ge(w_in[u.c4], u.n4 * 48 + 48)
                        if due(u.r - 1):
                            pe.wait_ge(y_ready, u.r - 1)
                        nc.tensor.matmul(proj_bank[u.c2][:, :], weight_s[:, u.c4, :], row_terms[:, :],
                                         start=True, stop=False)
                        pe.wait_ge(ht_ready, u.r + 1)
                        nc.tensor.matmul(ps_b[:, :], w1_s[:, :], ht_s[:, :], start=True, stop=False)
                        nc.tensor.matmul(ps_b[:, :], one_row[:, :], far_s[:, u.c4, :], start=False,
                                         stop=True).then_inc(hid_ready, 1)
                        for k in range(G):
                            nc.tensor.matmul(proj_bank[u.c2][:, k * D:(k + 1) * D],
                                             ht_s[:, k * P:(k + 1) * P], ident[:, :],
                                             start=False, stop=False)
                    if u := at.ahead(MSG):
                        if due(u.r - 1):
                            pe.wait_ge(m_ready, u.r - 1)
                        pe.wait_ge(h1t_ready, u.r + 1)
                        for k in range(G):
                            ins = nc.tensor.matmul(msg_bank[u.c2][:, k * D:(k + 1) * D],
                                                   h1t_s[:, u.c2, k * P:(k + 1) * P], wn_s[:, :],
                                                   start=True, stop=True)
                        ins.then_inc(m_proj, 1)
                    if u := at.ahead(MLP):
                        pe.wait_ge(act_ready, u.r + 1)
                        for k in range(G):
                            ins = nc.tensor.matmul(proj_bank[u.c2][:, k * D:(k + 1) * D],
                                                   act_s[:, k * P:(k + 1) * P], neg_wc_s[:, :],
                                                   start=False, stop=(k == G - 1))
                        ins.then_inc(proj_ready, 1)

                run(pe, step, MLP)

            @block.scalar
            def _(act):
                def root(mv, sd, u, var_ready, root_ready):
                    act.wait_ge(var_ready, u.r + 1)
                    nc.scalar.activation(sd[:, u.c, :], mv[:, u.c, :, 1], ACT.Sqrt,
                                         bias=eps_col[:, 0:1]).then_inc(root_ready, 1)

                def step(at):
                    if u := at.ahead(MLP):
                        act.wait_ge(tr_ready, u.r + 1)
                        nc.scalar.copy(ht_s[:, :], ps_a[:, :]).then_inc(ht_ready, 1)
                    if u := at.ahead(MSG):
                        act.wait_ge(tr1_ready, u.r + 1)
                        if due(u.r - 1):
                            act.wait_ge(m_proj, u.r - 1)
                            act.wait_ge(sq_ready, u.r - 1)
                        nc.scalar.copy(h1t_s[:, u.c2, :], tr1_bank[:, :]).then_inc(h1t_ready, 1)
                    if u := at.ahead(H0):
                        if due(u.r - 7):
                            act.wait_ge(x1_ready, u.r - 7)
                        act.wait_ge(x_in[u.c], u.n * 16 + 16)
                        act.wait_ge(terms_x, u.r + 1)
                        for k in range(G):
                            cols = slice(k * D, (k + 1) * D)
                            ins = nc.scalar.activation(y_s[:, u.c, cols], x_s[:, u.c, cols], ACT.Relu,
                                                       bias=shift_x[:, u.c, k:k + 1],
                                                       scale=rs_x[:, u.c, k:k + 1])
                        ins.then_inc(h_ready, 1)
                    if u := at.ahead(MLP):
                        if due(u.r):
                            act.wait_ge(proj_ready, u.r)
                        act.wait_ge(hid_ready, u.r + 1)
                        nc.scalar.activation(act_s[:, :], ps_b[:, :], ACT.Relu,
                                             bias=b1_s[:, 0:1]).then_inc(act_ready, 1)
                    if u := at.ahead(H1):
                        if due(u.r - 1):
                            act.wait_ge(tr1_ready, u.r - 1)
                        act.wait_ge(terms_1, u.r + 1)
                        act.nop(nofuse=True)
                        for k in range(G):
                            cols = slice(k * D, (k + 1) * D)
                            ins = nc.scalar.activation(h1_s[:, u.c2, cols], x1_of(u)[:, cols],
                                                       ACT.Relu, bias=neg_1[:, u.c, k:k + 1])
                        ins.then_inc(h1_ready, 1)
                    if u := at.ahead(SCALE):
                        if due(u.n4):
                            act.wait_ge(m_out[u.c4], u.n4 * 16)
                        act.wait_ge(m_proj, u.r + 1)
                        for k in range(G):
                            ins = nc.scalar.activation(msg_s[:, u.c4, k, 0:D],
                                                       msg_bank[u.c2][:, k * D:(k + 1) * D],
                                                       ACT.Copy, scale=rs_1[:, u.c, k:k + 1])
                        ins.then_inc(m_ready, 1)
                    if u := at.ahead(Y):
                        root(mv_y, sd_y, u, var_y, root_y)
                    if u := at.ahead(STATS_1):
                        root(mv_1, sd_1, u, var_1, root_1)
                    if u := at.ahead(STATS_X):
                        root(mv_x, sd_x, u, var_x, root_x)

                run(act, step, STATS_X)

        with ExitStack() as phase:
            def pb(name, shape, dt=F32):
                return sb("l1_" + name, shape, dt, phase)

            keys = pb("keys", [P, 4, UNIT], I32)
            halves = pb("halves", [P, 2, MORE * G], I32)
            key_p, key_t, to_spare = (pb(n, [P, MORE * G]) for n in ("key_p", "key_t", "to_spare"))
            cnt = pb("cnt", [P, TILES])
            onehot_p, onehot_t = pb("onehot_p", [P, HT, P], F16), pb("onehot_t", [P, HT, TILES], F16)
            take, put = pb("take", [P, 4, G], I32), pb("put", [P, 4, G], I32)
            taken = pb("taken", [P, 4, G, TW])
            marks, junk = pb("marks", [P, 2, SQ[G]]), pb("junk", [P, SQ[G]], BF16)
            repeat = pb("repeat", [P, 4, G])
            combined = pb("combined", [P, 2, UNIT])
            ea_s, ea_sq = pb("ea_s", [EC, 4, UNIT]), pb("ea_sq", [EC, 2, UNIT])
            norm2, norm, inv_norm = pb("norm2", [P, 4, G]), pb("norm", [P, 4, G]), pb("inv_norm", [P, 4, G])
            msg = pb("msg", [P, 4, G, D])

            keys_in, ea_in, got, added = sems("l1_keys_in", 4), sems("l1_ea_in", 4), sems("l1_got", 4), sem("l1_added")
            (take_ready, eq_ready, put_step, put_ready, sum_ready, comb_ready, sq_ready,
             edge_ready, n2_added, n2_ready, n2_root, inv_ready, m_ready, hot_ready, hot_used,
             key_step, max_done, cnt_closed) = (
                sem("l1_" + n) for n in (
                    "take_ready", "eq_ready", "put_step", "put_ready", "sum_ready",
                    "comb_ready", "sq_ready", "edge_ready", "n2_added", "n2_ready", "n2_root",
                    "inv_ready", "m_ready", "hot_ready", "hot_used", "key_step", "max_done",
                    "cnt_closed"))
            ps_n = [ps_a, ps_b]
            block = phase.enter_context(nc.Block())

            @block.sync
            def _(sp):
                def step(at):
                    if u := at.ahead(0):
                        if due(u.r - 3):
                            sp.wait_ge(edge_ready, u.r - 3)
                        sp.dma_start(ea_s[:, u.c, :], ea_t[:, bass.ds(u.r * UNIT, UNIT)]).then_inc(ea_in[u.c], 16)
                        load_keys(sp, u, keys, dst_rows, eq_ready, keys_in)

                run_units(sp, step, 0)

            @block.gpsimd
            def _(pool):
                def step(at):
                    if u := at.ahead(3):
                        gather_quad(pool, u, taken, node_msg, take, take_ready, m_ready, got)
                    if u := at.ahead(0):
                        scatter_quad(pool, u, combined, sum1, put, put_ready, comb_ready, added)

                run_units(pool, step, 3)
                pool.wait_ge(added, 16 * G * UNITS)

            @block.vector
            def _(dve):
                def rows_to_take(u):
                    if due(u.n):
                        dve.wait_ge(got[u.c], u.n * 16 * G)
                    nc.vector.tensor_scalar(take[:, u.c, :], src_i[:, bass.ds(u.r * G, G)],
                                            0, None, ALU.max).then_inc(take_ready, 1)

                def messages(u):
                    if due(u.r - 3):
                        dve.wait_ge(sum_ready, u.r - 3)
                    dve.wait_ge(edge_ready, u.r + 1)
                    dve.wait_ge(got[u.c], (u.n + 1) * 16 * G)
                    nc.vector.tensor_tensor(norm2[:, u.c, :], ps_n[u.c2][:, 0:G],
                                            taken[:, u.c, :, D], ALU.add).then_inc(n2_added, 1)
                    nc.vector.tensor_tensor(msg[:, u.c, :, :], ps_e[u.c2][:, :].rearrange(
                        "p (k d) -> p k d", k=G), taken[:, u.c, :, 0:D], ALU.add).then_inc(m_ready, 1)
                    dve.wait_ge(n2_added, u.r + 1)
                    nc.vector.tensor_scalar(norm2[:, u.c, :], norm2[:, u.c, :], L2_EPS * L2_EPS, None,
                                            ALU.max).then_inc(n2_ready, 1)

                def compare(u):
                    dve.wait_ge(n2_root, u.r + 1)
                    nc.vector.reciprocal(inv_norm[:, u.c, :], norm[:, u.c, :]).then_inc(inv_ready, 1)
                    if due(u.r - 1):
                        dve.wait_ge(sum_ready, u.r - 1)
                    if due(u.r - 3):
                        dve.wait_ge(added, (u.r - 3) * 16 * G)
                    dve.wait_ge(keys_in[u.c], u.n * 16 + 16)
                    dve.wait_ge(inv_ready, u.r + 1)
                    for k in range(G):
                        ins = nc.vector.tensor_scalar(marks[:, u.c2, SQ[k]:SQ[k + 1]],
                                                      keys[:, u.c, 0:(k + 1) * P],
                                                      dst_f[:, bass.ds(u.r * G + k, 1)],
                                                      inv_norm[:, u.c, k:k + 1],
                                                      ALU.is_equal, ALU.mult)
                    ins.then_inc(eq_ready, 1)
                    dve.wait_ge(eq_ready, u.r + 1)
                    mark_repeats(dve, u, marks, junk, repeat, put, dst_f, put_step, put_ready)

                def step(at):
                    if u := at.ahead(4):
                        rows_to_take(u)
                    if u := at.ahead(1):
                        compare(u)
                    if u := at.ahead(2):
                        messages(u)
                    if u := at.ahead(0):
                        one_hots(dve, u, u.r, onehot_p, onehot_t, hot_ready, hot_used)

                split_keys(dve, dst_i, halves, key_step)
                spare_distance(dve, dst_f, key_step)
                dve.wait_ge(key_step, 6)
                run_units(dve, step, 4)
                dve.wait_ge(cnt_closed, 1)
                nc.vector.tensor_scalar(cnt[:, :], ps_cnt[:, 0:TILES], 1.0, None,
                                        ALU.max).then_inc(max_done, 1)
                dve.wait_ge(max_done, 1)
                nc.vector.reciprocal(inv_cnt[:, :], cnt[:, :])

            @block.tensor
            def _(pe):
                def edge_parts(u):
                    if due(u.r - 1):
                        pe.wait_ge(m_ready, u.r - 1)
                        pe.wait_ge(n2_added, u.r - 1)
                    pe.wait_ge(ea_in[u.c], u.n * 16 + 16)
                    for k in range(G):
                        nc.tensor.matmul(ps_e[u.c2][:, k * D:(k + 1) * D],
                                         ea_s[:, u.c, k * P:(k + 1) * P], we_s[:, :],
                                         start=True, stop=True)
                    pe.wait_ge(sq_ready, u.r + 1)
                    for k in range(G):
                        ins = nc.tensor.matmul(ps_n[u.c2][:, k:k + 1], ea_sq[:, u.c2, k * P:(k + 1) * P],
                                               ones[0:EC, :], start=True, stop=True)
                    ins.then_inc(edge_ready, 1)

                def step(at):
                    if u := at.ahead(0):
                        if due(u.r - 1):
                            pe.wait_ge(comb_ready, u.r - 1)
                        pe.wait_ge(eq_ready, u.r + 1)
                        pe.wait_ge(m_ready, u.r + 1)
                        sum_quad(pe, u, marks, msg, 1, sum_ready)
                    if u := at.ahead(2):
                        edge_parts(u)
                    if u := at.ahead(0):
                        add_counts(pe, u, u.r, ps_cnt, onehot_p, onehot_t, hot_ready, hot_used)

                open_counts(ps_cnt)
                run_units(pe, step, 2)
                close_counts(ps_cnt).then_inc(cnt_closed, 1)

            @block.scalar
            def _(act):
                def step(at):
                    if u := at.ahead(3):
                        if due(u.r - 1):
                            act.wait_ge(edge_ready, u.r - 1)
                        act.wait_ge(ea_in[u.c], u.n * 16 + 16)
                        nc.scalar.activation(ea_sq[:, u.c2, :], ea_s[:, u.c, :],
                                             ACT.Square).then_inc(sq_ready, 1)
                    if u := at.ahead(0):
                        copy_sums(act, u, combined, added, sum_ready, comb_ready)
                    if u := at.ahead(2):
                        act.wait_ge(n2_ready, u.r + 1)
                        nc.scalar.activation(norm[:, u.c, :], norm2[:, u.c, :],
                                             ACT.Sqrt).then_inc(n2_root, 1)

                run_units(act, step, 3)

        with ExitStack() as phase:
            def pb(name, shape, dt=F32):
                return sb("out_" + name, shape, dt, phase)

            s_s, o_s = pb("s_s", [P, 4, G * D]), pb("o_s", [P, 4, G * D])
            x1_s = pb("x1_s", [P, WIDE - RES, G * D])
            res_s = pb("res_s", [P, 4, G * D])
            sq_junk = pb("sq_junk", [P, 2, G * D])
            norm2, inv_norm = pb("norm2", [P, 4, G]), pb("inv_norm", [P, 4, G])
            x1_in = sems("out_x1_in", WIDE - RES)
            s_in, res_out = sems("out_s_in", 4), sems("out_res_out", 4)
            o_ready, n_ready, max_ready, rn_ready, root_ready, res_ready, scaled, res_added = (
                sem("out_" + n) for n in ("o_ready", "n_ready", "max_ready", "rn_ready", "root_ready",
                                          "res_ready", "scaled", "res_added"))
            DVE_TILES = 3

            def x1_of(u):
                return kept[:, bass.ds(u.place, 1), :].rearrange("p a f -> p (a f)") if u.stays else x1_s[:, u.d, :]

            block = phase.enter_context(nc.Block())

            @block.sync
            def _(sp):
                def step(at):
                    if u := at.ahead(6):
                        if due(u.r - 3):
                            sp.wait_ge(o_ready, u.r - 3)
                        sp.dma_start(s_s[:, u.c4, :], group(sum1, u.r)).then_inc(s_in[u.c4], 16)
                    if u := at.ahead(5):
                        if not u.stays:
                            if due(u.r - 7):
                                sp.wait_ge(res_ready, u.r - 7)
                                sp.wait_ge(res_added, u.r - 7)
                            sp.dma_start(x1_s[:, u.d, :], group(x1, u.r)).then_inc(x1_in[u.d], 16)
                    if u := at.ahead(0):
                        sp.wait_ge(res_ready, u.r + 1)
                        sp.wait_ge(res_added, u.r + 1)
                        sp.dma_start(group(out, u.r), res_s[:, u.c4, :]).then_inc(res_out[u.c4], 16)

                run_units(sp, step, 6, 6, WIDE)
                for c in range(4):
                    sp.wait_ge(res_out[c], 16 * uses(c, 4))

            @block.gpsimd
            def _(pool):
                def step(at):
                    if u := at.ahead(1):
                        if not u.stays:
                            pool.wait_ge(x1_in[u.d], u.n * 16 + 16)
                        pool.wait_ge(scaled, u.r + 1)
                        pool.nop(nofuse=True)
                        rest = slice(DVE_TILES * D, G * D)
                        nc.gpsimd.tensor_tensor(res_s[:, u.c4, rest], res_s[:, u.c4, rest],
                                                x1_of(u)[:, rest], ALU.add).then_inc(res_added, 1)

                run_units(pool, step, 1, 6, WIDE)

            @block.vector
            def _(dve):
                def rows(u):
                    if due(u.r - 3):
                        dve.wait_ge(n_ready, u.r - 3)
                        dve.wait_ge(scaled, u.r - 3)
                    dve.wait_ge(s_in[u.c4], u.n4 * 16 + 16)
                    for k in range(G):
                        cols = slice(k * D, (k + 1) * D)
                        ins = nc.vector.scalar_tensor_tensor(
                            out=o_s[:, u.c4, cols], in0=s_s[:, u.c4, cols],
                            scalar=inv_cnt[:, bass.ds(u.r * G + k, 1)], in1=b_s[:, :],
                            op0=ALU.mult, op1=ALU.add)
                    ins.then_inc(o_ready, 1)

                def bounded(u):
                    dve.wait_ge(n_ready, u.r + 1)
                    nc.vector.tensor_scalar(norm2[:, u.c4, :], norm2[:, u.c4, :], L2_EPS * L2_EPS,
                                            None, ALU.max).then_inc(max_ready, 1)

                def inverse(u):
                    dve.wait_ge(max_ready, u.r + 1)
                    nc.vector.reciprocal(norm2[:, u.c4, :], norm2[:, u.c4, :]).then_inc(rn_ready, 1)

                def result(u):
                    x1_u = x1_of(u)
                    if not u.stays:
                        dve.wait_ge(x1_in[u.d], u.n * 16 + 16)
                    if due(u.n4):
                        dve.wait_ge(res_out[u.c4], u.n4 * 16)
                    dve.wait_ge(root_ready, u.r + 1)
                    for k in range(DVE_TILES):
                        cols = slice(k * D, (k + 1) * D)
                        ins = nc.vector.scalar_tensor_tensor(
                            out=res_s[:, u.c4, cols], in0=o_s[:, u.c4, cols],
                            scalar=inv_norm[:, u.c4, k:k + 1], in1=x1_u[:, cols],
                            op0=ALU.mult, op1=ALU.add)
                    ins.then_inc(res_ready, 1)

                def step(at):
                    if u := at.ahead(3):
                        rows(u)
                    if u := at.ahead(2):
                        bounded(u)
                    if u := at.ahead(1):
                        result(u)
                    if u := at.ahead(2):
                        inverse(u)

                run_units(dve, step, 3, 6, WIDE)

            @block.scalar
            def _(act):
                def step(at):
                    if u := at.ahead(1):
                        if due(u.r - 3):
                            act.wait_ge(res_ready, u.r - 3)
                            act.wait_ge(scaled, u.r - 3)
                        act.wait_ge(rn_ready, u.r + 1)
                        nc.scalar.activation(inv_norm[:, u.c4, :], norm2[:, u.c4, :],
                                             ACT.Sqrt).then_inc(root_ready, 1)
                    if u := at.ahead(1):
                        if due(u.n4):
                            act.wait_ge(res_out[u.c4], u.n4 * 16)
                        act.wait_ge(root_ready, u.r + 1)
                        for k in range(DVE_TILES, G):
                            cols = slice(k * D, (k + 1) * D)
                            ins = nc.scalar.activation(res_s[:, u.c4, cols], o_s[:, u.c4, cols],
                                                       ACT.Copy, scale=inv_norm[:, u.c4, k:k + 1])
                        ins.then_inc(scaled, 1)
                    if u := at.ahead(3):
                        if due(u.r - 1):
                            act.wait_ge(n_ready, u.r - 1)
                        if due(u.r - 3):
                            act.wait_ge(root_ready, u.r - 3)
                        act.wait_ge(o_ready, u.r + 1)
                        for k in range(G):
                            cols = slice(k * D, (k + 1) * D)
                            ins = nc.scalar.activation(sq_junk[:, u.c2, cols], o_s[:, u.c4, cols],
                                                       ACT.Square, accum_out=norm2[:, u.c4, k:k + 1])
                        ins.then_inc(n_ready, 1)

                run_units(act, step, 3, 6, WIDE)


def kernel(x, src, dst, edge_attr_64, L0_gnn_x_child, L0_gnn_W1, L0_gnn_b1, L0_gnn_W2, L0_gnn_b2,
           L0_gnn_Wu, L0_gnn_bu, L0_gnn_gamma, L0_gnn_beta, L1_gnn_W, L1_gnn_b):
    import numpy as np
    import concourse.bacc as bacc
    from concourse.bass_utils import run_bass_kernel_spmd

    def pad(a, rows, fill=0):
        a = np.asarray(a)
        return np.concatenate([a, np.full((rows - a.shape[0],) + a.shape[1:], fill, a.dtype)])

    src_p, dst_p = pad(src, MORE * UNIT, N), pad(dst, MORE * UNIT, N)
    w_t = np.ascontiguousarray(np.asarray(L1_gnn_W).T)
    arrays = {
        "x": pad(x, NP),
        "src_cols": np.ascontiguousarray(src_p.reshape(MORE * G, P).T),
        "dst_cols": np.ascontiguousarray(dst_p.reshape(MORE * G, P).T),
        "src_rows": src_p.reshape(MORE, UNIT),
        "dst_rows": dst_p.reshape(MORE, UNIT),
        "ea_t": np.ascontiguousarray(pad(edge_attr_64, NP).T),
        "child_t": np.ascontiguousarray(pad(L0_gnn_x_child, CROWS).T),
        "w1": np.asarray(L0_gnn_W1), "b1": np.asarray(L0_gnn_b1),
        "w2_t": np.ascontiguousarray(np.asarray(L0_gnn_W2).T), "b2": np.asarray(L0_gnn_b2),
        "wu": np.asarray(L0_gnn_Wu), "bu": np.asarray(L0_gnn_bu),
        "gamma": np.asarray(L0_gnn_gamma), "beta": np.asarray(L0_gnn_beta),
        "wn_t": np.ascontiguousarray(w_t[:D]), "we_t": np.ascontiguousarray(w_t[D:]),
        "b": np.asarray(L1_gnn_b),
    }
    nc = bacc.Bacc("TRN2", target_bir_lowering=False, num_devices=1)
    args = [nc.dram_tensor(f"in_{name}", a.shape, mybir.dt.from_np(a.dtype), kind="ExternalInput").ap()
            for name, a in arrays.items()]
    args.append(nc.dram_tensor("out", (NP, D), F32, kind="ExternalOutput").ap())
    build(nc, *args)
    r = run_bass_kernel_spmd(nc, [{f"in_{name}": a for name, a in arrays.items()}], core_ids=[0])
    return r.results[0]["out"][:N]
```
